# Optimizing a Trainium2 kernel written in Bass

```python
import numpy as np
import jax
import jax.numpy as jnp

def _softmax(x, axis=-1):
    return jax.nn.softmax(x, axis=axis)

def _gelu(x):
    return jax.nn.gelu(x, approximate=True)

def _silu(x):
    return jax.nn.silu(x)

def _sigmoid(x):
    return jax.nn.sigmoid(x)

def _layernorm(x, axis=-1, eps=1e-05):
    m = jnp.mean(x, axis=axis, keepdims=True)
    v = jnp.var(x, axis=axis, keepdims=True)
    return (x - m) / jnp.sqrt(v + eps)

def _scatter_add(tgt, idx, src, axis=0):
    return tgt.at[idx].add(src)

def _segment_sum(src, seg, n):
    return jax.ops.segment_sum(src, seg, n)
kernel_name = 'mk_flamingo_gated_d2_seqx_r8_7b34c7'

def setup_inputs(seed: int=0):
    np.random.seed(seed)
    _w = jnp.asarray

    def _rec_inputs():
        import jax
        import jax.numpy as jnp
        _rk = jax.random.key(seed)
        x = 0.002226 + 0.9996 * jax.random.normal(jax.random.fold_in(_rk, 1), (2, 512, 128), jnp.float32)
        _lenS = 512 - jax.random.randint(jax.random.fold_in(_rk, 7), (2,), 0, max(1, 512 // 4) + 1, jnp.int32)
        _lenS2 = 77 - jax.random.randint(jax.random.fold_in(_rk, 8), (2,), 0, max(1, 77 // 4) + 1, jnp.int32)
        _ctx_1024P = jax.random.normal(jax.random.fold_in(_rk, 11), (2, 16, 128), jnp.float32)
        _ctx_1024c = jax.random.dirichlet(jax.random.fold_in(_rk, 511), 0.3 * jnp.ones((16,), jnp.float32), (2, 77))
        _ctx_1024t = jnp.einsum('bsk,bkd->bsd', _ctx_1024c, _ctx_1024P)
        _ctx_1024t = _ctx_1024t * jax.lax.rsqrt(jnp.mean(jnp.square(_ctx_1024t)) + 1e-12) * 0.953939
        ctx_1024 = -0.000125008 + 0.999885 * (_ctx_1024t + 0.3 * jax.random.normal(jax.random.fold_in(_rk, 611), (2, 77, 128), jnp.float32))
        _g = jax.random.normal(jax.random.fold_in(_rk, 9001), (2, 2), jnp.float32)
        _g = jnp.sign(_g) * jnp.maximum(jnp.abs(_g), 1.0) + (_g == 0) * 1.0
        g_xattn = _g[0]
        g_ffn = _g[1]
        return (x, ctx_1024, g_xattn, g_ffn)
    x, ctx_1024, g_xattn, g_ffn = _rec_inputs()

    def _L0_xattn_setup():
        import jax, jax.numpy as jnp
        import numpy as np
        EPS = 1e-05

        def layer_norm(x, g, b):
            mu = jnp.mean(x, axis=-1, keepdims=True)
            var = jnp.var(x, axis=-1, keepdims=True)
            return (x - mu) * jax.lax.rsqrt(var + EPS) * g + b
        key = jax.random.key(seed)
        ks = jax.random.split(key, 8)
        dim, heads, dim_head = (128, 16, 64)
        inner = heads * dim_head
        b, n, m = (8, 512, 64)
        s = dim ** (-0.5)
        return {'x': jax.random.normal(ks[0], (b, n, dim), jnp.float32), 'latents': jax.random.normal(ks[1], (b, m, dim), jnp.float32), 'ln_m_g': jnp.ones((dim,), jnp.float32), 'ln_m_b': jnp.zeros((dim,), jnp.float32), 'ln_l_g': jnp.ones((dim,), jnp.float32), 'ln_l_b': jnp.zeros((dim,), jnp.float32), 'Wq': jax.random.normal(ks[2], (dim, inner), jnp.float32) * s, 'Wkv': jax.random.normal(ks[3], (dim, 2 * inner), jnp.float32) * s, 'Wout': jax.random.normal(ks[4], (inner, dim), jnp.float32) * s}
    _L0_xattn_all = _L0_xattn_setup()
    _L0_xattn_in = {k: v for k, v in _L0_xattn_all.items() if k in ('ln_m_g', 'ln_m_b', 'ln_l_g', 'ln_l_b', 'Wq', 'Wkv', 'Wout')}
    del _L0_xattn_all

    def _L0_ffn_setup():
        import jax, jax.numpy as jnp
        import numpy as np
        B, S, D = (1, 256, 128)
        E, K, F = (64, 8, 96)
        SF = 96
        C = 64
        ROUTED_SCALE = 1.0

        def _moe_forward(x, router_w, w_gate, w_up, w_down, ws_gate_up, ws_down):
            T = x.shape[0]
            logits = x.astype(jnp.float32) @ router_w.T
            probs = jax.nn.softmax(logits, axis=-1)
            topk_w, topk_ids = jax.lax.top_k(probs, K)
            topk_w = topk_w / jnp.sum(topk_w, axis=-1, keepdims=True)
            topk_w = topk_w.astype(x.dtype)
            N = T * K
            flat_e = topk_ids.reshape(-1)
            flat_w = topk_w.reshape(-1)
            tok = jnp.arange(N) // K
            onehot = flat_e[:, None] == jnp.arange(E)[None, :]
            pos = jnp.cumsum(onehot, axis=0)[jnp.arange(N), flat_e] - 1
            valid = pos < C
            idx = jnp.where(valid, flat_e * C + pos, E * C)
            x_buf = jnp.zeros((E * C + 1, x.shape[1]), x.dtype).at[idx].set(x[tok])
            xb = x_buf[:E * C].reshape(E, C, -1)
            g = jnp.einsum('ecd,edf->ecf', xb, w_gate)
            u = jnp.einsum('ecd,edf->ecf', xb, w_up)
            h = jax.nn.silu(g) * u
            y = jnp.einsum('ecf,efd->ecd', h, w_down).reshape(E * C, -1)
            safe = jnp.where(valid, idx, 0)
            contrib = y[safe] * (flat_w * valid.astype(flat_w.dtype))[:, None]
            routed = jax.ops.segment_sum(contrib, tok, num_segments=T)
            routed = routed * ROUTED_SCALE
            gu = x @ ws_gate_up
            sg, su = (gu[:, :SF], gu[:, SF:])
            shared = jax.nn.silu(sg) * su @ ws_down
            return routed + shared
        key = jax.random.key(seed)
        ks = jax.random.split(key, 7)
        w = 0.02
        return {'hidden_states': jax.random.normal(ks[0], (B, S, D), jnp.float32), 'router_w': jax.random.normal(ks[1], (E, D), jnp.float32) * w, 'w_gate': jax.random.normal(ks[2], (E, D, F), jnp.float32) * w, 'w_up': jax.random.normal(ks[3], (E, D, F), jnp.float32) * w, 'w_down': jax.random.normal(ks[4], (E, F, D), jnp.float32) * w, 'ws_gate_up': jax.random.normal(ks[5], (D, 2 * SF), jnp.float32) * w, 'ws_down': jax.random.normal(ks[6], (SF, D), jnp.float32) * w}
    _L0_ffn_all = _L0_ffn_setup()
    _L0_ffn_in = {k: v for k, v in _L0_ffn_all.items() if k in ('router_w', 'w_gate', 'w_up', 'w_down', 'ws_gate_up', 'ws_down')}
    del _L0_ffn_all

    def _L1_xattn_setup():
        import jax, jax.numpy as jnp
        import numpy as np
        B, L_ENC, L_DEC, D = (16, 64, 128, 128)
        key = jax.random.key(seed)
        k1, k2, k3, k4, k5, k6 = jax.random.split(key, 6)
        encoder_hc = jax.random.normal(k1, (B, L_ENC, D), dtype=jnp.float32)
        decoder_hq = jax.random.normal(k2, (B, L_DEC, D), dtype=jnp.float32)
        w_sim = jax.random.normal(k3, (3 * D,), dtype=jnp.float32) * 0.02
        b_sim = jax.random.normal(k4, (1,), dtype=jnp.float32) * 0.02
        W_qv = jax.random.normal(k5, (4 * D, D), dtype=jnp.float32) * 0.02
        b_qv = jax.random.normal(k6, (D,), dtype=jnp.float32) * 0.02
        return {'encoder_hc': encoder_hc, 'decoder_hq': decoder_hq, 'w_sim': w_sim, 'b_sim': b_sim, 'W_qv': W_qv, 'b_qv': b_qv}
    _L1_xattn_all = _L1_xattn_setup()
    _L1_xattn_in = {k: v for k, v in _L1_xattn_all.items() if k in ('w_sim', 'b_sim', 'W_qv', 'b_qv')}
    del _L1_xattn_all

    def _L1_ffn_setup():
        import jax, jax.numpy as jnp
        import numpy as np
        B, S, H, F, E = (8, 256, 128, 512, 8)
        INIT_LAMBDA = 0.2
        key = jax.random.key(seed)
        ks = jax.random.split(key, 12)
        std = 0.02
        return {'hidden_states': jax.random.normal(ks[0], (B, S, H), jnp.float32), 'gate_w1': jax.random.normal(ks[1], (H, H), jnp.float32) * 0.01, 'gate_b1': jnp.zeros((H,), jnp.float32), 'gate_w2': jax.random.normal(ks[2], (E, H), jnp.float32) * 0.01, 'gate_b2': jnp.full((E,), INIT_LAMBDA, jnp.float32), 'W1': jax.random.normal(ks[3], (F, H), jnp.float32) * std, 'b1': jax.random.normal(ks[4], (F,), jnp.float32) * std, 'W2': jax.random.normal(ks[5], (H, F), jnp.float32) * std, 'b2': jax.random.normal(ks[6], (H,), jnp.float32) * std, 'TW1': jax.random.normal(ks[7], (E, F, H), jnp.float32) * std, 'Tb1': jax.random.normal(ks[8], (E, F), jnp.float32) * std, 'TW2': jax.random.normal(ks[9], (E, H, F), jnp.float32) * std, 'Tb2': jax.random.normal(ks[10], (E, H), jnp.float32) * std}
    _L1_ffn_all = _L1_ffn_setup()
    _L1_ffn_in = {k: v for k, v in _L1_ffn_all.items() if k in ('gate_w1', 'gate_b1', 'gate_w2', 'gate_b2', 'W1', 'b1', 'W2', 'b2', 'TW1', 'Tb1', 'TW2', 'Tb2')}
    del _L1_ffn_all
    return {'x': x, 'ctx_1024': ctx_1024, 'g_xattn': g_xattn, 'g_ffn': g_ffn, 'L0_xattn_ln_m_g': _L0_xattn_in['ln_m_g'], 'L0_xattn_ln_m_b': _L0_xattn_in['ln_m_b'], 'L0_xattn_ln_l_g': _L0_xattn_in['ln_l_g'], 'L0_xattn_ln_l_b': _L0_xattn_in['ln_l_b'], 'L0_xattn_Wq': _L0_xattn_in['Wq'], 'L0_xattn_Wkv': _L0_xattn_in['Wkv'], 'L0_xattn_Wout': _L0_xattn_in['Wout'], 'L0_ffn_router_w': _L0_ffn_in['router_w'], 'L0_ffn_w_gate': _L0_ffn_in['w_gate'], 'L0_ffn_w_up': _L0_ffn_in['w_up'], 'L0_ffn_w_down': _L0_ffn_in['w_down'], 'L0_ffn_ws_gate_up': _L0_ffn_in['ws_gate_up'], 'L0_ffn_ws_down': _L0_ffn_in['ws_down'], 'L1_xattn_w_sim': _L1_xattn_in['w_sim'], 'L1_xattn_b_sim': _L1_xattn_in['b_sim'], 'L1_xattn_W_qv': _L1_xattn_in['W_qv'], 'L1_xattn_b_qv': _L1_xattn_in['b_qv'], 'L1_ffn_gate_w1': _L1_ffn_in['gate_w1'], 'L1_ffn_gate_b1': _L1_ffn_in['gate_b1'], 'L1_ffn_gate_w2': _L1_ffn_in['gate_w2'], 'L1_ffn_gate_b2': _L1_ffn_in['gate_b2'], 'L1_ffn_W1': _L1_ffn_in['W1'], 'L1_ffn_b1': _L1_ffn_in['b1'], 'L1_ffn_W2': _L1_ffn_in['W2'], 'L1_ffn_b2': _L1_ffn_in['b2'], 'L1_ffn_TW1': _L1_ffn_in['TW1'], 'L1_ffn_Tb1': _L1_ffn_in['Tb1'], 'L1_ffn_TW2': _L1_ffn_in['TW2'], 'L1_ffn_Tb2': _L1_ffn_in['Tb2']}

def reference(x, ctx_1024, g_xattn, g_ffn, L0_xattn_ln_m_g, L0_xattn_ln_m_b, L0_xattn_ln_l_g, L0_xattn_ln_l_b, L0_xattn_Wq, L0_xattn_Wkv, L0_xattn_Wout, L0_ffn_router_w, L0_ffn_w_gate, L0_ffn_w_up, L0_ffn_w_down, L0_ffn_ws_gate_up, L0_ffn_ws_down, L1_xattn_w_sim, L1_xattn_b_sim, L1_xattn_W_qv, L1_xattn_b_qv, L1_ffn_gate_w1, L1_ffn_gate_b1, L1_ffn_gate_w2, L1_ffn_gate_b2, L1_ffn_W1, L1_ffn_b1, L1_ffn_W2, L1_ffn_b2, L1_ffn_TW1, L1_ffn_Tb1, L1_ffn_TW2, L1_ffn_Tb2):
    import jax
    import jax.numpy as jnp

    def _L0_xattn_ref(x, latents, ln_m_g, ln_m_b, ln_l_g, ln_l_b, Wq, Wkv, Wout):
        import jax, jax.numpy as jnp
        import numpy as np
        EPS = 1e-05

        def layer_norm(x, g, b):
            mu = jnp.mean(x, axis=-1, keepdims=True)
            var = jnp.var(x, axis=-1, keepdims=True)
            return (x - mu) * jax.lax.rsqrt(var + EPS) * g + b
        heads, dim_head = (16, 64)
        scale = dim_head ** (-0.5)
        x = layer_norm(x, ln_m_g, ln_m_b)
        lat = layer_norm(latents, ln_l_g, ln_l_b)
        b, m, _ = lat.shape
        q = lat @ Wq
        kv_input = jnp.concatenate([x, lat], axis=1)
        kv = kv_input @ Wkv
        k, v = jnp.split(kv, 2, axis=-1)

        def split_heads(t):
            return t.reshape(t.shape[0], t.shape[1], heads, dim_head).transpose(0, 2, 1, 3)
        q, k, v = (split_heads(q), split_heads(k), split_heads(v))
        dots = jnp.einsum('bhid,bhjd->bhij', q, k) * scale
        attn = jax.nn.softmax(dots, axis=-1)
        out = jnp.einsum('bhij,bhjd->bhid', attn, v)
        out = out.transpose(0, 2, 1, 3).reshape(b, m, heads * dim_head)
        return out @ Wout

    def _L0_ffn_ref(hidden_states, router_w, w_gate, w_up, w_down, ws_gate_up, ws_down):
        import jax, jax.numpy as jnp
        import numpy as np
        B, S, D = (1, 256, 128)
        E, K, F = (64, 8, 96)
        SF = 96
        C = 64
        ROUTED_SCALE = 1.0

        def _moe_forward(x, router_w, w_gate, w_up, w_down, ws_gate_up, ws_down):
            T = x.shape[0]
            logits = x.astype(jnp.float32) @ router_w.T
            probs = jax.nn.softmax(logits, axis=-1)
            topk_w, topk_ids = jax.lax.top_k(probs, K)
            topk_w = topk_w / jnp.sum(topk_w, axis=-1, keepdims=True)
            topk_w = topk_w.astype(x.dtype)
            N = T * K
            flat_e = topk_ids.reshape(-1)
            flat_w = topk_w.reshape(-1)
            tok = jnp.arange(N) // K
            onehot = flat_e[:, None] == jnp.arange(E)[None, :]
            pos = jnp.cumsum(onehot, axis=0)[jnp.arange(N), flat_e] - 1
            valid = pos < C
            idx = jnp.where(valid, flat_e * C + pos, E * C)
            x_buf = jnp.zeros((E * C + 1, x.shape[1]), x.dtype).at[idx].set(x[tok])
            xb = x_buf[:E * C].reshape(E, C, -1)
            g = jnp.einsum('ecd,edf->ecf', xb, w_gate)
            u = jnp.einsum('ecd,edf->ecf', xb, w_up)
            h = jax.nn.silu(g) * u
            y = jnp.einsum('ecf,efd->ecd', h, w_down).reshape(E * C, -1)
            safe = jnp.where(valid, idx, 0)
            contrib = y[safe] * (flat_w * valid.astype(flat_w.dtype))[:, None]
            routed = jax.ops.segment_sum(contrib, tok, num_segments=T)
            routed = routed * ROUTED_SCALE
            gu = x @ ws_gate_up
            sg, su = (gu[:, :SF], gu[:, SF:])
            shared = jax.nn.silu(sg) * su @ ws_down
            return routed + shared
        b, s, d = hidden_states.shape
        x = hidden_states.reshape(-1, d)
        out = _moe_forward(x, router_w, w_gate, w_up, w_down, ws_gate_up, ws_down)
        return out.reshape(b, s, d)

    def _L1_xattn_ref(encoder_hc, decoder_hq, w_sim, b_sim, W_qv, b_qv):
        import jax, jax.numpy as jnp
        import numpy as np
        B, L_ENC, L_DEC, D = (16, 64, 128, 128)
        d = encoder_hc.shape[-1]
        w1, w2, w3 = (w_sim[:d], w_sim[d:2 * d], w_sim[2 * d:])
        Sim = (encoder_hc @ w1)[:, :, None] + (decoder_hq @ w2)[:, None, :] + jnp.einsum('bid,bjd->bij', encoder_hc * w3, decoder_hq) + b_sim[0]
        A = jax.nn.softmax(Sim, axis=2)
        hq_hat = jnp.einsum('bij,bjd->bid', A, decoder_hq)
        Batt = jax.nn.softmax(jnp.max(Sim, axis=2), axis=1)
        hc_bar = jnp.einsum('bi,bid->bd', Batt, encoder_hc)[:, None, :]
        hc_hat = jnp.broadcast_to(hc_bar, encoder_hc.shape)
        feats = jnp.concatenate([encoder_hc, hq_hat, encoder_hc * hq_hat, encoder_hc * hc_hat], axis=-1)
        hcq = feats @ W_qv + b_qv
        return hcq

    def _L1_ffn_ref(hidden_states, gate_w1, gate_b1, gate_w2, gate_b2, W1, b1, W2, b2, TW1, Tb1, TW2, Tb2):
        import jax, jax.numpy as jnp
        import numpy as np
        B, S, H, F, E = (8, 256, 128, 512, 8)
        INIT_LAMBDA = 0.2
        x = hidden_states
        h = jax.nn.relu(jnp.einsum('bsh,oh->bso', x, gate_w1) + gate_b1)
        g = jnp.einsum('bso,eo->bse', h, gate_w2) + gate_b2
        g = g.mean(axis=1)
        mW1 = W1 + jnp.einsum('be,efh->bfh', g, TW1)
        mb1 = b1 + g @ Tb1
        mW2 = W2 + jnp.einsum('be,ehf->bhf', g, TW2)
        mb2 = b2 + g @ Tb2
        u = jax.nn.gelu(jnp.einsum('bsh,bfh->bsf', x, mW1) + mb1[:, None, :])
        out = jnp.einsum('bsf,bhf->bsh', u, mW2) + mb2[:, None, :]
        return out
    x = x + jnp.tanh(g_xattn[0]) * _L0_xattn_ref(ctx_1024, _layernorm(x, axis=-1), L0_xattn_ln_m_g, L0_xattn_ln_m_b, L0_xattn_ln_l_g, L0_xattn_ln_l_b, L0_xattn_Wq, L0_xattn_Wkv, L0_xattn_Wout)
    x = x + jnp.tanh(g_ffn[0]) * _L0_ffn_ref(_layernorm(x, axis=-1), L0_ffn_router_w, L0_ffn_w_gate, L0_ffn_w_up, L0_ffn_w_down, L0_ffn_ws_gate_up, L0_ffn_ws_down)
    x = x + jnp.tanh(g_xattn[1]) * _L1_xattn_ref(_layernorm(x, axis=-1), ctx_1024, L1_xattn_w_sim, L1_xattn_b_sim, L1_xattn_W_qv, L1_xattn_b_qv)
    x = x + jnp.tanh(g_ffn[1]) * _L1_ffn_ref(_layernorm(x, axis=-1), L1_ffn_gate_w1, L1_ffn_gate_b1, L1_ffn_gate_w2, L1_ffn_gate_b2, L1_ffn_W1, L1_ffn_b1, L1_ffn_W2, L1_ffn_b2, L1_ffn_TW1, L1_ffn_Tb1, L1_ffn_TW2, L1_ffn_Tb2)
    return x

_drawn_inputs = setup_inputs


def setup_inputs(seed=0):
    import zlib

    import numpy as np

    out = dict(_drawn_inputs(seed))
    spreads = {'g_ffn': (-1.0, 0.6),
     'L0_xattn_ln_m_g': (1.0, 0.2),
     'L0_xattn_ln_m_b': (0.0, 0.1),
     'L0_xattn_ln_l_g': (1.0, 0.2),
     'L0_xattn_ln_l_b': (0.0, 0.1),
     'L1_ffn_gate_b1': (0.0, 0.8),
     'L1_ffn_gate_b2': (0.20000000298023224, 0.6)}
    factors = {'L0_ffn_router_w': 8.0,
     'L0_ffn_w_gate': 8.0,
     'L0_ffn_w_up': 8.0,
     'L0_ffn_w_down': 8.0,
     'L0_ffn_ws_gate_up': 8.0,
     'L0_ffn_ws_down': 8.0,
     'L1_xattn_w_sim': 2.766,
     'L1_xattn_b_qv': 2.826,
     'L1_ffn_gate_w1': 22.383,
     'L1_ffn_gate_w2': 8.0,
     'L1_ffn_b1': 8.0,
     'L1_ffn_b2': 3.549,
     'L1_ffn_Tb1': 8.0,
     'L1_ffn_Tb2': 6.205}
    for name, (base, spread) in spreads.items():
        noise = np.random.default_rng([zlib.crc32(name.encode()), seed]).standard_normal(out[name].shape)
        drawn = base * np.exp(spread * noise) if base else spread * noise
        out[name] = jnp.asarray(drawn.astype(out[name].dtype))
    for name, factor in factors.items():
        out[name] = (out[name] * factor).astype(out[name].dtype)
    return out
```

```python
from contextlib import ExitStack

import concourse.bass as bass
from concourse import mybir

ALU = mybir.AluOpType
ACT = mybir.ActivationFunctionType
AX = mybir.AxisListType
F32 = mybir.dt.float32
F32R = mybir.dt.float32r
BF16 = mybir.dt.bfloat16

P = 128
EPS = 1e-5

SMALL = {}


def _place(names):
    at = 0
    for name, width in names:
        SMALL[name] = (at, at + width)
        at += width
    return at


SMALL_WIDTH = _place([
    ("ln_l_g", 1), ("ln_l_b", 1), ("ln_m_g", 1), ("ln_m_b", 1),
    ("g_xattn", 2), ("g_ffn", 2), ("w_sim", 3), ("b_sim", 1),
    ("gate_b1", 1), ("gate_b2", 8), ("gate_b2_col", 1), ("b1", 4), ("Tb1", 32),
    ("b_qv_row", 128), ("b2_row", 128),
])


class Order:

    def __init__(self, eng, sem):
        self.eng, self.sem, self.n = eng, sem, 0

    def mark(self, ins):
        ins.then_inc(self.sem, 1)
        self.n += 1

    def settle(self):
        self.eng.wait_ge(self.sem, self.n)


def flamingo_block(nc, x_in, ctx_in, small_in, wqkv_in, wout_in, rw_in, wgu_in, wdn_in, wsgu_in, wsdn_in,
                   wqv_in, gw1_in, gw2_in, w1_in, tw1_in, w2_in, tw2_in, tb2_in, out):
    B, N, D = x_in.shape
    M = ctx_in.shape[1]
    TILES = N // P
    T = B * TILES
    HP = wqkv_in.shape[0]
    DH = 64
    SCALE = float(DH) ** -0.5
    KV = N + M
    KVP = KV + KV % 2
    JT = N // P + 1
    W_LAST = KV - N
    U = B * HP
    JW = [P] * TILES + [W_LAST]
    E, CAP, FF = rw_in.shape[1], 64, wdn_in.shape[1]
    G = wgu_in.shape[0]
    EG = E // G
    PG = EG // 2
    TOPK = 8
    E2, F2 = tb2_in.shape[0], w1_in.shape[1]
    FC = F2 // P
    XSTEPS = 13

    with ExitStack() as stack:
        def sb(name, shape, dt=F32):
            return stack.enter_context(nc.sbuf_tensor(name, shape, dt))

        sems = {}

        def sem(name):
            if name not in sems:
                sems[name] = stack.enter_context(nc.semaphore(name))
            return sems[name]

        psum = stack.enter_context(nc.psum_tensor("psum", [P, 8 * 512], F32))

        def bank(k, n=1):
            return psum[:, 512 * k:512 * (k + n)]

        xs = sb("xs", [P, T, D])
        cs = sb("cs", [P, B, D])
        small = sb("small", [P, SMALL_WIDTH])
        ident = sb("ident", [P, P])
        ones_f = sb("ones_f", [P, P])
        eps_t = sb("eps_t", [P, 1])
        tg = sb("tg", [P, 4])
        stats = sb("stats", [P, T + B, 6])
        mv = sb("mv", [P, T + B, 2])
        std = sb("std", [P, T + B])
        rstd = sb("rstd", [P, T + B])
        ya = sb("ya", [P, T, D])
        yb = sb("yb", [P, T, D])
        cn = sb("cn", [P, B, D])
        kvT = [sb(f"kvT{b}", [P, KV]) for b in range(B)]
        ctxT = sb("ctxT", [P, B, M])

        ones_b = sb("ones_b", [P, P], BF16)
        before = sb("before", [P, P], BF16)
        spread = sb("spread", [P, P * 64], BF16)
        slots = sb("slots", [P, CAP])
        slot_of = sb("slot_of", [P, 1])
        own_e = sb("own_e", [2 * EG, EG, CAP])
        rw = sb("rw", [P, E])
        wgu = sb("wgu", [P, EG, 2 * FF])
        wdn = sb("wdn", [FF, EG, D])
        wsgu = sb("wsgu", [P, 2 * FF])
        wsdn = sb("wsdn", [FF, D])
        wqv = sb("wqv", [P, 4, D])
        gw1 = sb("gw1", [P, D])
        gw2 = sb("gw2", [P, E2])
        w1 = sb("w1", [P, F2])
        w2 = sb("w2", [P, F2 // P, D])
        tb2 = sb("tb2", [E2, D])

        scope = ExitStack()

        def sb(name, shape, dt=F32):
            return scope.enter_context(nc.sbuf_tensor(name, shape, dt))

        wx = sb("wx", [P, 3 * P])
        wo = sb("wo", [P, D])
        qq = [sb(f"qq{b}", [P, 2, N], F32R) for b in range(B)]
        qlm = [sb(f"qlm{b}", [P, 2, N], F32R) for b in range(B)]
        kk = [sb(f"kk{b}", [P, 2, KVP], F32R) for b in range(B)]
        ko = [sb(f"ko{b}", [P, 2, KVP], F32R) for b in range(B)]
        vv = [sb(f"vv{b}", [P, JT, P]) for b in range(B)]
        pt = [sb(f"pt{b}", [P, JT, 2, N]) for b in range(B)]
        psm = [sb(f"psm{b}", [P, 2, N]) for b in range(B)]
        nmax = sb("nmax", [P, B, 2, TILES])
        mask4 = sb("mask4", [TILES, TILES, P])
        r8 = sb("r8", [P, TILES, 2])
        osb = sb("osb", [P, N])
        onorm = sb("onorm", [P, N])

        scope.close()
        scope2 = stack.enter_context(ExitStack())

        def sb(name, shape, dt=F32):
            return scope2.enter_context(nc.sbuf_tensor(name, shape, dt))

        tw1 = sb("tw1", [P, E2, F2])
        tw2 = sb("tw2", [P, E2, FC, D])
        scope3 = ExitStack()

        def sb(name, shape, dt=F32):
            return scope3.enter_context(nc.sbuf_tensor(name, shape, dt))

        yhi = sb("yhi", [P, T, D], F32R)
        ylo = sb("ylo", [P, T, D], F32R)
        yT = sb("yT", [P, T, P])
        lg = sb("lg", [P, T, E])
        top = sb("top", [P, T, TOPK])
        rest = sb("rest", [P, T, E])
        chosen = sb("chosen", [P, T, E], BF16)
        wgt = sb("wgt", [P, T, E])
        den = sb("den", [P, T])
        rden = sb("rden", [P, T])
        whl = sb("whl", [P, T, E, 2], F32R)
        whg = sb("whg", [P, T, 2 * EG], F32R)
        val = sb("val", [P, T, E])
        valT = sb("valT", [P, T // 2 * P], BF16)
        sth = sb("sth", [FF, T * P])
        hs = sb("hs", [FF, T * P])
        take = sb("take", [P, T, EG, CAP], F32R)
        give = [sb(f"give{p}", [P, T * P], F32R) for p in range(PG)]
        xg = sb("xg", [P, EG * CAP])
        th = sb("th", [P, PG, FF])
        hh = sb("hh", [P, PG, FF])
        hT = sb("hT", [FF, EG * CAP])
        wm = sb("wm", [2 * EG, EG * CAP])
        ws = sb("ws", [P, PG])
        ys = sb("ys", [P, PG, D])
        ehi = sb("ehi", [P, PG, D], F32R)
        elo = sb("elo", [P, PG, D], F32R)
        outT = sb("outT", [P, T * P])
        scope3.close()

        def sb(name, shape, dt=F32):
            return scope2.enter_context(nc.sbuf_tensor(name, shape, dt))

        hcT = sb("hcT", [P, T * P])
        hcp = sb("hcp", [P, T * P])
        nmx = sb("nmx", [P, T])
        aw = sb("aw", [P, T, M])
        asum = sb("asum", [P, T])
        aT = sb("aT", [M, T * P])
        hqh = sb("hqh", [P, T * P])
        f3 = sb("f3", [P, T * P])
        mi = sb("mi", [P, T])
        mbest = sb("mbest", [P, B])
        m2 = sb("m2", [B, 1])
        dm = sb("dm", [B, B])
        negm = sb("negm", [P, B])
        e8 = sb("e8", [P, T])
        es = sb("es", [P, B])
        rtot = sb("rtot", [P, B])
        hcb = sb("hcb", [P, B])
        wc = sb("wc", [P, B, D])
        row = sb("row", [P, D])
        hsum = sb("hsum", [P, B])
        gB = sb("gB", [P, B, E2])
        gT = sb("gT", [E2, B])
        tb = sb("tb", [P, B, FC, E2])
        mb1 = sb("mb1", [P, B, FC])
        mw1 = [sb(f"mw1{b}", [P, F2]) for b in range(B)]
        mw2 = [sb(f"mw2{b}", [P, FC, D]) for b in range(B)]
        diag = sb("diag", [P, B, E2, P])
        uT = [sb(f"uT{b}", [P, FC, N]) for b in range(B)]
        res = sb("res", [P, T, D])

        def small_at(name, n=P):
            a, b = SMALL[name]
            return small[0:n, a:b]

        xbuf = [bank(0, 2), bank(2, 2)]
        sbank = [bank(4), bank(5)]
        obank = bank(6)
        mbank = bank(7)

        def xb(u, j):
            return xbuf[(u + j) % 2]

        block = stack.enter_context(nc.Block())

        def over_pairs(eng, body):
            body(0, True, False)
            with eng.Fori(1, HP - 1) as i:
                body(i, False, False)
            body(HP - 1, False, True)

        def over_groups(eng, body):
            body(0, True, False)
            with eng.Fori(1, G - 1) as g:
                body(g, False, False)
            body(G - 1, False, True)

        @block.sync
        def _(sp):
            for b in range(B):
                sp.dma_start(xs[:, TILES * b:TILES * (b + 1), :],
                             x_in[b].rearrange("(t p) d -> p t d", p=P)).then_inc(sem(f"x_loaded{b}"), 16)
                if b == 0:
                    sp.dma_start(small[:, :], small_in).then_inc(sem("small_loaded"), 16)
            sp.dma_start(cs[0:M, :, :], ctx_in.rearrange("b m d -> m b d")).then_inc(sem("ctx_loaded"), 16)
            sp.dma_start(wx[:, :], wqkv_in[0]).then_inc(sem("wx_loaded"), 16)
            sp.dma_start(wo[:, :], wout_in[0]).then_inc(sem("wo_loaded"), 16)

            def pair(i, first, last):
                if not last:
                    sp.wait_ge(sem("x_full"), i * (2 * XSTEPS) + XSTEPS + 3)
                    src = wqkv_in[i + 1] if isinstance(i, int) else wqkv_in[bass.ds(i + 1, 1)].rearrange("a p n -> p (a n)")
                    sp.dma_start(wx[:, :], src).then_inc(sem("wx_loaded"), 16)
                if not first:
                    sp.wait_ge(sem("mb_full"), i * 6)
                    src = wout_in[i] if isinstance(i, int) else wout_in[bass.ds(i, 1)].rearrange("a p n -> p (a n)")
                    sp.dma_start(wo[:, :], src).then_inc(sem("wo_loaded"), 16)

            later = ((rw, rw_in), (wsgu, wsgu_in), (wsdn, wsdn_in), (wgu, wgu_in[0]), (wdn, wdn_in[0]), (wqv, wqv_in),
                     (gw1, gw1_in), (gw2, gw2_in), (w1, w1_in), (w2, w2_in), (tb2, tb2_in))
            for dst, src in later:
                name = {"wgu": "wgu_loaded", "wdn": "wdn_loaded"}.get(dst.name, "weights_loaded")
                sp.dma_start(dst[(slice(None),) * len(dst.shape)], src).then_inc(sem(name), 16)

            over_pairs(sp, pair)
            sp.wait_ge(sem("x_added"), U)
            sp.dma_start(tw1[:, :, :], tw1_in).then_inc(sem("tw_loaded"), 16)
            sp.dma_start(tw2[:, :, :, :], tw2_in).then_inc(sem("tw_loaded"), 16)

            def group(g, first, last):
                if last:
                    return
                sp.wait_ge(sem("gu_full"), g + 1)
                src = wgu_in[g + 1] if isinstance(g, int) else wgu_in[bass.ds(g + 1, 1)].rearrange("a p e n -> p (a e) n")
                sp.dma_start(wgu[:, :, :], src).then_inc(sem("wgu_loaded"), 16)
                sp.wait_ge(sem("y_full"), g + 1)
                src = wdn_in[g + 1] if isinstance(g, int) else wdn_in[bass.ds(g + 1, 1)].rearrange("a p e n -> p (a e) n")
                sp.dma_start(wdn[:, :, :], src).then_inc(sem("wdn_loaded"), 16)

            over_groups(sp, group)
            for b in range(B):
                sp.wait_ge(sem("out_ready"), b + 1)
                sp.dma_start(out[b].rearrange("(t p) d -> p t d", p=P), res[:, TILES * b:TILES * (b + 1), :])\
                    .then_inc(sem("out_stored"), 16)
            sp.wait_ge(sem("out_stored"), 16 * B)

        @block.gpsimd
        def _(pool):
            po = Order(pool, sem("pool_self"))
            po.mark(pool.memset(ident[:, :], 0.0))
            po.mark(pool.memset(mask4[:, :, :], 0.0))
            po.mark(pool.memset(ones_f[:, :], 1.0))
            po.mark(pool.memset(eps_t[:, :], EPS))
            po.settle()
            pool.affine_select(out=ident[:, :], in_=ident[:, :], compare_op=ALU.not_equal, fill=1.0,
                               base=0, pattern=[[-1, P]], channel_multiplier=1).then_inc(sem("consts"), 1)
            pool.affine_select(out=mask4[:, :, :], in_=mask4[:, :, :], compare_op=ALU.not_equal, fill=1.0,
                               base=0, pattern=[[-1, TILES], [0, P]], channel_multiplier=1).then_inc(sem("consts"), 1)
            for b in range(B):
                for t in (qlm[b], kk[b]):
                    pool.memset(t[:, :, :].bitcast(F32), 0.0).then_inc(sem("pads"), 1)
                pool.memset(ko[b][:, :, :].bitcast(F32), 1.0).then_inc(sem("pads"), 1)

            po.mark(pool.memset(spread[:, :], 0.0))
            po.mark(pool.memset(before[:, :], 1.0))
            po.mark(pool.memset(ones_b[:, :], 1.0))
            po.mark(pool.memset(own_e[:, :, :], 1.0))
            po.settle()
            pool.affine_select(out=spread[:, :], in_=spread[:, :], compare_op=ALU.not_equal, fill=1.0,
                               base=0, pattern=[[-1, P], [0, 64]], channel_multiplier=1).then_inc(sem("consts2"), 1)
            pool.affine_select(out=before[:, :], in_=before[:, :], compare_op=ALU.is_gt, fill=0.0,
                               base=0, pattern=[[1, P]], channel_multiplier=-1).then_inc(sem("consts2"), 1)
            po.mark(pool.affine_select(out=own_e[:, :, :], in_=own_e[:, :, :], compare_op=ALU.is_ge, fill=0.0,
                                       base=0, pattern=[[-2, EG], [0, CAP]], channel_multiplier=1))
            po.settle()
            pool.affine_select(out=own_e[:, :, :], in_=own_e[:, :, :], compare_op=ALU.is_ge, fill=0.0,
                               base=1, pattern=[[2, EG], [0, CAP]], channel_multiplier=-1).then_inc(sem("consts2"), 1)
            pool.iota(slots[:, :], pattern=[[1, CAP]], base=1, channel_multiplier=0,
                      allow_small_or_imprecise_dtypes=True).then_inc(sem("consts2"), 1)
            for h in range(2):
                pool.wait_ge(sem("consts2"), 4 + h)
                pool.iota(slot_of[64 * h:64 * (h + 1), :], pattern=[[0, 1]], base=1, channel_multiplier=1,
                          allow_small_or_imprecise_dtypes=True).then_inc(sem("consts2"), 1)

            pool.wait_ge(sem("consts2"), 6)

            def unit(i, b):
                pool.wait_ge(sem("exp_done"), i * (4 * JT) + 2 * JT * b + 4)
                pool.tensor_tensor(psm[b][:, :, :], pt[b][:, 0, :, :], pt[b][:, 1, :, :], ALU.add)\
                    .then_inc(sem("pool_added"), 1)
                for jt in range(2, JT):
                    w = JW[jt]
                    pool.wait_ge(sem("exp_done"), i * (4 * JT) + 2 * JT * b + 2 * jt + 2)
                    pool.wait_ge(sem("pool_added"), i * (2 * (JT - 1)) + (JT - 1) * b + jt - 1)
                    pool.tensor_tensor(psm[b][0:w, :, :], psm[b][0:w, :, :], pt[b][0:w, jt, :, :], ALU.add)\
                        .then_inc(sem("pool_added"), 1)

            def pair(i, first, last):
                for b in range(B):
                    unit(i, b)

            over_pairs(pool, pair)

            def group_weights(g):
                c = 2 * EG * g
                src = whl[:, :, :, :].rearrange("p t e k -> p t (e k)")
                src = src[:, :, c:c + 2 * EG] if isinstance(g, int) else src[:, :, bass.ds(c, 2 * EG)]
                pool.tensor_copy(whg[:, :, :], src).then_inc(sem("whg_ready"), 1)

            pool.wait_ge(sem("whl_ready"), 2)
            group_weights(0)

            def group(g, first, last):
                if not last:
                    pool.wait_ge(sem("wr_full"), g + 1)
                    group_weights(g + 1)

            over_groups(pool, group)

        @block.scalar
        def _(act):
            act.wait_ge(sem("small_loaded"), 16)
            act.activation(tg[:, :], small[:, SMALL["g_xattn"][0]:SMALL["g_ffn"][1]], ACT.Tanh).then_inc(sem("gates"), 1)
            act.wait_ge(sem("consts"), 2)
            for n in range(2 * B + 1):
                act.wait_ge(sem("var0"), n + 1)
                a, b = (T, T + B) if n == 2 * B else (TILES * (n // 2), TILES * (n // 2 + 1))
                rows = M if n == 2 * B else P
                act.activation(std[0:rows, a:b], mv[0:rows, a:b, 1], ACT.Sqrt, bias=eps_t[0:rows, :])\
                    .then_inc(sem("std0"), 1)
            lat_g, lat_b = small_at("ln_l_g"), small_at("ln_l_b")
            for b in range(B):
                act.wait_ge(sem("lat_t"), TILES * (b + 1))
                act.activation(kvT[b][:, 0:N], bank(b), ACT.Identity, scale=lat_g, bias=lat_b).then_inc(sem("kv_ready"), 1)
            act.wait_ge(sem("lat_t"), TILES * B + B)
            act.activation(kvT[0][:, N:KV], bank(2)[:, 0:M], ACT.Identity, scale=small_at("ln_m_g"),
                           bias=small_at("ln_m_b")).then_inc(sem("kv_ready"), 1)
            act.activation(kvT[1][:, N:KV], bank(2)[:, P:P + M], ACT.Identity, scale=small_at("ln_m_g"),
                           bias=small_at("ln_m_b")).then_inc(sem("kv_ready"), 1)
            act.wait_ge(sem("pads"), 3 * B)

            def exp(i, b, jt, h):
                w = JW[jt]
                act.wait_ge(sem("s_full"), i * (4 * JT) + 2 * JT * b + 2 * jt + h + 1)
                act.activation(pt[b][0:w, jt, h, :], sbank[h][0:w, :], ACT.Exp, scale=SCALE)\
                    .then_inc(sem("exp_done"), 1)

            def round_k(i, c, h):
                b = c % 2
                if h == 0:
                    act.wait_ge(sem("x_full"), i * (2 * XSTEPS) + XSTEPS * c + 1)
                act.activation(kk[b][0:DH, h, 0:KV], xb(c, 0)[DH * h:DH * (h + 1), 0:KV], ACT.Copy)\
                    .then_inc(sem("k_hi"), 1)

            def round_q(i, c, h):
                b = c % 2
                if h == 0:
                    act.wait_ge(sem("x_full"), i * (2 * XSTEPS) + XSTEPS * c + 2)
                act.activation(qq[b][0:DH, h, :], xb(c, 1)[DH * h:DH * (h + 1), 0:N], ACT.Copy)\
                    .then_inc(sem("q_hi"), 1)

            def save_v(i, c):
                b = c % 2
                act.wait_ge(sem("x_full"), i * (2 * XSTEPS) + XSTEPS * c + 3)
                act.activation(vv[b][:, 0:TILES, :], xb(c, 2)[:, 0:N], ACT.Copy).then_inc(sem("v_ready"), 1)
                act.activation(vv[b][0:W_LAST, TILES, :], xb(c, 2)[0:W_LAST, N:N + P], ACT.Copy)\
                    .then_inc(sem("v_ready"), 1)

            def copy_k(i, c, h):
                b = c % 2
                act.wait_ge(sem("k_hi"), i * 4 + 2 * c + h + 1)
                act.activation(ko[b][0:DH, h, 0:KV], kk[b][0:DH, h, 0:KV].bitcast(F32), ACT.Copy)\
                    .then_inc(sem("k_dup"), 1)

            def save_o(i, c):
                act.wait_ge(sem("av_done"), i * (2 * JT) + JT * c)
                if not (isinstance(i, int) and 2 * i + c < 2):
                    act.wait_ge(sem("normed"), i * 2 + c - 1)
                act.activation(osb[:, :], obank, ACT.Copy).then_inc(sem("o_saved"), 1)

            round_k(0, 0, 0)
            round_k(0, 0, 1)
            round_q(0, 0, 0)
            round_q(0, 0, 1)
            save_v(0, 0)
            copy_k(0, 0, 0)
            copy_k(0, 0, 1)

            def unit(i, b, tail, ahead):
                c = b + 1
                if isinstance(i, int) and i == 0:
                    pass
                else:
                    act.wait_ge(sem("pool_added"), i * (2 * (JT - 1)) + (JT - 1) * (b - 1))
                exp(i, b, 0, 0)
                if ahead:
                    round_k(i, c, 0)
                    round_k(i, c, 1)
                exp(i, b, 0, 1)
                if tail:
                    save_o(i, b)
                if ahead:
                    round_q(i, c, 0)
                    round_q(i, c, 1)
                exp(i, b, 1, 0)
                if ahead:
                    save_v(i, c)
                exp(i, b, 1, 1)
                if ahead:
                    copy_k(i, c, 0)
                    copy_k(i, c, 1)
                for jt in range(2, JT):
                    exp(i, b, jt, 0)
                    exp(i, b, jt, 1)

            def pair(i, first, last):
                unit(i, 0, not first, True)
                unit(i, 1, True, not last)

            over_pairs(act, pair)
            save_o(HP, 0)

            def root(n):
                act.wait_ge(sem("var"), n)
                act.activation(std[:, 0:T], mv[:, 0:T, 1], ACT.Sqrt, bias=eps_t[:, :]).then_inc(sem("std"), 1)

            root(1)
            for k in range(2):
                act.wait_ge(sem("yT_full"), k + 1)
                act.activation(yT[:, 4 * k:4 * k + 4, :], bank(k).rearrange("p (t n) -> p t n", n=P), ACT.Copy)\
                    .then_inc(sem("yT_ready"), 1)
            act.wait_ge(sem("lg_full"), 1)
            act.activation(lg[:, :, :], bank(2).rearrange("p (t e) -> p t e", e=E), ACT.Copy).then_inc(sem("lg_ready"), 1)
            act.wait_ge(sem("shared_gate_full"), 1)
            act.activation(sth[:, :], bank(3, 2)[0:FF, :], ACT.Tanh, scale=0.5).then_inc(sem("sth_ready"), 1)
            act.wait_ge(sem("logits_shifted"), 1)
            act.activation(wgt[:, :, :], wgt[:, :, :], ACT.Exp).then_inc(sem("logits_exp"), 1)
            act.wait_ge(sem("valT_full"), 1)
            act.activation(valT[:, :], bank(2), ACT.Copy).then_inc(sem("valT_ready"), 1)

            def save_gathered(n):
                act.wait_ge(sem("g_full"), n)
                act.activation(xg[:, :], bank(4), ACT.Copy).then_inc(sem("xg_ready"), 1)

            save_gathered(1)

            def group(g, first, last):
                act.wait_ge(sem("gu_full"), g + 1)
                gate = bank(5, 2).rearrange("p (k n) -> p k n", k=PG)[:, :, 0:FF]
                act.activation(th[:, :, :], gate, ACT.Tanh, scale=0.5).then_inc(sem("th_ready"), 1)
                act.wait_ge(sem("ht_full"), g + 1)
                act.activation(hT[:, :], bank(5)[0:FF, :], ACT.Copy).then_inc(sem("hT_ready"), 1)
                if not last:
                    save_gathered(g + 2)

            over_groups(act, group)
            for k in range(2):
                act.wait_ge(sem("scattered"), PG * G)
                act.activation(outT[:, 512 * k:512 * (k + 1)], bank(k), ACT.Copy).then_inc(sem("outT_ready"), 1)

            root(2)
            for k in range(2):
                act.wait_ge(sem("hcT_full"), k + 1)
                act.activation(hcT[:, 512 * k:512 * (k + 1)], bank(k), ACT.Copy).then_inc(sem("hcT_ready"), 1)
                act.activation(hcp[:, 512 * k:512 * (k + 1)], bank(k), ACT.Identity, scale=small[:, SMALL["w_sim"][0] + 2:SMALL["w_sim"][0] + 3],
                               bias=small[:, SMALL["w_sim"][0] + 1:SMALL["w_sim"][0] + 2]).then_inc(sem("hcp_ready"), 1)
            act.wait_ge(sem("nmx_ready"), 1)
            for t in range(T):
                act.activation(aw[:, t, :], bank(2 + t // 4)[:, P * (t % 4):P * (t % 4) + M], ACT.Exp,
                               bias=nmx[:, t:t + 1], accum_out=asum[:, t:t + 1]).then_inc(sem("aw_ready"), 1)
            act.wait_ge(sem("negm_ready"), 1)
            for b in range(B):
                act.activation(e8[:, TILES * b:TILES * (b + 1)], mi[:, TILES * b:TILES * (b + 1)], ACT.Exp,
                               bias=negm[:, b:b + 1], accum_out=es[:, b:b + 1]).then_inc(sem("e8_ready"), 1)
            act.wait_ge(sem("aT_full"), 1)
            act.activation(aT[:, :], bank(5, 2)[0:M, :], ACT.Copy).then_inc(sem("aT_ready"), 1)
            act.wait_ge(sem("hqh_full"), 1)
            act.activation(hqh[:, :], bank(2, 2), ACT.Copy).then_inc(sem("hqh_ready"), 1)

            root(3)
            for k in range(2):
                act.wait_ge(sem("zT_full"), k + 1)
                act.activation(hcT[:, 512 * k:512 * (k + 1)], bank(2 + k), ACT.Copy).then_inc(sem("zT_ready"), 1)
            for b in range(B):
                act.wait_ge(sem("gate_full"), b + 1)
                act.activation(hcp[:, 512 * b:512 * (b + 1)], bank(4 + b), ACT.Relu, bias=small_at("gate_b1"),
                               accum_out=hsum[:, b:b + 1]).then_inc(sem("hsum_ready"), 1)
            act.wait_ge(sem("g_ready"), 2)
            for b in range(B):
                for e in range(E2):
                    act.activation(diag[:, b, e, :], ident[:, :], ACT.Copy, scale=gB[:, b, e:e + 1])\
                        .then_inc(sem("diag_ready"), 1)
            for b in range(B):
                act.wait_ge(sem("mw2_full"), b + 1)
                act.activation(mw2[b][:, :, :], bank(b).rearrange("p (c d) -> p c d", d=D), ACT.Copy)\
                    .then_inc(sem("mw2_ready"), 1)
            act.wait_ge(sem("mb1_ready"), 1)
            for n in range(B * FC):
                b, c = n // FC, n % FC
                act.wait_ge(sem("u_full"), n + 1)
                act.activation(uT[b][:, c, :], bank(2 + n % 4), ACT.Gelu_apprx_tanh, bias=mb1[:, b, c:c + 1])\
                    .then_inc(sem("u_ready"), 1)

        @block.vector
        def _(dve):
            vo = Order(dve, sem("dve_self"))

            def norm(src, dst, a, rows, n, var, stdev):
                for t in range(n):
                    vo.mark(dve.bn_stats(stats[0:rows, a + t, :], src[0:rows, t, :]))
                vo.settle()
                for t in range(n):
                    ins = dve.bn_aggr(mv[0:rows, a + t, :], stats[0:rows, a + t, :])
                ins.then_inc(var[0], 1)
                dve.wait_ge(*stdev)
                vo.mark(dve.reciprocal(rstd[0:rows, a:a + n], std[0:rows, a:a + n]))
                vo.settle()
                dve.wait_ge(var[0], var[1])
                for t in range(n):
                    vo.mark(dve.tensor_scalar(dst[0:rows, t, :], src[0:rows, t, :], mv[0:rows, a + t, 0:1],
                                              rstd[0:rows, a + t:a + t + 1], ALU.subtract, ALU.mult))

            for b in range(B):
                dve.wait_ge(sem(f"x_loaded{b}"), 16)
                lo, hi = TILES * b, TILES * (b + 1)
                norm(xs[:, lo:hi, :], ya[:, lo:hi, :], lo, P, TILES, (sem("var0"), 2 * b + 1), (sem("std0"), 2 * b + 1))
                vo.settle()
                norm(ya[:, lo:hi, :], yb[:, lo:hi, :], lo, P, TILES, (sem("var0"), 2 * b + 2), (sem("std0"), 2 * b + 2))
                vo.settle()
                dve.engine_nop().then_inc(sem("lat_normed"), 1)
            dve.wait_ge(sem("ctx_loaded"), 16)
            norm(cs[:, :, :], cn[:, :, :], T, M, B, (sem("var0"), 2 * B + 1), (sem("std0"), 2 * B + 1))
            vo.settle()
            dve.engine_nop().then_inc(sem("lat_normed"), 1)
            dve.wait_ge(sem("lat_t"), TILES * B + 2 * B)
            dve.tensor_copy(ctxT[:, 0, :], bank(3)[:, 0:M]).then_inc(sem("ctxT_ready"), 1)
            dve.tensor_copy(ctxT[:, 1, :], bank(3)[:, P:P + M]).then_inc(sem("ctxT_ready"), 1)
            dve.wait_ge(sem("gates"), 1)
            dve.wait_ge(sem("pads"), 3 * B)

            def k_low(i, c, h):
                b = c % 2
                dve.wait_ge(sem("k_hi"), i * 4 + 2 * c + 2)
                dve.tensor_tensor(kk[b][DH:P, h, 0:KV], xb(c, 0)[DH * h:DH * (h + 1), 0:KV],
                                  kk[b][0:DH, h, 0:KV].bitcast(F32), ALU.subtract).then_inc(sem("k_lo"), 1)

            def q_low(i, c, h):
                b = c % 2
                dve.wait_ge(sem("q_hi"), i * 4 + 2 * c + 2)
                dve.tensor_tensor(qlm[b][0:DH, h, :], xb(c, 1)[DH * h:DH * (h + 1), 0:N],
                                  qq[b][0:DH, h, :].bitcast(F32), ALU.subtract).then_inc(sem("q_lo"), 1)

            def q_dup(i, c, h):
                b = c % 2
                dve.tensor_copy(qq[b][DH:P, h, :], qq[b][0:DH, h, :]).then_inc(sem("q_dup"), 1)

            def row_max(i, c, r):
                b, j = c % 2, 3 + r + (r >= TILES)
                dve.wait_ge(sem("x_full"), i * (2 * XSTEPS) + XSTEPS * c + j + 1)
                dve.tensor_reduce(nmax[:, b, r // TILES, r % TILES:r % TILES + 1], xb(c, j)[:, 0:KV], AX.X, ALU.max,
                                  negate=True).then_inc(sem("max_done"), 1)

            def shift_rows(i, c, h):
                b, j = c % 2, (7, 12)[h]
                dve.wait_ge(sem("x_full"), i * (2 * XSTEPS) + XSTEPS * c + j + 1)
                dve.tensor_tensor(qlm[b][DH:DH + TILES, h, :].rearrange("p (t n) -> p t n", n=P),
                                  xb(c, j)[0:TILES, 0:P].unsqueeze(1).broadcast_to([TILES, TILES, P]),
                                  mask4[:, :, :], ALU.mult).then_inc(sem("shifts"), 1)

            def recip(i, c):
                dve.wait_ge(sem("mb_full"), i * 6 + 3 * c - 2)
                dve.reciprocal(r8[:, :, :], mbank[:, 0:2 * TILES].rearrange("p (t h) -> p t h", h=2))\
                    .then_inc(sem("recips"), 1)

            def normalise(i, c):
                dve.wait_ge(sem("mb_full"), i * 6 + 3 * c - 1)
                dve.wait_ge(sem("o_saved"), i * 2 + c)
                dve.tensor_tensor(onorm[:, :], osb[:, :], mbank, ALU.mult).then_inc(sem("normed"), 1)

            def residual(i, c):
                b = (c - 1) % 2
                dve.wait_ge(sem("mb_full"), i * 6 + 3 * c)
                if not (isinstance(i, int) and 2 * i + c - 1 < 2):
                    dve.wait_ge(sem("x_added"), i * 2 + c - 2)
                acc = xs[:, TILES * b:TILES * (b + 1), :]
                dve.scalar_tensor_tensor(out=acc, in0=mbank.rearrange("p (t d) -> p t d", d=D),
                                         scalar=tg[:, 0:1], in1=acc, op0=ALU.mult, op1=ALU.add)\
                    .then_inc(sem("x_added"), 1)

            def unit(i, b, tail, ahead, lead=False):
                c = b if lead else b + 1
                if ahead:
                    k_low(i, c, 0)
                    k_low(i, c, 1)
                    q_low(i, c, 0)
                    q_low(i, c, 1)
                    q_dup(i, c, 0)
                    q_dup(i, c, 1)
                    row_max(i, c, 0)
                    row_max(i, c, 1)
                if tail:
                    recip(i, b)
                if ahead:
                    row_max(i, c, 2)
                    row_max(i, c, 3)
                    shift_rows(i, c, 0)
                    row_max(i, c, 4)
                if tail:
                    normalise(i, b)
                if ahead:
                    row_max(i, c, 5)
                    row_max(i, c, 6)
                if tail:
                    residual(i, b)
                if ahead:
                    row_max(i, c, 7)
                    shift_rows(i, c, 1)

            unit(0, 0, False, True, lead=True)

            def pair(i, first, last):
                unit(i, 0, not first, True)
                unit(i, 1, True, not last)

            over_pairs(dve, pair)
            unit(HP, 0, True, False)

            dve.wait_ge(sem("x_added"), U)
            norm(xs, ya, 0, P, T, (sem("var"), 1), (sem("std"), 1))
            vo.settle()
            dve.tensor_copy(yhi[:, :, :], ya[:, :, :]).then_inc(sem("y_ready"), 1)
            dve.wait_ge(sem("y_ready"), 1)
            dve.tensor_tensor(ylo[:, :, :], ya[:, :, :], yhi[:, :, :].bitcast(F32), ALU.subtract).then_inc(sem("ylo_ready"), 1)
            dve.wait_ge(sem("lg_ready"), 1)
            for t in range(T):
                vo.mark(dve.max(top[:, t, :], lg[:, t, :]))
            vo.settle()
            for t in range(T):
                vo.mark(dve.match_replace(out=rest[:, t, :], in_to_replace=top[:, t, :], in_values=lg[:, t, :],
                                          imm_value=-3.0e38))
            vo.settle()
            dve.tensor_tensor(chosen[:, :, :], rest[:, :, :], lg[:, :, :], ALU.not_equal).then_inc(sem("chosen_ready"), 1)
            dve.tensor_tensor(wgt[:, :, :], lg[:, :, :], top[:, :, 0:1].broadcast_to([P, T, E]), ALU.subtract)\
                .then_inc(sem("logits_shifted"), 1)
            dve.wait_ge(sem("sth_ready"), 1)
            vo.mark(dve.scalar_tensor_tensor(out=hs[:, :], in0=sth[:, :], scalar=1.0, in1=bank(3, 2)[0:FF, :],
                                             op0=ALU.add, op1=ALU.mult))
            vo.settle()
            dve.wait_ge(sem("shared_up_full"), 1)
            dve.scalar_tensor_tensor(out=hs[:, :], in0=hs[:, :], scalar=0.5, in1=bank(5, 2)[0:FF, :],
                                     op0=ALU.mult, op1=ALU.mult).then_inc(sem("hs_ready"), 1)
            dve.wait_ge(sem("queue_full"), 1)
            dve.scalar_tensor_tensor(out=val[:, :, :], in0=bank(7).rearrange("p (t e) -> p t e", e=E), scalar=1.0,
                                     in1=chosen[:, :, :], op0=ALU.add, op1=ALU.mult).then_inc(sem("val_ready"), 1)
            dve.wait_ge(sem("logits_exp"), 1)
            vo.mark(dve.tensor_tensor(wgt[:, :, :], wgt[:, :, :], chosen[:, :, :], ALU.mult))
            vo.settle()
            vo.mark(dve.reduce_sum(den[:, :], wgt[:, :, :], AX.X))
            vo.settle()
            vo.mark(dve.reciprocal(rden[:, :], den[:, :]))
            vo.settle()
            vo.mark(dve.tensor_tensor(wgt[:, :, :], wgt[:, :, :], rden[:, :].unsqueeze(2).broadcast_to([P, T, E]),
                                      ALU.mult))
            vo.settle()
            dve.tensor_copy(whl[:, :, :, 0], wgt[:, :, :]).then_inc(sem("whl_ready"), 1)
            dve.wait_ge(sem("whl_ready"), 1)
            dve.tensor_tensor(whl[:, :, :, 1], wgt[:, :, :], whl[:, :, :, 0].bitcast(F32), ALU.subtract)\
                .then_inc(sem("whl_ready"), 1)
            dve.wait_ge(sem("consts2"), 6)
            dve.wait_ge(sem("val_ready"), 1)

            def build_take(g):
                v = val[:, :, EG * g:EG * (g + 1)] if isinstance(g, int) else val[:, :, bass.ds(EG * g, EG)]
                dve.tensor_tensor(take[:, :, :, :], v.unsqueeze(3).broadcast_to([P, T, EG, CAP]),
                                  slots[:, :].unsqueeze(1).unsqueeze(1).broadcast_to([P, T, EG, CAP]), ALU.is_equal)\
                    .then_inc(sem("take_ready"), 1)

            build_take(0)

            def build_give(g, p):
                dve.wait_ge(sem("bc_full"), g * PG + p + 1)
                dve.tensor_scalar(give[p][:, :], bank(2, 2), slot_of[:, 0:1], None, ALU.is_equal)\
                    .then_inc(sem("give_ready"), 1)

            def group(g, first, last):
                dve.wait_ge(sem("wr_full"), g + 1)
                dve.tensor_tensor(wm[:, :], bank(7)[0:2 * EG, :], own_e[:, :, :].rearrange("p e s -> p (e s)"), ALU.mult)\
                    .then_inc(sem("wm_ready"), 1)
                gu = bank(5, 2).rearrange("p (k n) -> p k n", k=PG)
                dve.wait_ge(sem("th_ready"), g + 1)
                dve.scalar_tensor_tensor(out=hh[:, :, :], in0=th[:, :, :], scalar=1.0, in1=gu[:, :, 0:FF],
                                         op0=ALU.add, op1=ALU.mult).then_inc(sem("h_half"), 1)
                dve.wait_ge(sem("h_half"), g + 1)
                dve.scalar_tensor_tensor(out=hh[:, :, :], in0=hh[:, :, :], scalar=0.5, in1=gu[:, :, FF:2 * FF],
                                         op0=ALU.mult, op1=ALU.mult).then_inc(sem("h_ready"), 1)
                build_give(g, 0)
                dve.wait_ge(sem("wt_full"), g + 1)
                dve.reduce_sum(ws[:, :], bank(6)[:, 0:2 * EG * PG].rearrange("p (k n) -> p k n", k=PG), AX.X)\
                    .then_inc(sem("ws_ready"), 1)
                if not last:
                    build_take(g + 1)
                dve.wait_ge(sem("ws_ready"), g + 1)
                dve.wait_ge(sem("y_full"), g + 1)
                dve.tensor_tensor(ys[:, :, :], bank(7).rearrange("p (k d) -> p k d", d=D),
                                  ws[:, :].unsqueeze(2).broadcast_to([P, PG, D]), ALU.mult).then_inc(sem("ys_ready"), 1)
                dve.wait_ge(sem("ys_ready"), g + 1)
                dve.tensor_copy(ehi[:, :, :], ys[:, :, :]).then_inc(sem("ehi_ready"), 1)
                dve.wait_ge(sem("ehi_ready"), g + 1)
                dve.tensor_tensor(elo[:, :, :], ys[:, :, :], ehi[:, :, :].bitcast(F32), ALU.subtract)\
                    .then_inc(sem("elo_ready"), 1)
                for p in range(1, PG):
                    build_give(g, p)

            over_groups(dve, group)
            dve.wait_ge(sem("moe_full"), 1)
            for k in range(2):
                acc = xs[:, 4 * k:4 * k + 4, :]
                dve.scalar_tensor_tensor(out=acc, in0=bank(2 + k).rearrange("p (t d) -> p t d", d=D), scalar=tg[:, 2:3],
                                         in1=acc, op0=ALU.mult, op1=ALU.add).then_inc(sem("x2_ready"), 1)
            dve.wait_ge(sem("x2_ready"), 2)

            norm(xs, ya, 0, P, T, (sem("var"), 2), (sem("std"), 2))
            vo.settle()
            dve.engine_nop().then_inc(sem("hc_ready"), 1)
            vo.mark(dve.tensor_scalar(row[:, :], small_at("b_qv_row"), tg[:, 1:2], None, ALU.mult))
            vo.settle()
            vo.mark(dve.tensor_tensor(xs[:, :, :], xs[:, :, :], row[:, :].unsqueeze(1).broadcast_to([P, T, D]), ALU.add))
            dve.wait_ge(sem("sim_full"), 1)
            dve.tensor_reduce(nmx[:, :], bank(2, 2).rearrange("p (t n) -> p t n", n=P)[:, :, 0:M], AX.X, ALU.max,
                              negate=True).then_inc(sem("nmx_ready"), 1)
            dve.wait_ge(sem("nmx_ready"), 1)
            dve.wait_ge(sem("s0_full"), 1)
            vo.mark(dve.scalar_tensor_tensor(out=mi[:, :], in0=bank(4)[:, 0:T], scalar=small_at("b_sim"), in1=nmx[:, :],
                                             op0=ALU.add, op1=ALU.subtract))
            vo.settle()
            dve.tensor_reduce(mbest[:, :], mi[:, :].rearrange("p (b t) -> p b t", b=B), AX.X, ALU.max)\
                .then_inc(sem("mbest_ready"), 1)
            dve.wait_ge(sem("mbestT_full"), 1)
            vo.mark(dve.tensor_reduce(m2[:, :], bank(7)[0:B, 0:P], AX.X, ALU.max, negate=True))
            vo.settle()
            dve.tensor_scalar(dm[:, :], ident[0:B, 0:B], m2[:, 0:1], None, ALU.mult).then_inc(sem("dm_ready"), 1)
            dve.wait_ge(sem("negm_full"), 1)
            dve.tensor_copy(negm[:, :], bank(7)[:, 0:B]).then_inc(sem("negm_ready"), 1)
            dve.wait_ge(sem("aw_ready"), T)
            vo.mark(dve.reciprocal(asum[:, :], asum[:, :]))
            vo.settle()
            dve.tensor_tensor(aw[:, :, :], aw[:, :, :], asum[:, :].unsqueeze(2).broadcast_to([P, T, M]), ALU.mult)\
                .then_inc(sem("a_ready"), 1)
            dve.wait_ge(sem("hcb_full"), 1)
            vo.mark(dve.reciprocal(rtot[:, :], bank(7)[:, 0:B]))
            vo.settle()
            vo.mark(dve.tensor_tensor(hcb[:, :], bank(7)[:, 2:2 + B], rtot[:, :], ALU.mult))
            vo.settle()
            for b in range(B):
                dve.scalar_tensor_tensor(out=wc[:, b, :], in0=wqv[:, 3, :], scalar=hcb[:, b:b + 1], in1=wqv[:, 0, :],
                                         op0=ALU.mult, op1=ALU.add).then_inc(sem("wc_ready"), 1)
            dve.wait_ge(sem("hqh_ready"), 1)
            dve.tensor_tensor(f3[:, :], hcT[:, :], hqh[:, :], ALU.mult).then_inc(sem("f3_ready"), 1)
            vo.settle()
            for k in range(2):
                dve.wait_ge(sem("hcq_full"), k + 1)
                acc = xs[:, 4 * k:4 * k + 4, :]
                dve.scalar_tensor_tensor(out=acc, in0=bank(k).rearrange("p (t d) -> p t d", d=D), scalar=tg[:, 1:2],
                                         in1=acc, op0=ALU.mult, op1=ALU.add).then_inc(sem("x3_ready"), 1)
            dve.wait_ge(sem("x3_ready"), 2)

            norm(xs, ya, 0, P, T, (sem("var"), 3), (sem("std"), 3))
            vo.settle()
            dve.engine_nop().then_inc(sem("z_ready"), 1)
            vo.mark(dve.tensor_scalar(row[:, :], small_at("b2_row"), tg[:, 3:4], None, ALU.mult))
            vo.settle()
            vo.mark(dve.tensor_tensor(xs[:, :, :], xs[:, :, :], row[:, :].unsqueeze(1).broadcast_to([P, T, D]), ALU.add))
            dve.wait_ge(sem("gB_full"), 1)
            dve.scalar_tensor_tensor(out=gB[:, :, :], in0=bank(6)[:, 0:B * E2].rearrange("p (b e) -> p b e", b=B),
                                     scalar=1.0 / N, in1=small_at("gate_b2").unsqueeze(1).broadcast_to([P, B, E2]),
                                     op0=ALU.mult, op1=ALU.add).then_inc(sem("g_ready"), 1)
            dve.scalar_tensor_tensor(out=gT[:, :], in0=bank(7)[0:E2, 0:B], scalar=1.0 / N,
                                     in1=small_at("gate_b2_col", E2).broadcast_to([E2, B]),
                                     op0=ALU.mult, op1=ALU.add).then_inc(sem("g_ready"), 1)
            dve.wait_ge(sem("g_ready"), 2)
            for b in range(B):
                vo.mark(dve.tensor_tensor(tb[:, b, :, :], small_at("Tb1").rearrange("p (c e) -> p c e", e=E2),
                                          gB[:, b, :].unsqueeze(1).broadcast_to([P, FC, E2]), ALU.mult))
            vo.settle()
            vo.mark(dve.reduce_sum(mb1[:, :, :], tb[:, :, :, :], AX.X))
            vo.settle()
            dve.tensor_tensor(mb1[:, :, :], mb1[:, :, :], small_at("b1").unsqueeze(1).broadcast_to([P, B, FC]), ALU.add)\
                .then_inc(sem("mb1_ready"), 1)
            dve.wait_ge(sem("weights_loaded"), 16 * 9)
            dve.wait_ge(sem("tw_loaded"), 32)
            for b in range(B):
                for e in range(E2):
                    if e:
                        dve.wait_ge(sem("mw1_ready"), E2 * b + e)
                    dve.scalar_tensor_tensor(out=mw1[b][:, :], in0=tw1[:, e, :], scalar=gB[:, b, e:e + 1],
                                             in1=mw1[b][:, :] if e else w1[:, :], op0=ALU.mult, op1=ALU.add)\
                        .then_inc(sem("mw1_ready"), 1)
            vo.settle()
            for b in range(B):
                dve.wait_ge(sem("ffn_full"), b + 1)
                lo, hi = TILES * b, TILES * (b + 1)
                dve.scalar_tensor_tensor(out=res[:, lo:hi, :], in0=bank(6 + b).rearrange("p (t d) -> p t d", d=D),
                                         scalar=tg[:, 3:4], in1=xs[:, lo:hi, :], op0=ALU.mult, op1=ALU.add)\
                    .then_inc(sem("out_ready"), 1)

        @block.tensor
        def _(pe):
            pe.wait_ge(sem("consts"), 2)
            for b in range(B):
                pe.wait_ge(sem("lat_normed"), b + 1)
                for t in range(TILES):
                    pe.transpose(bank(b)[:, P * t:P * (t + 1)], yb[:, TILES * b + t, :], ident[:, :])\
                        .then_inc(sem("lat_t"), 1)
            pe.wait_ge(sem("lat_normed"), B + 1)
            for b in range(B):
                pe.transpose(bank(2)[:, P * b:P * b + M], cn[0:M, b, :], ident[0:M, 0:M]).then_inc(sem("lat_t"), 1)
            for b in range(B):
                pe.transpose(bank(3)[:, P * b:P * b + M], cs[0:M, b, :], ident[0:M, 0:M]).then_inc(sem("lat_t"), 1)

            def proj_k(i, c):
                if isinstance(i, int) and 2 * i + c == 0:
                    pe.wait_ge(sem("kv_ready"), 2 * B)
                    pe.wait_ge(sem("ctxT_ready"), B)
                else:
                    pe.wait_ge(sem("max_done"), i * (4 * TILES) + 2 * TILES * c)
                pe.wait_ge(sem("wx_loaded"), (i + (c + 2) // 2) * 16)
                kv = kvT[c % 2]
                pe.matmul(xb(c, 0)[:, 0:N], wx[:, P:2 * P], kv[:, 0:N], start=True, stop=True)
                pe.matmul(xb(c, 0)[:, N:KV], wx[:, P:2 * P], kv[:, N:KV], start=True, stop=True)\
                    .then_inc(sem("x_full"), 1)

            def proj_q(i, c):
                if not (isinstance(i, int) and 2 * i + c == 0):
                    pe.wait_ge(sem("shifts"), i * 4 + 2 * c)
                pe.matmul(xb(c, 1)[:, 0:N], wx[:, 0:P], kvT[c % 2][:, 0:N], start=True, stop=True)\
                    .then_inc(sem("x_full"), 1)

            def proj_v(i, c):
                pe.wait_ge(sem("k_lo"), i * 4 + 2 * c + 2)
                for jt in range(JT):
                    w = JW[jt]
                    ins = pe.matmul(xb(c, 2)[0:w, P * jt:P * (jt + 1)], kvT[c % 2][:, P * jt:P * jt + w],
                                    wx[:, 2 * P:3 * P], start=True, stop=True)
                ins.then_inc(sem("x_full"), 1)

            def scores_for_max(i, c, r):
                b, j, h, t = c % 2, 3 + r + (r >= TILES), r // TILES, r % TILES
                if r == 0:
                    pe.wait_ge(sem("q_lo"), i * 4 + 2 * c + 2)
                elif r == 1:
                    pe.wait_ge(sem("v_ready"), i * 4 + 2 * c + 2)
                elif r == 5:
                    pe.wait_ge(sem("shifts"), i * 4 + 2 * c + 1)
                else:
                    pe.wait_ge(sem("max_done"), i * (4 * TILES) + 2 * TILES * c + r - (r != TILES))
                if t == 0:
                    pe.wait_ge(sem("q_dup"), i * 4 + 2 * c + h + 1)
                pe.matmul(xb(c, j)[:, 0:N], qq[b][:, h, P * t:P * (t + 1)], kk[b][:, h, 0:N], start=True, stop=True)
                pe.matmul(xb(c, j)[:, N:KVP], qq[b][:, h, P * t:P * (t + 1)], kk[b][:, h, N:KVP],
                          start=True, stop=True).then_inc(sem("x_full"), 1)

            def turn_max(i, c, h):
                b, j = c % 2, (7, 12)[h]
                pe.wait_ge(sem("max_done"), i * (4 * TILES) + 2 * TILES * c + TILES * (h + 1))
                pe.transpose(xb(c, j)[0:TILES, 0:P], nmax[:, b, h, :], ident[:, :]).then_inc(sem("x_full"), 1)

            def scores(i, b, jt, h):
                w = JW[jt]
                if jt == 0:
                    pe.wait_ge(sem("k_dup"), i * 4 + 2 * b + h + 1)
                    pe.wait_ge(sem("shifts"), i * 4 + 2 * b + h + 1)
                if not (isinstance(i, int) and i == 0 and b == 0 and jt == 0):
                    pe.wait_ge(sem("exp_done"), i * (4 * JT) + 2 * JT * b + 2 * jt + h - 1)
                pe.matmul(sbank[h][0:w, :], kk[b][:, h, P * jt:P * jt + w], qq[b][:, h, :], start=True, stop=False)
                pe.matmul(sbank[h][0:w, :], ko[b][0:DH + TILES, h, P * jt:P * jt + w], qlm[b][0:DH + TILES, h, :],
                          start=False, stop=True).then_inc(sem("s_full"), 1)

            def values(i, b, jt):
                w = JW[jt]
                if jt == 0:
                    if not (isinstance(i, int) and i == 0 and b == 0):
                        pe.wait_ge(sem("o_saved"), i * 2 + b)
                    pe.wait_ge(sem("v_ready"), i * 4 + 2 * b + 2)
                pe.wait_ge(sem("exp_done"), i * (4 * JT) + 2 * JT * b + 2 * jt + 2)
                for h in range(2):
                    ins = pe.matmul(obank[DH * h:DH * (h + 1), :], vv[b][0:w, jt, DH * h:DH * (h + 1)],
                                    pt[b][0:w, jt, h, :], start=(jt == 0), stop=(jt == JT - 1))
                ins.then_inc(sem("av_done"), 1)

            def sums(i, c):
                b = (c - 1) % 2
                pe.wait_ge(sem("pool_added"), i * (2 * (JT - 1)) + (JT - 1) * c)
                if not (isinstance(i, int) and 2 * i + c - 1 == 0):
                    pe.wait_ge(sem("x_added"), i * 2 + c - 1)
                for t in range(TILES):
                    for h in range(2):
                        ins = pe.matmul(mbank[:, 2 * t + h:2 * t + h + 1], psm[b][:, h, P * t:P * (t + 1)],
                                        ones_f[:, 0:1], start=True, stop=True)
                ins.then_inc(sem("mb_full"), 1)

            def spread_recip(i, c):
                pe.wait_ge(sem("recips"), i * 2 + c)
                for t in range(TILES):
                    for h in range(2):
                        ins = pe.matmul(mbank[DH * h:DH * (h + 1), P * t:P * (t + 1)],
                                        r8[:, t, h:h + 1].broadcast_to([P, DH]), ident[:, :], start=True, stop=True)
                ins.then_inc(sem("mb_full"), 1)

            def out_proj(i, c):
                pe.wait_ge(sem("normed"), i * 2 + c)
                pe.wait_ge(sem("wo_loaded"), (i + (c + 1) // 2) * 16)
                for t in range(TILES):
                    ins = pe.matmul(mbank[:, P * t:P * (t + 1)], onorm[:, P * t:P * (t + 1)], wo[:, :],
                                    start=True, stop=True)
                ins.then_inc(sem("mb_full"), 1)

            def unit(i, b, tail, ahead):
                c = b + 1
                scores(i, b, 0, 0)
                if ahead:
                    proj_k(i, c)
                scores(i, b, 0, 1)
                if tail:
                    values(i - 1 if b == 0 else i, 1 - b, JT - 1)
                if ahead:
                    proj_q(i, c)
                scores(i, b, 1, 0)
                if ahead:
                    proj_v(i, c)
                scores(i, b, 1, 1)
                values(i, b, 0)
                scores(i, b, 2, 0)
                if ahead:
                    scores_for_max(i, c, 0)
                scores(i, b, 2, 1)
                if ahead:
                    scores_for_max(i, c, 1)
                values(i, b, 1)
                if tail:
                    sums(i, b)
                scores(i, b, 3, 0)
                if ahead:
                    scores_for_max(i, c, 2)
                scores(i, b, 3, 1)
                if ahead:
                    scores_for_max(i, c, 3)
                values(i, b, 2)
                if tail:
                    spread_recip(i, b)
                scores(i, b, 4, 0)
                if ahead:
                    turn_max(i, c, 0)
                scores(i, b, 4, 1)
                if ahead:
                    scores_for_max(i, c, 4)
                values(i, b, 3)
                if ahead:
                    scores_for_max(i, c, 5)
                if tail:
                    out_proj(i, b)
                if ahead:
                    scores_for_max(i, c, 6)
                    scores_for_max(i, c, 7)
                    turn_max(i, c, 1)

            proj_k(0, 0)
            proj_q(0, 0)
            proj_v(0, 0)
            for r in range(TILES):
                scores_for_max(0, 0, r)
            turn_max(0, 0, 0)
            for r in range(TILES, 2 * TILES):
                scores_for_max(0, 0, r)
            turn_max(0, 0, 1)

            def pair(i, first, last):
                unit(i, 0, not first, True)
                unit(i, 1, True, not last)

            over_pairs(pe, pair)
            values(HP - 1, 1, JT - 1)
            sums(HP, 0)
            spread_recip(HP, 0)
            out_proj(HP, 0)

            def turn_tiles(k0, full):
                for t in range(T):
                    ins = pe.transpose(bank(k0 + t // 4)[:, P * (t % 4):P * (t % 4 + 1)], ya[:, t, :], ident[:, :])
                    if t % 4 == 3:
                        ins.then_inc(sem(full), 1)

            pe.wait_ge(sem("y_ready"), 1)
            turn_tiles(0, "yT_full")
            pe.wait_ge(sem("weights_loaded"), 16 * 9)
            for t in range(T):
                if t % 4 == 0:
                    pe.wait_ge(sem("yT_ready"), t // 4 + 1)
                ins = pe.matmul(bank(2)[:, E * t:E * (t + 1)], yT[:, t, :], rw[:, :], start=True, stop=True)
            ins.then_inc(sem("lg_full"), 1)
            for part, full in ((0, "shared_gate_full"), (1, "shared_up_full")):
                for k in range(2):
                    ins = pe.matmul(bank(3 + 2 * part + k)[0:FF, :], wsgu[:, FF * part:FF * (part + 1)],
                                    yT[:, 4 * k:4 * k + 4, :], start=True, stop=True)
                ins.then_inc(sem(full), 1)
            pe.wait_ge(sem("chosen_ready"), 1)
            pe.wait_ge(sem("consts2"), 6)
            ch = chosen[:, :, :].rearrange("p t e -> p (t e)")
            pe.matmul(bank(7), before[:, :], ch, start=True, stop=False)
            for s in range(1, T):
                ins = pe.matmul(bank(7)[:, E * s:], ones_b[:, :], ch[:, 0:E * (T - s)], start=False, stop=(s == T - 1))
            ins.then_inc(sem("queue_full"), 1)
            pe.wait_ge(sem("hs_ready"), 1)
            for k in range(2):
                pe.matmul(bank(k), wsdn[:, :], hs[:, :].rearrange("f (q k n) -> f k q n", k=2, n=P)[:, k, :, :],
                          start=True, stop=False)
            pe.wait_ge(sem("val_ready"), 1)
            for q in range(T // 2):
                ins = pe.transpose(bank(2)[:, P * q:P * (q + 1)], val[:, 2 * q:2 * q + 2, :].rearrange("p t e -> p (t e)"),
                                   ident[:, :])
            ins.then_inc(sem("valT_full"), 1)

            def gather(g, tiles):
                if tiles[0] == 0:
                    pe.wait_ge(sem("take_ready"), g + 1)
                for t in tiles:
                    for part in (yhi, ylo):
                        ins = pe.matmul(bank(4), part[:, t, :], take[:, t, :, :].rearrange("p e s -> p (e s)"),
                                        start=(t == 0 and part is yhi), stop=(t == T - 1 and part is ylo))
                if tiles[-1] == T - 1:
                    ins.then_inc(sem("g_full"), 1)

            def weight_rows(g):
                pe.wait_ge(sem("whg_ready"), g + 1)
                for t in range(T):
                    ins = pe.matmul(bank(7)[0:2 * EG, :], whg[:, t, :], take[:, t, :, :].rearrange("p e s -> p (e s)"),
                                    start=(t == 0), stop=(t == T - 1))
                ins.then_inc(sem("wr_full"), 1)

            def broadcast(g, p):
                if not (isinstance(g, int) and g == 0 and p == 0):
                    pe.wait_ge(sem("give_ready"), g * PG + p)
                for k in range(2):
                    if isinstance(g, int):
                        a = (k * E + EG * g + 2 * p) * 64
                        sel = spread[:, a:a + P]
                    else:
                        sel = spread[:, bass.ds(g * (EG * 64) + (k * E + 2 * p) * 64, P)]
                    ins = pe.matmul(bank(2 + k), sel, valT[:, :], start=True, stop=True)
                ins.then_inc(sem("bc_full"), 1)

            def scatter(g, p, last=False):
                pe.wait_ge(sem("elo_ready"), g + 1)
                pe.wait_ge(sem("give_ready"), g * PG + p + 1)
                for part in (ehi, elo):
                    for k in range(2):
                        ins = pe.matmul(bank(k), part[:, p, :], give[p][:, 512 * k:512 * (k + 1)], start=False,
                                        stop=last and part is elo)
                ins.then_inc(sem("scattered"), 1)

            pe.wait_ge(sem("ylo_ready"), 1)
            gather(0, range(T))
            weight_rows(0)
            pe.wait_ge(sem("valT_ready"), 1)

            def group(g, first, last):
                pe.wait_ge(sem("xg_ready"), g + 1)
                pe.wait_ge(sem("wgu_loaded"), (g + 1) * 16)
                if not first:
                    pe.wait_ge(sem("hT_ready"), g)
                    pe.wait_ge(sem("ws_ready"), g)
                for e in range(EG):
                    a = 256 * (e // 2)
                    ins = pe.matmul(bank(5, 2)[64 * (e % 2):64 * (e % 2) + 64, a:a + 2 * FF], xg[:, CAP * e:CAP * (e + 1)],
                                    wgu[:, e, :], start=True, stop=True)
                ins.then_inc(sem("gu_full"), 1)
                if not first:
                    scatter(g - 1, 2)
                broadcast(g, 0)
                if not first:
                    scatter(g - 1, 3)
                pe.wait_ge(sem("wm_ready"), g + 1)
                pe.wait_ge(sem("h_ready"), g + 1)
                for p in range(PG):
                    ins = pe.transpose(bank(5)[0:FF, P * p:P * (p + 1)], hh[:, p, :], ident[:, :])
                ins.then_inc(sem("ht_full"), 1)
                for p in range(PG):
                    ins = pe.transpose(bank(6)[:, 2 * EG * p:2 * EG * (p + 1)], wm[:, P * p:P * (p + 1)],
                                       ident[0:2 * EG, 0:2 * EG])
                ins.then_inc(sem("wt_full"), 1)
                broadcast(g, 1)
                pe.wait_ge(sem("hT_ready"), g + 1)
                pe.wait_ge(sem("wdn_loaded"), (g + 1) * 16)
                for e in range(EG):
                    a = D * (e // 2)
                    ins = pe.matmul(bank(7)[64 * (e % 2):64 * (e % 2) + 64, a:a + D], hT[:, CAP * e:CAP * (e + 1)],
                                    wdn[:, e, :], start=True, stop=True)
                ins.then_inc(sem("y_full"), 1)
                if not last:
                    gather(g + 1, range(0, T // 2))
                broadcast(g, 2)
                if not last:
                    gather(g + 1, range(T // 2, T))
                    pe.wait_ge(sem("ys_ready"), g + 1)
                    weight_rows(g + 1)
                broadcast(g, 3)
                scatter(g, 0)
                scatter(g, 1)

            over_groups(pe, group)
            scatter(G - 1, 2)
            scatter(G - 1, 3, last=True)
            for k in range(2):
                pe.wait_ge(sem("outT_ready"), k + 1)
                for q in range(T // 2):
                    t = 2 * q + k
                    ins = pe.transpose(bank(2 + t // 4)[:, P * (t % 4):P * (t % 4 + 1)],
                                       outT[:, 512 * k + P * q:512 * k + P * (q + 1)], ident[:, :])
            ins.then_inc(sem("moe_full"), 1)

            pe.wait_ge(sem("hc_ready"), 1)
            turn_tiles(0, "hcT_full")
            for t in range(T):
                pe.wait_ge(sem("hcp_ready"), t // 4 + 1)
                ins = pe.matmul(bank(2 + t // 4)[:, P * (t % 4):P * (t % 4) + M], hcp[:, P * t:P * (t + 1)],
                                ctxT[:, t // TILES, :], start=True, stop=True)
            ins.then_inc(sem("sim_full"), 1)
            for t in range(T):
                ins = pe.matmul(bank(4)[:, t:t + 1], hcT[:, P * t:P * (t + 1)],
                                small[:, SMALL["w_sim"][0]:SMALL["w_sim"][0] + 1], start=True, stop=True)
            ins.then_inc(sem("s0_full"), 1)
            pe.wait_ge(sem("mbest_ready"), 1)
            pe.transpose(bank(7)[0:B, 0:P], mbest[:, :], ident[:, :]).then_inc(sem("mbestT_full"), 1)
            pe.wait_ge(sem("dm_ready"), 1)
            pe.matmul(bank(7)[:, 0:B], ones_f[0:B, :], dm[:, :], start=True, stop=True).then_inc(sem("negm_full"), 1)
            pe.wait_ge(sem("a_ready"), 1)
            for t in range(T):
                ins = pe.transpose(bank(5 + t // 4)[0:M, P * (t % 4):P * (t % 4 + 1)], aw[:, t, :], ident[:, :])
            ins.then_inc(sem("aT_full"), 1)
            pe.wait_ge(sem("e8_ready"), B)
            pe.matmul(bank(7)[:, 0:B], ones_f[:, :], es[:, :], start=True, stop=True)
            for b in range(B):
                for t in range(TILES):
                    k = TILES * b + t
                    ins = pe.matmul(bank(7)[:, 2 + b:3 + b], ya[:, k, :], e8[:, k:k + 1], start=(t == 0),
                                    stop=(t == TILES - 1))
            ins.then_inc(sem("hcb_full"), 1)
            pe.wait_ge(sem("aT_ready"), 1)
            for b in range(B):
                ins = pe.matmul(bank(2 + b), cs[0:M, b, :], aT[:, N * b:N * (b + 1)], start=True, stop=True)
            ins.then_inc(sem("hqh_full"), 1)
            pe.wait_ge(sem("wc_ready"), 2)
            pe.wait_ge(sem("f3_ready"), 1)
            for t in range(T):
                dst, tok = bank(t // 4)[:, P * (t % 4):P * (t % 4 + 1)], slice(P * t, P * (t + 1))
                pe.matmul(dst, hcT[:, tok], wc[:, t // TILES, :], start=True, stop=False)
                pe.matmul(dst, hqh[:, tok], wqv[:, 1, :], start=False, stop=False)
                ins = pe.matmul(dst, f3[:, tok], wqv[:, 2, :], start=False, stop=True)
                if t % 4 == 3:
                    ins.then_inc(sem("hcq_full"), 1)

            pe.wait_ge(sem("z_ready"), 1)
            turn_tiles(2, "zT_full")
            for b in range(B):
                pe.wait_ge(sem("zT_ready"), b + 1)
                pe.matmul(bank(4 + b), gw1[:, :], hcT[:, N * b:N * (b + 1)], start=True, stop=True)\
                    .then_inc(sem("gate_full"), 1)
            pe.wait_ge(sem("hsum_ready"), B)
            for b in range(B):
                ins = pe.matmul(bank(6)[:, E2 * b:E2 * (b + 1)], hsum[:, b:b + 1].broadcast_to([P, P]), gw2[:, :],
                                start=True, stop=True)
            pe.matmul(bank(7)[0:E2, 0:B], gw2[:, :], hsum[:, :], start=True, stop=True).then_inc(sem("gB_full"), 1)
            pe.wait_ge(sem("tw_loaded"), 32)
            for b in range(B):
                pe.matmul(bank(b), ident[:, :], w2[:, :, :].rearrange("p c d -> p (c d)"), start=True, stop=False)
                for e in range(E2):
                    pe.wait_ge(sem("diag_ready"), E2 * b + e + 1)
                    ins = pe.matmul(bank(b), diag[:, b, e, :], tw2[:, e, :, :].rearrange("p c d -> p (c d)"),
                                    start=False, stop=(e == E2 - 1))
                ins.then_inc(sem("mw2_full"), 1)
            for n in range(B * FC):
                b, c = n // FC, n % FC
                if c == 0:
                    pe.wait_ge(sem("mw1_ready"), E2 * (b + 1))
                if n >= 4:
                    pe.wait_ge(sem("u_ready"), n - 3)
                pe.matmul(bank(2 + n % 4), mw1[b][:, P * c:P * (c + 1)], hcT[:, N * b:N * (b + 1)], start=True, stop=True)\
                    .then_inc(sem("u_full"), 1)
            for b in range(B):
                pe.wait_ge(sem("u_ready"), FC * (b + 1))
                pe.wait_ge(sem("mw2_ready"), b + 1)
                if b == 0:
                    pe.wait_ge(sem("g_ready"), 2)
                for t in range(TILES):
                    dst = bank(6 + b)[:, D * t:D * (t + 1)]
                    for c in range(FC):
                        pe.matmul(dst, uT[b][:, c, P * t:P * (t + 1)], mw2[b][:, c, :], start=(c == 0), stop=False)
                    ins = pe.matmul(dst, gT[:, b:b + 1].broadcast_to([E2, P]), tb2[:, :], start=False, stop=True)
                ins.then_inc(sem("ffn_full"), 1)


_IN_NAMES = ["x", "ctx", "small", "wqkv", "wout", "rw", "wgu", "wdn", "wsgu", "wsdn", "wqv", "gw1", "gw2", "w1", "tw1",
             "w2", "tw2", "tb2"]


def lay_out(a):
    import numpy as np

    small = np.zeros((P, SMALL_WIDTH), np.float32)

    def put(name, value):
        start, end = SMALL[name]
        small[:, start:end] = value

    for name, key in (("ln_l_g", "L0_xattn_ln_l_g"), ("ln_l_b", "L0_xattn_ln_l_b"), ("ln_m_g", "L0_xattn_ln_m_g"),
                      ("ln_m_b", "L0_xattn_ln_m_b"), ("gate_b1", "L1_ffn_gate_b1")):
        put(name, a[key][:, None])
    for name, key in (("g_xattn", "g_xattn"), ("g_ffn", "g_ffn"), ("b_sim", "L1_xattn_b_sim"),
                      ("gate_b2", "L1_ffn_gate_b2"), ("b_qv_row", "L1_xattn_b_qv"), ("b2_row", "L1_ffn_b2")):
        put(name, a[key][None])
    put("w_sim", a["L1_xattn_w_sim"].reshape(3, P).T)
    small[0:8, SMALL["gate_b2_col"][0]] = a["L1_ffn_gate_b2"]
    put("b1", a["L1_ffn_b1"].reshape(4, P).T)
    put("Tb1", a["L1_ffn_Tb1"].reshape(8, 4, P).transpose(2, 1, 0).reshape(P, 32))
    wq = a["L0_xattn_Wq"].reshape(P, 8, P)
    wkv = a["L0_xattn_Wkv"].reshape(P, 2, 8, P)
    gate_up = np.concatenate([a["L0_ffn_w_gate"], a["L0_ffn_w_up"]], axis=2)
    laid = {
        "x": a["x"], "ctx": a["ctx_1024"], "small": small,
        "wqkv": np.concatenate([w.transpose(1, 0, 2) for w in (wq, wkv[:, 0], wkv[:, 1])], axis=2),
        "wout": a["L0_xattn_Wout"].reshape(8, P, P),
        "rw": a["L0_ffn_router_w"].T,
        "wgu": gate_up.reshape(8, 8, P, 192).transpose(0, 2, 1, 3),
        "wdn": a["L0_ffn_w_down"].reshape(8, 8, 96, P).transpose(0, 2, 1, 3),
        "wsgu": a["L0_ffn_ws_gate_up"], "wsdn": a["L0_ffn_ws_down"],
        "wqv": a["L1_xattn_W_qv"].reshape(4, P, P).transpose(1, 0, 2),
        "gw1": a["L1_ffn_gate_w1"].T, "gw2": a["L1_ffn_gate_w2"].T,
        "w1": a["L1_ffn_W1"].T, "tw1": a["L1_ffn_TW1"].transpose(2, 0, 1),
        "w2": a["L1_ffn_W2"].T.reshape(4, P, P).transpose(1, 0, 2),
        "tw2": a["L1_ffn_TW2"].transpose(0, 2, 1).reshape(8, 4, P, P).transpose(2, 0, 1, 3),
        "tb2": a["L1_ffn_Tb2"],
    }
    return {k: np.ascontiguousarray(v) for k, v in laid.items()}


def kernel(**inputs):
    import numpy as _np
    import concourse.bacc as _bacc
    from concourse import mybir as _mybir
    from concourse.bass_utils import run_bass_kernel_spmd as _run

    nc = _bacc.Bacc("TRN2", target_bir_lowering=False, num_devices=1)
    laid = lay_out({k: _np.asarray(v) for k, v in inputs.items()})
    arrays, args = {}, []
    for name in _IN_NAMES:
        arrays[f"in_{name}_dram"] = laid[name]
        args.append(nc.dram_tensor(f"in_{name}_dram", laid[name].shape, _mybir.dt.from_np(laid[name].dtype),
                                   kind="ExternalInput").ap())
    out = nc.dram_tensor("out_dram", laid["x"].shape, _mybir.dt.float32, kind="ExternalOutput").ap()
    flamingo_block(nc, *args, out)
    r = _run(nc, [arrays], core_ids=[0])
    return r.results[0]["out_dram"]
```

```python
from contextlib import ExitStack

import concourse.bass as bass
from concourse import mybir

ALU = mybir.AluOpType
ACT = mybir.ActivationFunctionType
AX = mybir.AxisListType
F32 = mybir.dt.float32
F32R = mybir.dt.float32r
BF16 = mybir.dt.bfloat16

P = 128
EPS = 1e-5

SMALL = {}


def _place(names):
    at = 0
    for name, width in names:
        SMALL[name] = (at, at + width)
        at += width
    return at


SMALL_WIDTH = _place([
    ("ln_l_g", 1), ("ln_l_b", 1), ("ln_m_g", 1), ("ln_m_b", 1),
    ("g_xattn", 2), ("g_ffn", 2), ("w_sim", 3), ("b_sim", 1),
    ("gate_b1", 1), ("gate_b2", 8), ("gate_b2_col", 1), ("b1", 4), ("Tb1", 32),
    ("b_qv_row", 128), ("b2_row", 128),
])


class Order:

    def __init__(self, eng, sem):
        self.eng, self.sem, self.n = eng, sem, 0

    def mark(self, ins):
        ins.then_inc(self.sem, 1)
        self.n += 1

    def settle(self):
        self.eng.wait_ge(self.sem, self.n)


def flamingo_block(nc, x_in, ctx_in, small_in, wqkv_in, wout_in, rw_in, wgu_in, wdn_in, wsgu_in, wsdn_in,
                   wqv_in, gw1_in, gw2_in, w1_in, tw1_in, w2_in, tw2_in, tb2_in, out):
    B, N, D = x_in.shape
    M = ctx_in.shape[1]
    TILES = N // P
    T = B * TILES
    HP = wqkv_in.shape[0]
    DH = 64
    SCALE = float(DH) ** -0.5
    KV = N + M
    KVP = KV + KV % 2
    JT = N // P + 1
    W_LAST = KV - N
    U = B * HP
    JW = [P] * TILES + [W_LAST]
    E, CAP, FF = rw_in.shape[1], 64, wdn_in.shape[1]
    G = wgu_in.shape[0]
    EG = E // G
    PG = EG // 2
    TOPK = 8
    E2, F2 = tb2_in.shape[0], w1_in.shape[1]
    FC = F2 // P
    RECIPS = 2
    XSTEPS = 11

    with ExitStack() as stack:
        def sb(name, shape, dt=F32):
            return stack.enter_context(nc.sbuf_tensor(name, shape, dt))

        sems = {}

        def sem(name):
            if name not in sems:
                sems[name] = stack.enter_context(nc.semaphore(name))
            return sems[name]

        psum = stack.enter_context(nc.psum_tensor("psum", [P, 8 * 512], F32))

        def bank(k, n=1):
            return psum[:, 512 * k:512 * (k + n)]

        xs = sb("xs", [P, T, D])
        cs = sb("cs", [P, B, D])
        small = sb("small", [P, SMALL_WIDTH])
        ident = sb("ident", [P, P])
        ones_f = sb("ones_f", [P, P])
        eps_t = sb("eps_t", [P, 1])
        tg = sb("tg", [P, 4])
        stats = sb("stats", [P, T + B, 6])
        mv = sb("mv", [P, T + B, 2])
        std = sb("std", [P, T + B])
        rstd = sb("rstd", [P, T + B])
        ya = sb("ya", [P, T, D])
        yb = sb("yb", [P, T, D])
        cn = sb("cn", [P, B, D])
        kvT = [sb(f"kvT{b}", [P, KV]) for b in range(B)]
        ctxT = sb("ctxT", [P, B, M])

        ones_b = sb("ones_b", [P, P], BF16)
        before = sb("before", [P, P], BF16)
        spread = sb("spread", [P, P * 64], BF16)
        slots = sb("slots", [P, CAP])
        slot_of = sb("slot_of", [P, 1])
        minus_slot = sb("minus_slot", [P, 1])
        own_e = sb("own_e", [2 * EG, EG, CAP])
        ones_r = sb("ones_r", [P, 2], F32R)
        wm = sb("wm", [P, EG * CAP], F32R)
        rw = sb("rw", [P, E])
        wgu = sb("wgu", [P, EG, 2 * FF])
        wdn = sb("wdn", [FF, EG, D])
        wsgu = sb("wsgu", [P, 2 * FF])
        wsdn = sb("wsdn", [FF, D])
        wqv = sb("wqv", [P, 4, D])
        gw1 = sb("gw1", [P, D])
        gw2 = sb("gw2", [P, E2])
        w1 = sb("w1", [P, F2])
        w2 = sb("w2", [P, F2 // P, D])
        tb2 = sb("tb2", [E2, D])

        scope = ExitStack()

        def sb(name, shape, dt=F32):
            return scope.enter_context(nc.sbuf_tensor(name, shape, dt))

        wx = sb("wx", [P, 3 * P])
        wo = sb("wo", [P, D])
        qq = [sb(f"qq{b}", [P, 2, N], F32R) for b in range(B)]
        qlm = [sb(f"qlm{b}", [P, 2, N], F32R) for b in range(B)]
        kk = [sb(f"kk{b}", [P, 2, KVP], F32R) for b in range(B)]
        ko = [sb(f"ko{b}", [P, 2, KVP], F32R) for b in range(B)]
        vv = [sb(f"vv{b}", [P, JT, P]) for b in range(B)]
        pt = [sb(f"pt{b}", [P, JT, 2, N]) for b in range(B)]
        psm = [sb(f"psm{b}", [P, 2, N]) for b in range(B)]
        nmax = sb("nmax", [P, B, 2, TILES])
        mask4 = sb("mask4", [TILES, TILES, P])
        rsum = sb("rsum", [P, N])
        osb = [sb(f"osb{b}", [P, N]) for b in range(B)]
        onorm = sb("onorm", [P, N])

        scope.close()
        scope2 = stack.enter_context(ExitStack())

        def sb(name, shape, dt=F32):
            return scope2.enter_context(nc.sbuf_tensor(name, shape, dt))

        tw1 = sb("tw1", [P, E2, F2])
        tw2 = sb("tw2", [P, E2, FC, D])
        scope3 = ExitStack()

        def sb(name, shape, dt=F32):
            return scope3.enter_context(nc.sbuf_tensor(name, shape, dt))

        yhi = sb("yhi", [P, T, D], F32R)
        ylo = sb("ylo", [P, T, D], F32R)
        yT = sb("yT", [P, T, P])
        lg = sb("lg", [P, T, E])
        top = sb("top", [P, T, TOPK])
        rest = sb("rest", [P, T, E])
        chosen = sb("chosen", [P, T, E], BF16)
        wgt = sb("wgt", [P, T, E])
        den = sb("den", [P, T])
        rden = sb("rden", [P, T])
        whl = sb("whl", [P, T, E, 2], F32R)
        val = sb("val", [P, T, E])
        valT = sb("valT", [P, T // 2 * P], BF16)
        sth = sb("sth", [FF, T * P])
        hs = sb("hs", [FF, T * P])
        take = sb("take", [P, T, EG, CAP], F32R)
        give = [sb(f"give{p}", [P, T * P], F32R) for p in range(PG)]
        xg = sb("xg", [P, EG * CAP])
        th = sb("th", [P, PG, FF])
        hh = sb("hh", [P, PG, FF])
        hT = sb("hT", [FF, EG * CAP])
        whg = sb("whg", [P, T, 2 * EG], F32R)
        ws = sb("ws", [P, PG])
        gsq = sb("gsq", [P, T * P])
        ys = sb("ys", [P, PG, D])
        ehi = sb("ehi", [P, PG, D], F32R)
        elo = sb("elo", [P, PG, D], F32R)
        outT = sb("outT", [P, T * P])
        scope3.close()

        def sb(name, shape, dt=F32):
            return scope2.enter_context(nc.sbuf_tensor(name, shape, dt))

        hcT = sb("hcT", [P, T * P])
        hcp = sb("hcp", [P, T * P])
        nmx = sb("nmx", [P, T])
        aw = sb("aw", [P, T, M])
        asum = sb("asum", [P, T])
        aT = sb("aT", [M, T * P])
        hqh = sb("hqh", [P, T * P])
        f3 = sb("f3", [P, T * P])
        mi = sb("mi", [P, T])
        mbest = sb("mbest", [P, B])
        m2 = sb("m2", [B, 1])
        dm = sb("dm", [B, B])
        negm = sb("negm", [P, B])
        e8 = sb("e8", [P, T])
        es = sb("es", [P, B])
        rtot = sb("rtot", [P, B])
        hcb = sb("hcb", [P, B])
        wc = sb("wc", [P, B, D])
        row = sb("row", [P, D])
        hsum = sb("hsum", [P, B])
        gB = sb("gB", [P, B, E2])
        gT = sb("gT", [E2, B])
        tb = sb("tb", [P, B, FC, E2])
        mb1 = sb("mb1", [P, B, FC])
        mw1 = [sb(f"mw1{b}", [P, F2]) for b in range(B)]
        mw2 = [sb(f"mw2{b}", [P, FC, D]) for b in range(B)]
        diag = sb("diag", [P, B, E2, P])
        uT = [sb(f"uT{b}", [P, FC, N]) for b in range(B)]
        res = sb("res", [P, T, D])

        def small_at(name, n=P):
            a, b = SMALL[name]
            return small[0:n, a:b]

        xbuf = [bank(0, 2), bank(2, 2)]
        sbank = [bank(4), bank(5)]
        obank = bank(6)
        mbank = bank(7)

        def xb(u, j):
            return xbuf[(u + j) % 2]

        block = stack.enter_context(nc.Block())

        def over_pairs(eng, body):
            body(0, True, False)
            with eng.Fori(1, HP - 1) as i:
                body(i, False, False)
            body(HP - 1, False, True)

        def over_groups(eng, body):
            body(0, True, False)
            with eng.Fori(1, G - 1) as g:
                body(g, False, False)
            body(G - 1, False, True)

        @block.sync
        def _(sp):
            for b in range(B):
                sp.dma_start(xs[:, TILES * b:TILES * (b + 1), :],
                             x_in[b].rearrange("(t p) d -> p t d", p=P)).then_inc(sem(f"x_loaded{b}"), 16)
                if b == 0:
                    sp.dma_start(small[:, :], small_in).then_inc(sem("small_loaded"), 16)
            sp.dma_start(cs[0:M, :, :], ctx_in.rearrange("b m d -> m b d")).then_inc(sem("ctx_loaded"), 16)
            sp.dma_start(wx[:, :], wqkv_in[0]).then_inc(sem("wx_loaded"), 16)
            sp.dma_start(wo[:, :], wout_in[0]).then_inc(sem("wo_loaded"), 16)

            def pair(i, first, last):
                if not last:
                    sp.wait_ge(sem("x_full"), i * (2 * XSTEPS) + XSTEPS + 3)
                    src = wqkv_in[i + 1] if isinstance(i, int) else wqkv_in[bass.ds(i + 1, 1)].rearrange("a p n -> p (a n)")
                    sp.dma_start(wx[:, :], src).then_inc(sem("wx_loaded"), 16)
                if not first:
                    sp.wait_ge(sem("mb_full"), i * 4)
                    src = wout_in[i] if isinstance(i, int) else wout_in[bass.ds(i, 1)].rearrange("a p n -> p (a n)")
                    sp.dma_start(wo[:, :], src).then_inc(sem("wo_loaded"), 16)

            later = ((rw, rw_in), (wsgu, wsgu_in), (wsdn, wsdn_in), (wgu, wgu_in[0]), (wdn, wdn_in[0]), (wqv, wqv_in),
                     (gw1, gw1_in), (gw2, gw2_in), (w1, w1_in), (w2, w2_in), (tb2, tb2_in))
            for dst, src in later:
                name = {"wgu": "wgu_loaded", "wdn": "wdn_loaded"}.get(dst.name, "weights_loaded")
                sp.dma_start(dst[(slice(None),) * len(dst.shape)], src).then_inc(sem(name), 16)

            over_pairs(sp, pair)
            sp.wait_ge(sem("x_added"), U + 1)
            sp.dma_start(tw1[:, :, :], tw1_in).then_inc(sem("tw_loaded"), 16)
            sp.dma_start(tw2[:, :, :, :], tw2_in).then_inc(sem("tw_loaded"), 16)

            def group(g, first, last):
                if last:
                    return
                sp.wait_ge(sem("gu_full"), g + 1)
                src = wgu_in[g + 1] if isinstance(g, int) else wgu_in[bass.ds(g + 1, 1)].rearrange("a p e n -> p (a e) n")
                sp.dma_start(wgu[:, :, :], src).then_inc(sem("wgu_loaded"), 16)
                sp.wait_ge(sem("y_full"), g + 1)
                src = wdn_in[g + 1] if isinstance(g, int) else wdn_in[bass.ds(g + 1, 1)].rearrange("a p e n -> p (a e) n")
                sp.dma_start(wdn[:, :, :], src).then_inc(sem("wdn_loaded"), 16)

            over_groups(sp, group)
            for b in range(B):
                sp.wait_ge(sem("out_ready"), b + 1)
                sp.dma_start(out[b].rearrange("(t p) d -> p t d", p=P), res[:, TILES * b:TILES * (b + 1), :])\
                    .then_inc(sem("out_stored"), 16)
            sp.wait_ge(sem("out_stored"), 16 * B)

        @block.gpsimd
        def _(pool):
            po = Order(pool, sem("pool_self"))
            po.mark(pool.memset(ident[:, :], 0.0))
            po.mark(pool.memset(mask4[:, :, :], 0.0))
            po.mark(pool.memset(ones_f[:, :], 1.0))
            po.mark(pool.memset(eps_t[:, :], EPS))
            po.settle()
            pool.affine_select(out=ident[:, :], in_=ident[:, :], compare_op=ALU.not_equal, fill=1.0,
                               base=0, pattern=[[-1, P]], channel_multiplier=1).then_inc(sem("consts"), 1)
            pool.affine_select(out=mask4[:, :, :], in_=mask4[:, :, :], compare_op=ALU.not_equal, fill=1.0,
                               base=0, pattern=[[-1, TILES], [0, P]], channel_multiplier=1).then_inc(sem("consts"), 1)
            for b in range(B):
                for t in (qlm[b], kk[b]):
                    pool.memset(t[:, :, :].bitcast(F32), 0.0).then_inc(sem("pads"), 1)
                pool.memset(ko[b][:, :, :].bitcast(F32), 1.0).then_inc(sem("pads"), 1)

            po.mark(pool.memset(spread[:, :], 0.0))
            po.mark(pool.memset(before[:, :], 1.0))
            po.mark(pool.memset(ones_b[:, :], 1.0))
            po.mark(pool.memset(own_e[:, :, :], 0.0))
            po.mark(pool.memset(ones_r[:, :].bitcast(F32), 1.0))
            po.mark(pool.memset(wm[:, :].bitcast(F32), 0.0))
            po.settle()
            pool.affine_select(out=spread[:, :], in_=spread[:, :], compare_op=ALU.not_equal, fill=1.0,
                               base=0, pattern=[[-1, P], [0, 64]], channel_multiplier=1).then_inc(sem("consts2"), 1)
            pool.affine_select(out=before[:, :], in_=before[:, :], compare_op=ALU.is_gt, fill=0.0,
                               base=0, pattern=[[1, P]], channel_multiplier=-1).then_inc(sem("consts2"), 1)
            for k in range(2):
                po.mark(pool.affine_select(out=own_e[:, :, :], in_=own_e[:, :, :], compare_op=ALU.not_equal, fill=1.0,
                                           base=-k, pattern=[[-2, EG], [0, CAP]], channel_multiplier=1))
                po.settle()
            pool.engine_nop().then_inc(sem("consts2"), 1)
            pool.iota(slots[:, :], pattern=[[1, CAP]], base=1, channel_multiplier=0,
                      allow_small_or_imprecise_dtypes=True).then_inc(sem("consts2"), 1)
            n = 4
            for sign, dst in ((1, slot_of), (-1, minus_slot)):
                for h in range(2):
                    pool.wait_ge(sem("consts2"), n)
                    pool.iota(dst[64 * h:64 * (h + 1), :], pattern=[[0, 1]], base=sign, channel_multiplier=sign,
                              allow_small_or_imprecise_dtypes=True).then_inc(sem("consts2"), 1)
                    n += 1

            pool.wait_ge(sem("consts2"), 8)

            def unit(i, b):
                pool.wait_ge(sem("exp_done"), i * (4 * JT) + 2 * JT * b + 4)
                if not (isinstance(i, int) and i == 0):
                    pool.wait_ge(sem("mb_full"), i * 4 + 2 * b - 3)
                pool.tensor_tensor(psm[b][:, :, :], pt[b][:, 0, :, :], pt[b][:, 1, :, :], ALU.add)\
                    .then_inc(sem("pool_added"), 1)
                for jt in range(2, JT):
                    w = JW[jt]
                    pool.wait_ge(sem("exp_done"), i * (4 * JT) + 2 * JT * b + 2 * jt + 2)
                    pool.wait_ge(sem("pool_added"), i * (2 * (JT - 1)) + (JT - 1) * b + jt - 1)
                    pool.tensor_tensor(psm[b][0:w, :, :], psm[b][0:w, :, :], pt[b][0:w, jt, :, :], ALU.add)\
                        .then_inc(sem("pool_added"), 1)

            def pair(i, first, last):
                for b in range(B):
                    unit(i, b)

            over_pairs(pool, pair)

            def group_weights(g):
                c = 2 * EG * g
                src = whl[:, :, :, :].rearrange("p t e k -> p t (e k)")
                src = src[:, :, c:c + 2 * EG] if isinstance(g, int) else src[:, :, bass.ds(c, 2 * EG)]
                pool.tensor_copy(whg[:, :, :], src).then_inc(sem("whg_ready"), 1)

            pool.wait_ge(sem("whl_ready"), 2)
            group_weights(0)

            def group(g, first, last):
                if not last:
                    pool.wait_ge(sem("wr_full"), g + 1)
                    group_weights(g + 1)

            over_groups(pool, group)

        @block.scalar
        def _(act):
            act.wait_ge(sem("small_loaded"), 16)
            act.activation(tg[:, :], small[:, SMALL["g_xattn"][0]:SMALL["g_ffn"][1]], ACT.Tanh).then_inc(sem("gates"), 1)
            act.wait_ge(sem("consts"), 2)
            for n in range(2 * B + 1):
                act.wait_ge(sem("var0"), n + 1)
                a, b = (T, T + B) if n == 2 * B else (TILES * (n // 2), TILES * (n // 2 + 1))
                rows = M if n == 2 * B else P
                act.activation(std[0:rows, a:b], mv[0:rows, a:b, 1], ACT.Sqrt, bias=eps_t[0:rows, :])\
                    .then_inc(sem("std0"), 1)
            lat_g, lat_b = small_at("ln_l_g"), small_at("ln_l_b")
            for b in range(B):
                act.wait_ge(sem("lat_t"), TILES * (b + 1))
                act.activation(kvT[b][:, 0:N], bank(b), ACT.Identity, scale=lat_g, bias=lat_b).then_inc(sem("kv_ready"), 1)
            act.wait_ge(sem("lat_t"), TILES * B + B)
            act.activation(kvT[0][:, N:KV], bank(2)[:, 0:M], ACT.Identity, scale=small_at("ln_m_g"),
                           bias=small_at("ln_m_b")).then_inc(sem("kv_ready"), 1)
            act.activation(kvT[1][:, N:KV], bank(2)[:, P:P + M], ACT.Identity, scale=small_at("ln_m_g"),
                           bias=small_at("ln_m_b")).then_inc(sem("kv_ready"), 1)
            act.wait_ge(sem("pads"), 3 * B)

            def exp(i, b, jt, h):
                w = JW[jt]
                act.wait_ge(sem("s_full"), i * (4 * JT) + 2 * JT * b + 2 * jt + h + 1)
                act.activation(pt[b][0:w, jt, h, :], sbank[h][0:w, :], ACT.Exp, scale=SCALE)\
                    .then_inc(sem("exp_done"), 1)

            def round_k(i, c, h):
                b = c % 2
                if h == 0:
                    act.wait_ge(sem("x_full"), i * (2 * XSTEPS) + XSTEPS * c + 1)
                act.activation(kk[b][0:DH, h, 0:KV], xb(c, 0)[DH * h:DH * (h + 1), 0:KV], ACT.Copy)\
                    .then_inc(sem("k_hi"), 1)

            def round_q(i, c, h):
                b = c % 2
                if h == 0:
                    act.wait_ge(sem("x_full"), i * (2 * XSTEPS) + XSTEPS * c + 2)
                act.activation(qq[b][0:DH, h, :], xb(c, 1)[DH * h:DH * (h + 1), 0:N], ACT.Copy)\
                    .then_inc(sem("q_hi"), 1)

            def save_v(i, c):
                b = c % 2
                act.wait_ge(sem("x_full"), i * (2 * XSTEPS) + XSTEPS * c + 3)
                act.activation(vv[b][:, 0:TILES, :], xb(c, 2)[:, 0:N], ACT.Copy).then_inc(sem("v_ready"), 1)
                act.activation(vv[b][0:W_LAST, TILES, :], xb(c, 2)[0:W_LAST, N:N + P], ACT.Copy)\
                    .then_inc(sem("v_ready"), 1)

            def copy_k(i, c, h):
                b = c % 2
                act.wait_ge(sem("k_hi"), i * 4 + 2 * c + h + 1)
                act.activation(ko[b][0:DH, h, 0:KV], kk[b][0:DH, h, 0:KV].bitcast(F32), ACT.Copy)\
                    .then_inc(sem("k_dup"), 1)

            def copy_q(i, c, h):
                b = c % 2
                act.wait_ge(sem("q_hi"), i * 4 + 2 * c + h + 1)
                act.activation(qq[b][DH:P, h, :], qq[b][0:DH, h, :].bitcast(F32), ACT.Copy)\
                    .then_inc(sem("q_dup"), 1)

            def save_o(i, c):
                act.wait_ge(sem("av_done"), i * (2 * JT) + JT * c)
                if not (isinstance(i, int) and 2 * i + c - 1 < 2):
                    act.wait_ge(sem("normed"), i * 2 + c - 1)
                act.activation(osb[(c - 1) % 2][:, :], obank, ACT.Copy).then_inc(sem("o_saved"), 1)

            round_k(0, 0, 0)
            round_k(0, 0, 1)
            round_q(0, 0, 0)
            round_q(0, 0, 1)
            copy_q(0, 0, 0)
            copy_q(0, 0, 1)
            save_v(0, 0)
            copy_k(0, 0, 0)
            copy_k(0, 0, 1)

            def unit(i, b, tail, ahead):
                c = b + 1
                if not (isinstance(i, int) and i == 0):
                    act.wait_ge(sem("pool_added"), i * (2 * (JT - 1)) + (JT - 1) * (b - 1))
                exp(i, b, 0, 0)
                if ahead:
                    round_k(i, c, 0)
                    round_k(i, c, 1)
                if tail:
                    save_o(i, b)
                exp(i, b, 0, 1)
                if ahead:
                    round_q(i, c, 0)
                    round_q(i, c, 1)
                exp(i, b, 1, 0)
                if ahead:
                    copy_q(i, c, 0)
                    copy_q(i, c, 1)
                    save_v(i, c)
                exp(i, b, 1, 1)
                exp(i, b, 2, 0)
                if ahead:
                    copy_k(i, c, 0)
                    copy_k(i, c, 1)
                exp(i, b, 2, 1)
                for jt in range(3, JT):
                    exp(i, b, jt, 0)
                    exp(i, b, jt, 1)

            def pair(i, first, last):
                unit(i, 0, not first, True)
                unit(i, 1, True, not last)

            over_pairs(act, pair)
            save_o(HP, 0)

            def root(n):
                act.wait_ge(sem("var"), n)
                act.activation(std[:, 0:T], mv[:, 0:T, 1], ACT.Sqrt, bias=eps_t[:, :]).then_inc(sem("std"), 1)

            root(1)
            for k in range(2):
                act.wait_ge(sem("yT_full"), k + 1)
                act.activation(yT[:, 4 * k:4 * k + 4, :], bank(k).rearrange("p (t n) -> p t n", n=P), ACT.Copy)\
                    .then_inc(sem("yT_ready"), 1)
            act.wait_ge(sem("lg_full"), 1)
            act.activation(lg[:, :, :], bank(2).rearrange("p (t e) -> p t e", e=E), ACT.Copy).then_inc(sem("lg_ready"), 1)
            act.wait_ge(sem("shared_gate_full"), 1)
            act.activation(sth[:, :], bank(3, 2)[0:FF, :], ACT.Tanh, scale=0.5).then_inc(sem("sth_ready"), 1)
            act.wait_ge(sem("logits_shifted"), 1)
            act.activation(wgt[:, :, :], wgt[:, :, :], ACT.Exp).then_inc(sem("logits_exp"), 1)
            act.wait_ge(sem("valT_full"), 1)
            act.activation(valT[:, :], bank(2), ACT.Copy).then_inc(sem("valT_ready"), 1)

            def save_gathered(n):
                act.wait_ge(sem("g_full"), n)
                act.activation(xg[:, :], bank(4), ACT.Copy).then_inc(sem("xg_ready"), 1)

            save_gathered(1)

            def even_give(g, n):
                act.wait_ge(sem("bc_full"), g * PG + 2 * n + 1)
                if not (isinstance(g, int) and g == 0 and n == 0):
                    act.wait_ge(sem("give_even_ready"), g * 2 + n)
                act.activation(gsq[:, :], bank(2, 2), ACT.Square, bias=minus_slot[:, 0:1]).then_inc(sem("gsq_ready"), 1)
                act.wait_ge(sem("gsq_ready"), g * 2 + n + 1)
                act.activation(give[2 * n][:, :], gsq[:, :], ACT.Relu, bias=ones_f[:, 0:1], scale=-2.0)\
                    .then_inc(sem("give_even_ready"), 1)

            def group(g, first, last):
                act.wait_ge(sem("gu_full"), g + 1)
                gate = bank(5, 2).rearrange("p (k n) -> p k n", k=PG)[:, :, 0:FF]
                act.activation(th[:, :, :], gate, ACT.Tanh, scale=0.5).then_inc(sem("th_ready"), 1)
                act.wait_ge(sem("ht_full"), g + 1)
                act.activation(hT[:, :], bank(5)[0:FF, :], ACT.Copy).then_inc(sem("hT_ready"), 1)
                even_give(g, 0)
                if not last:
                    save_gathered(g + 2)
                even_give(g, 1)

            over_groups(act, group)
            for k in range(2):
                act.wait_ge(sem("scattered"), PG * G)
                act.activation(outT[:, 512 * k:512 * (k + 1)], bank(k), ACT.Copy).then_inc(sem("outT_ready"), 1)

            root(2)
            for k in range(2):
                act.wait_ge(sem("hcT_full"), k + 1)
                act.activation(hcT[:, 512 * k:512 * (k + 1)], bank(k), ACT.Copy).then_inc(sem("hcT_ready"), 1)
                act.activation(hcp[:, 512 * k:512 * (k + 1)], bank(k), ACT.Identity, scale=small[:, SMALL["w_sim"][0] + 2:SMALL["w_sim"][0] + 3],
                               bias=small[:, SMALL["w_sim"][0] + 1:SMALL["w_sim"][0] + 2]).then_inc(sem("hcp_ready"), 1)
            act.wait_ge(sem("nmx_ready"), 1)
            for t in range(T):
                act.activation(aw[:, t, :], bank(2 + t // 4)[:, P * (t % 4):P * (t % 4) + M], ACT.Exp,
                               bias=nmx[:, t:t + 1], accum_out=asum[:, t:t + 1]).then_inc(sem("aw_ready"), 1)
            act.wait_ge(sem("negm_ready"), 1)
            for b in range(B):
                act.activation(e8[:, TILES * b:TILES * (b + 1)], mi[:, TILES * b:TILES * (b + 1)], ACT.Exp,
                               bias=negm[:, b:b + 1], accum_out=es[:, b:b + 1]).then_inc(sem("e8_ready"), 1)
            act.wait_ge(sem("aT_full"), 1)
            act.activation(aT[:, :], bank(5, 2)[0:M, :], ACT.Copy).then_inc(sem("aT_ready"), 1)
            act.wait_ge(sem("hqh_full"), 1)
            act.activation(hqh[:, :], bank(2, 2), ACT.Copy).then_inc(sem("hqh_ready"), 1)

            root(3)
            for k in range(2):
                act.wait_ge(sem("zT_full"), k + 1)
                act.activation(hcT[:, 512 * k:512 * (k + 1)], bank(2 + k), ACT.Copy).then_inc(sem("zT_ready"), 1)
            for b in range(B):
                act.wait_ge(sem("gate_full"), b + 1)
                act.activation(hcp[:, 512 * b:512 * (b + 1)], bank(4 + b), ACT.Relu, bias=small_at("gate_b1"),
                               accum_out=hsum[:, b:b + 1]).then_inc(sem("hsum_ready"), 1)
            act.wait_ge(sem("g_ready"), 2)
            for b in range(B):
                for e in range(E2):
                    act.activation(diag[:, b, e, :], ident[:, :], ACT.Copy, scale=gB[:, b, e:e + 1])\
                        .then_inc(sem("diag_ready"), 1)
            for b in range(B):
                act.wait_ge(sem("mw2_full"), b + 1)
                act.activation(mw2[b][:, :, :], bank(b).rearrange("p (c d) -> p c d", d=D), ACT.Copy)\
                    .then_inc(sem("mw2_ready"), 1)
            act.wait_ge(sem("mb1_ready"), 1)
            for n in range(B * FC):
                b, c = n // FC, n % FC
                act.wait_ge(sem("u_full"), n + 1)
                act.activation(uT[b][:, c, :], bank(2 + n % 4), ACT.Gelu_apprx_tanh, bias=mb1[:, b, c:c + 1])\
                    .then_inc(sem("u_ready"), 1)

        @block.vector
        def _(dve):
            vo = Order(dve, sem("dve_self"))

            def norm(src, dst, a, rows, n, var, stdev):
                for t in range(n):
                    vo.mark(dve.bn_stats(stats[0:rows, a + t, :], src[0:rows, t, :]))
                vo.settle()
                for t in range(n):
                    ins = dve.bn_aggr(mv[0:rows, a + t, :], stats[0:rows, a + t, :])
                ins.then_inc(var[0], 1)
                dve.wait_ge(*stdev)
                vo.mark(dve.reciprocal(rstd[0:rows, a:a + n], std[0:rows, a:a + n]))
                vo.settle()
                dve.wait_ge(var[0], var[1])
                for t in range(n):
                    vo.mark(dve.tensor_scalar(dst[0:rows, t, :], src[0:rows, t, :], mv[0:rows, a + t, 0:1],
                                              rstd[0:rows, a + t:a + t + 1], ALU.subtract, ALU.mult))

            for b in range(B):
                dve.wait_ge(sem(f"x_loaded{b}"), 16)
                lo, hi = TILES * b, TILES * (b + 1)
                norm(xs[:, lo:hi, :], ya[:, lo:hi, :], lo, P, TILES, (sem("var0"), 2 * b + 1), (sem("std0"), 2 * b + 1))
                vo.settle()
                norm(ya[:, lo:hi, :], yb[:, lo:hi, :], lo, P, TILES, (sem("var0"), 2 * b + 2), (sem("std0"), 2 * b + 2))
                vo.settle()
                dve.engine_nop().then_inc(sem("lat_normed"), 1)
            dve.wait_ge(sem("ctx_loaded"), 16)
            norm(cs[:, :, :], cn[:, :, :], T, M, B, (sem("var0"), 2 * B + 1), (sem("std0"), 2 * B + 1))
            vo.settle()
            dve.engine_nop().then_inc(sem("lat_normed"), 1)
            dve.wait_ge(sem("lat_t"), TILES * B + 2 * B)
            dve.tensor_copy(ctxT[:, 0, :], bank(3)[:, 0:M]).then_inc(sem("ctxT_ready"), 1)
            dve.tensor_copy(ctxT[:, 1, :], bank(3)[:, P:P + M]).then_inc(sem("ctxT_ready"), 1)
            dve.wait_ge(sem("gates"), 1)
            dve.wait_ge(sem("pads"), 3 * B)

            dve.engine_nop().then_inc(sem("x_added"), 1)
            dve.engine_nop().then_inc(sem("normed"), 1)

            def k_low(i, c, h):
                b = c % 2
                dve.wait_ge(sem("k_hi"), i * 4 + 2 * c + 2)
                dve.tensor_tensor(kk[b][DH:P, h, 0:KV], xb(c, 0)[DH * h:DH * (h + 1), 0:KV],
                                  kk[b][0:DH, h, 0:KV].bitcast(F32), ALU.subtract).then_inc(sem("k_lo"), 1)

            def q_low(i, c, h):
                b = c % 2
                dve.wait_ge(sem("q_hi"), i * 4 + 2 * c + 2)
                dve.tensor_tensor(qlm[b][0:DH, h, :], xb(c, 1)[DH * h:DH * (h + 1), 0:N],
                                  qq[b][0:DH, h, :].bitcast(F32), ALU.subtract).then_inc(sem("q_lo"), 1)

            def row_max(i, c, r):
                b, j = c % 2, 3 + r
                dve.wait_ge(sem("x_full"), i * (2 * XSTEPS) + XSTEPS * c + j + 1)
                dve.tensor_reduce(nmax[:, b, r // TILES, r % TILES:r % TILES + 1], xb(c, j)[:, 0:KV], AX.X, ALU.max,
                                  negate=True).then_inc(sem("max_done"), 1)

            def shift_rows(i, c, h):
                b = c % 2
                dve.wait_ge(sem("max_turned"), i * 4 + 2 * c + h + 1)
                dve.tensor_tensor(qlm[b][DH:DH + TILES, h, :].rearrange("p (t n) -> p t n", n=P),
                                  sbank[h][0:TILES, 0:P].unsqueeze(1).broadcast_to([TILES, TILES, P]),
                                  mask4[:, :, :], ALU.mult).then_inc(sem("shifts"), 1)

            def recip(i, c, part):
                if part == 0:
                    dve.wait_ge(sem("mb_full"), i * 4 + 2 * c + 1)
                a, e = part * (N // RECIPS), (part + 1) * (N // RECIPS)
                dve.reciprocal(rsum[:, a:e], mbank[:, a:e]).then_inc(sem("recips"), 1)

            def normalise(i, c):
                dve.wait_ge(sem("recips"), i * (2 * RECIPS) + RECIPS * (c + 1))
                dve.wait_ge(sem("o_saved"), i * 2 + c + 1)
                dve.tensor_tensor(onorm[:, :], osb[c % 2][:, :], rsum[:, :], ALU.mult).then_inc(sem("normed"), 1)

            def residual(i, c):
                b = c % 2
                dve.wait_ge(sem("mb_full"), i * 4 + 2 * c + 2)
                if not (isinstance(i, int) and 2 * i + c < 2):
                    dve.wait_ge(sem("x_added"), i * 2 + c + 1)
                acc = xs[:, TILES * b:TILES * (b + 1), :]
                dve.scalar_tensor_tensor(out=acc, in0=mbank.rearrange("p (t d) -> p t d", d=D),
                                         scalar=tg[:, 0:1], in1=acc, op0=ALU.mult, op1=ALU.add)\
                    .then_inc(sem("x_added"), 1)

            def unit(i, b, tail, ahead):
                c = b + 1
                shift_rows(i, b, 1)
                if ahead:
                    k_low(i, c, 0)
                    k_low(i, c, 1)
                    q_low(i, c, 0)
                    q_low(i, c, 1)
                if tail:
                    recip(i, b - 2, 0)
                if ahead:
                    row_max(i, c, 0)
                    row_max(i, c, 1)
                if tail:
                    recip(i, b - 2, 1)
                if ahead:
                    row_max(i, c, 2)
                    row_max(i, c, 3)
                if tail:
                    normalise(i, b - 2)
                if ahead:
                    row_max(i, c, 4)
                    row_max(i, c, 5)
                    shift_rows(i, c, 0)
                    row_max(i, c, 6)
                if tail:
                    residual(i, b - 2)
                if ahead:
                    row_max(i, c, 7)

            for h in range(2):
                k_low(0, 0, h)
            for h in range(2):
                q_low(0, 0, h)
            for r in range(2 * TILES):
                row_max(0, 0, r)
            shift_rows(0, 0, 0)

            def pair(i, first, last):
                unit(i, 0, not first, True)
                unit(i, 1, not first, not last)

            over_pairs(dve, pair)
            for c in range(2):
                for part in range(RECIPS):
                    recip(HP - 1, c, part)
                normalise(HP - 1, c)
                residual(HP - 1, c)

            dve.wait_ge(sem("x_added"), U + 1)
            norm(xs, ya, 0, P, T, (sem("var"), 1), (sem("std"), 1))
            vo.settle()
            dve.tensor_copy(yhi[:, :, :], ya[:, :, :]).then_inc(sem("y_ready"), 1)
            dve.wait_ge(sem("y_ready"), 1)
            dve.tensor_tensor(ylo[:, :, :], ya[:, :, :], yhi[:, :, :].bitcast(F32), ALU.subtract).then_inc(sem("ylo_ready"), 1)
            dve.wait_ge(sem("lg_ready"), 1)
            for t in range(T):
                vo.mark(dve.max(top[:, t, :], lg[:, t, :]))
            vo.settle()
            for t in range(T):
                vo.mark(dve.match_replace(out=rest[:, t, :], in_to_replace=top[:, t, :], in_values=lg[:, t, :],
                                          imm_value=-3.0e38))
            vo.settle()
            dve.tensor_tensor(chosen[:, :, :], rest[:, :, :], lg[:, :, :], ALU.not_equal).then_inc(sem("chosen_ready"), 1)
            dve.tensor_tensor(wgt[:, :, :], lg[:, :, :], top[:, :, 0:1].broadcast_to([P, T, E]), ALU.subtract)\
                .then_inc(sem("logits_shifted"), 1)
            dve.wait_ge(sem("sth_ready"), 1)
            vo.mark(dve.scalar_tensor_tensor(out=hs[:, :], in0=sth[:, :], scalar=1.0, in1=bank(3, 2)[0:FF, :],
                                             op0=ALU.add, op1=ALU.mult))
            vo.settle()
            dve.wait_ge(sem("shared_up_full"), 1)
            dve.scalar_tensor_tensor(out=hs[:, :], in0=hs[:, :], scalar=0.5, in1=bank(5, 2)[0:FF, :],
                                     op0=ALU.mult, op1=ALU.mult).then_inc(sem("hs_ready"), 1)
            dve.wait_ge(sem("queue_full"), 1)
            dve.scalar_tensor_tensor(out=val[:, :, :], in0=bank(7).rearrange("p (t e) -> p t e", e=E), scalar=1.0,
                                     in1=chosen[:, :, :], op0=ALU.add, op1=ALU.mult).then_inc(sem("val_ready"), 1)
            dve.wait_ge(sem("logits_exp"), 1)
            vo.mark(dve.tensor_tensor(wgt[:, :, :], wgt[:, :, :], chosen[:, :, :], ALU.mult))
            vo.settle()
            vo.mark(dve.reduce_sum(den[:, :], wgt[:, :, :], AX.X))
            vo.settle()
            vo.mark(dve.reciprocal(rden[:, :], den[:, :]))
            vo.settle()
            vo.mark(dve.tensor_tensor(wgt[:, :, :], wgt[:, :, :], rden[:, :].unsqueeze(2).broadcast_to([P, T, E]),
                                      ALU.mult))
            vo.settle()
            dve.tensor_copy(whl[:, :, :, 0], wgt[:, :, :]).then_inc(sem("whl_ready"), 1)
            dve.wait_ge(sem("whl_ready"), 1)
            dve.tensor_tensor(whl[:, :, :, 1], wgt[:, :, :], whl[:, :, :, 0].bitcast(F32), ALU.subtract)\
                .then_inc(sem("whl_ready"), 1)
            dve.wait_ge(sem("consts2"), 8)
            dve.wait_ge(sem("val_ready"), 1)

            def build_take(g):
                v = val[:, :, EG * g:EG * (g + 1)] if isinstance(g, int) else val[:, :, bass.ds(EG * g, EG)]
                dve.tensor_tensor(take[:, :, :, :], v.unsqueeze(3).broadcast_to([P, T, EG, CAP]),
                                  slots[:, :].unsqueeze(1).unsqueeze(1).broadcast_to([P, T, EG, CAP]), ALU.is_equal)\
                    .then_inc(sem("take_ready"), 1)

            build_take(0)

            def odd_give(g, n):
                dve.wait_ge(sem("bc_full"), g * PG + 2 * n + 2)
                dve.tensor_scalar(give[2 * n + 1][:, :], bank(2, 2), slot_of[:, 0:1], None, ALU.is_equal)\
                    .then_inc(sem("give_odd_ready"), 1)

            def group(g, first, last):
                dve.wait_ge(sem("wr_full"), g + 1)
                dve.tensor_tensor(wm[0:2 * EG, :], bank(7)[0:2 * EG, :], own_e[:, :, :].rearrange("p e s -> p (e s)"), ALU.mult)\
                    .then_inc(sem("wm_ready"), 1)
                if not first:
                    odd_give(g - 1, 1)
                gu = bank(5, 2).rearrange("p (k n) -> p k n", k=PG)
                dve.wait_ge(sem("th_ready"), g + 1)
                dve.scalar_tensor_tensor(out=hh[:, :, :], in0=th[:, :, :], scalar=1.0, in1=gu[:, :, 0:FF],
                                         op0=ALU.add, op1=ALU.mult).then_inc(sem("h_half"), 1)
                dve.wait_ge(sem("h_half"), g + 1)
                dve.scalar_tensor_tensor(out=hh[:, :, :], in0=hh[:, :, :], scalar=0.5, in1=gu[:, :, FF:2 * FF],
                                         op0=ALU.mult, op1=ALU.mult).then_inc(sem("h_ready"), 1)
                if not last:
                    build_take(g + 1)
                dve.wait_ge(sem("ws_full"), g + 1)
                dve.wait_ge(sem("y_full"), g + 1)
                dve.tensor_copy(ws[:, :], bank(6)[:, 0:2 * PG].rearrange("p (k n) -> p k n", n=2)[:, :, 0])\
                    .then_inc(sem("ws_ready"), 1)
                dve.wait_ge(sem("ws_ready"), g + 1)
                dve.tensor_tensor(ys[:, :, :], bank(7).rearrange("p (k d) -> p k d", d=D),
                                  ws[:, :].unsqueeze(2).broadcast_to([P, PG, D]), ALU.mult).then_inc(sem("ys_ready"), 1)
                dve.wait_ge(sem("ys_ready"), g + 1)
                dve.tensor_copy(ehi[:, :, :], ys[:, :, :]).then_inc(sem("ehi_ready"), 1)
                dve.wait_ge(sem("ehi_ready"), g + 1)
                dve.tensor_tensor(elo[:, :, :], ys[:, :, :], ehi[:, :, :].bitcast(F32), ALU.subtract)\
                    .then_inc(sem("elo_ready"), 1)
                odd_give(g, 0)

            over_groups(dve, group)
            odd_give(G - 1, 1)
            dve.wait_ge(sem("moe_full"), 1)
            for k in range(2):
                acc = xs[:, 4 * k:4 * k + 4, :]
                dve.scalar_tensor_tensor(out=acc, in0=bank(2 + k).rearrange("p (t d) -> p t d", d=D), scalar=tg[:, 2:3],
                                         in1=acc, op0=ALU.mult, op1=ALU.add).then_inc(sem("x2_ready"), 1)
            dve.wait_ge(sem("x2_ready"), 2)

            norm(xs, ya, 0, P, T, (sem("var"), 2), (sem("std"), 2))
            vo.settle()
            dve.engine_nop().then_inc(sem("hc_ready"), 1)
            vo.mark(dve.tensor_scalar(row[:, :], small_at("b_qv_row"), tg[:, 1:2], None, ALU.mult))
            vo.settle()
            vo.mark(dve.tensor_tensor(xs[:, :, :], xs[:, :, :], row[:, :].unsqueeze(1).broadcast_to([P, T, D]), ALU.add))
            dve.wait_ge(sem("sim_full"), 1)
            dve.tensor_reduce(nmx[:, :], bank(2, 2).rearrange("p (t n) -> p t n", n=P)[:, :, 0:M], AX.X, ALU.max,
                              negate=True).then_inc(sem("nmx_ready"), 1)
            dve.wait_ge(sem("nmx_ready"), 1)
            dve.wait_ge(sem("s0_full"), 1)
            vo.mark(dve.scalar_tensor_tensor(out=mi[:, :], in0=bank(4)[:, 0:T], scalar=small_at("b_sim"), in1=nmx[:, :],
                                             op0=ALU.add, op1=ALU.subtract))
            vo.settle()
            dve.tensor_reduce(mbest[:, :], mi[:, :].rearrange("p (b t) -> p b t", b=B), AX.X, ALU.max)\
                .then_inc(sem("mbest_ready"), 1)
            dve.wait_ge(sem("mbestT_full"), 1)
            vo.mark(dve.tensor_reduce(m2[:, :], bank(7)[0:B, 0:P], AX.X, ALU.max, negate=True))
            vo.settle()
            dve.tensor_scalar(dm[:, :], ident[0:B, 0:B], m2[:, 0:1], None, ALU.mult).then_inc(sem("dm_ready"), 1)
            dve.wait_ge(sem("negm_full"), 1)
            dve.tensor_copy(negm[:, :], bank(7)[:, 0:B]).then_inc(sem("negm_ready"), 1)
            dve.wait_ge(sem("aw_ready"), T)
            vo.mark(dve.reciprocal(asum[:, :], asum[:, :]))
            vo.settle()
            dve.tensor_tensor(aw[:, :, :], aw[:, :, :], asum[:, :].unsqueeze(2).broadcast_to([P, T, M]), ALU.mult)\
                .then_inc(sem("a_ready"), 1)
            dve.wait_ge(sem("hcb_full"), 1)
            vo.mark(dve.reciprocal(rtot[:, :], bank(7)[:, 0:B]))
            vo.settle()
            vo.mark(dve.tensor_tensor(hcb[:, :], bank(7)[:, 2:2 + B], rtot[:, :], ALU.mult))
            vo.settle()
            for b in range(B):
                dve.scalar_tensor_tensor(out=wc[:, b, :], in0=wqv[:, 3, :], scalar=hcb[:, b:b + 1], in1=wqv[:, 0, :],
                                         op0=ALU.mult, op1=ALU.add).then_inc(sem("wc_ready"), 1)
            dve.wait_ge(sem("hqh_ready"), 1)
            dve.tensor_tensor(f3[:, :], hcT[:, :], hqh[:, :], ALU.mult).then_inc(sem("f3_ready"), 1)
            vo.settle()
            for k in range(2):
                dve.wait_ge(sem("hcq_full"), k + 1)
                acc = xs[:, 4 * k:4 * k + 4, :]
                dve.scalar_tensor_tensor(out=acc, in0=bank(k).rearrange("p (t d) -> p t d", d=D), scalar=tg[:, 1:2],
                                         in1=acc, op0=ALU.mult, op1=ALU.add).then_inc(sem("x3_ready"), 1)
            dve.wait_ge(sem("x3_ready"), 2)

            norm(xs, ya, 0, P, T, (sem("var"), 3), (sem("std"), 3))
            vo.settle()
            dve.engine_nop().then_inc(sem("z_ready"), 1)
            vo.mark(dve.tensor_scalar(row[:, :], small_at("b2_row"), tg[:, 3:4], None, ALU.mult))
            vo.settle()
            vo.mark(dve.tensor_tensor(xs[:, :, :], xs[:, :, :], row[:, :].unsqueeze(1).broadcast_to([P, T, D]), ALU.add))
            dve.wait_ge(sem("gB_full"), 1)
            dve.scalar_tensor_tensor(out=gB[:, :, :], in0=bank(6)[:, 0:B * E2].rearrange("p (b e) -> p b e", b=B),
                                     scalar=1.0 / N, in1=small_at("gate_b2").unsqueeze(1).broadcast_to([P, B, E2]),
                                     op0=ALU.mult, op1=ALU.add).then_inc(sem("g_ready"), 1)
            dve.scalar_tensor_tensor(out=gT[:, :], in0=bank(7)[0:E2, 0:B], scalar=1.0 / N,
                                     in1=small_at("gate_b2_col", E2).broadcast_to([E2, B]),
                                     op0=ALU.mult, op1=ALU.add).then_inc(sem("g_ready"), 1)
            dve.wait_ge(sem("g_ready"), 2)
            for b in range(B):
                vo.mark(dve.tensor_tensor(tb[:, b, :, :], small_at("Tb1").rearrange("p (c e) -> p c e", e=E2),
                                          gB[:, b, :].unsqueeze(1).broadcast_to([P, FC, E2]), ALU.mult))
            vo.settle()
            vo.mark(dve.reduce_sum(mb1[:, :, :], tb[:, :, :, :], AX.X))
            vo.settle()
            dve.tensor_tensor(mb1[:, :, :], mb1[:, :, :], small_at("b1").unsqueeze(1).broadcast_to([P, B, FC]), ALU.add)\
                .then_inc(sem("mb1_ready"), 1)
            dve.wait_ge(sem("weights_loaded"), 16 * 9)
            dve.wait_ge(sem("tw_loaded"), 32)
            for b in range(B):
                for e in range(E2):
                    if e:
                        dve.wait_ge(sem("mw1_ready"), E2 * b + e)
                    dve.scalar_tensor_tensor(out=mw1[b][:, :], in0=tw1[:, e, :], scalar=gB[:, b, e:e + 1],
                                             in1=mw1[b][:, :] if e else w1[:, :], op0=ALU.mult, op1=ALU.add)\
                        .then_inc(sem("mw1_ready"), 1)
            vo.settle()
            for b in range(B):
                dve.wait_ge(sem("ffn_full"), b + 1)
                lo, hi = TILES * b, TILES * (b + 1)
                dve.scalar_tensor_tensor(out=res[:, lo:hi, :], in0=bank(6 + b).rearrange("p (t d) -> p t d", d=D),
                                         scalar=tg[:, 3:4], in1=xs[:, lo:hi, :], op0=ALU.mult, op1=ALU.add)\
                    .then_inc(sem("out_ready"), 1)

        @block.tensor
        def _(pe):
            pe.wait_ge(sem("consts"), 2)
            for b in range(B):
                pe.wait_ge(sem("lat_normed"), b + 1)
                for t in range(TILES):
                    pe.transpose(bank(b)[:, P * t:P * (t + 1)], yb[:, TILES * b + t, :], ident[:, :])\
                        .then_inc(sem("lat_t"), 1)
            pe.wait_ge(sem("lat_normed"), B + 1)
            for b in range(B):
                pe.transpose(bank(2)[:, P * b:P * b + M], cn[0:M, b, :], ident[0:M, 0:M]).then_inc(sem("lat_t"), 1)
            for b in range(B):
                pe.transpose(bank(3)[:, P * b:P * b + M], cs[0:M, b, :], ident[0:M, 0:M]).then_inc(sem("lat_t"), 1)

            def proj_k(i, c):
                if isinstance(i, int) and 2 * i + c == 0:
                    pe.wait_ge(sem("kv_ready"), 2 * B)
                    pe.wait_ge(sem("ctxT_ready"), B)
                else:
                    pe.wait_ge(sem("max_done"), i * (4 * TILES) + 2 * TILES * c - 1)
                pe.wait_ge(sem("wx_loaded"), (i + (c + 2) // 2) * 16)
                kv = kvT[c % 2]
                pe.matmul(xb(c, 0)[:, 0:N], wx[:, P:2 * P], kv[:, 0:N], start=True, stop=True)
                pe.matmul(xb(c, 0)[:, N:KV], wx[:, P:2 * P], kv[:, N:KV], start=True, stop=True)\
                    .then_inc(sem("x_full"), 1)

            def proj_q(i, c):
                if not (isinstance(i, int) and 2 * i + c == 0):
                    pe.wait_ge(sem("max_done"), i * (4 * TILES) + 2 * TILES * c)
                pe.matmul(xb(c, 1)[:, 0:N], wx[:, 0:P], kvT[c % 2][:, 0:N], start=True, stop=True)\
                    .then_inc(sem("x_full"), 1)

            def proj_v(i, c):
                pe.wait_ge(sem("k_lo"), i * 4 + 2 * c + 2)
                for jt in range(JT):
                    w = JW[jt]
                    ins = pe.matmul(xb(c, 2)[0:w, P * jt:P * (jt + 1)], kvT[c % 2][:, P * jt:P * jt + w],
                                    wx[:, 2 * P:3 * P], start=True, stop=True)
                ins.then_inc(sem("x_full"), 1)

            def scores_for_max(i, c, r):
                b, j, h, t = c % 2, 3 + r, r // TILES, r % TILES
                if r == 0:
                    pe.wait_ge(sem("q_lo"), i * 4 + 2 * c + 2)
                elif r == 1:
                    pe.wait_ge(sem("v_ready"), i * 4 + 2 * c + 2)
                else:
                    pe.wait_ge(sem("max_done"), i * (4 * TILES) + 2 * TILES * c + r - 1)
                if t == 0:
                    pe.wait_ge(sem("q_dup"), i * 4 + 2 * c + h + 1)
                pe.matmul(xb(c, j)[:, 0:N], qq[b][:, h, P * t:P * (t + 1)], kk[b][:, h, 0:N], start=True, stop=True)
                pe.matmul(xb(c, j)[:, N:KVP], qq[b][:, h, P * t:P * (t + 1)], kk[b][:, h, N:KVP],
                          start=True, stop=True).then_inc(sem("x_full"), 1)

            def turn_max(i, c, h):
                pe.wait_ge(sem("max_done"), i * (4 * TILES) + 2 * TILES * c + TILES * (h + 1))
                if not (isinstance(i, int) and 2 * i + c == 0):
                    pe.wait_ge(sem("exp_done"), i * (4 * JT) + 2 * JT * c + h - 1)
                pe.transpose(sbank[h][0:TILES, 0:P], nmax[:, c % 2, h, :], ident[:, :]).then_inc(sem("max_turned"), 1)

            def scores(i, b, jt, h):
                w = JW[jt]
                if jt == 0:
                    pe.wait_ge(sem("k_dup"), i * 4 + 2 * b + h + 1)
                    pe.wait_ge(sem("shifts"), i * 4 + 2 * b + h + 1)
                else:
                    pe.wait_ge(sem("exp_done"), i * (4 * JT) + 2 * JT * b + 2 * jt + h - 1)
                pe.matmul(sbank[h][0:w, :], kk[b][:, h, P * jt:P * jt + w], qq[b][:, h, :], start=True, stop=False)
                pe.matmul(sbank[h][0:w, :], ko[b][0:DH + TILES, h, P * jt:P * jt + w], qlm[b][0:DH + TILES, h, :],
                          start=False, stop=True).then_inc(sem("s_full"), 1)

            def values(i, b, jt):
                w = JW[jt]
                if jt == 0:
                    if not (isinstance(i, int) and i == 0 and b == 0):
                        pe.wait_ge(sem("o_saved"), i * 2 + b)
                    pe.wait_ge(sem("v_ready"), i * 4 + 2 * b + 2)
                pe.wait_ge(sem("exp_done"), i * (4 * JT) + 2 * JT * b + 2 * jt + 2)
                for h in range(2):
                    ins = pe.matmul(obank[DH * h:DH * (h + 1), :], vv[b][0:w, jt, DH * h:DH * (h + 1)],
                                    pt[b][0:w, jt, h, :], start=(jt == 0), stop=(jt == JT - 1))
                ins.then_inc(sem("av_done"), 1)

            def sums(i, c):
                pe.wait_ge(sem("pool_added"), i * (2 * (JT - 1)) + (JT - 1) * (c + 1))
                if not (isinstance(i, int) and 2 * i + c == 0):
                    pe.wait_ge(sem("x_added"), i * 2 + c + 1)
                for h in range(2):
                    ins = pe.matmul(mbank[DH * h:DH * (h + 1), :], ones_f[:, 0:DH], psm[c % 2][:, h, :],
                                    start=True, stop=True)
                ins.then_inc(sem("mb_full"), 1)

            def out_proj(i, c):
                pe.wait_ge(sem("normed"), i * 2 + c + 2)
                pe.wait_ge(sem("wo_loaded"), (i + c // 2 + 1) * 16)
                for t in range(TILES):
                    ins = pe.matmul(mbank[:, P * t:P * (t + 1)], onorm[:, P * t:P * (t + 1)], wo[:, :],
                                    start=True, stop=True)
                ins.then_inc(sem("mb_full"), 1)

            def unit(i, b, tail, tail2, ahead):
                c = b + 1
                scores(i, b, 0, 0)
                if ahead:
                    proj_k(i, c)
                turn_max(i, b, 1)
                if tail:
                    values(i - 1 if b == 0 else i, 1 - b, JT - 1)
                scores(i, b, 0, 1)
                if ahead:
                    proj_q(i, c)
                if tail2:
                    sums(i, b - 2)
                scores(i, b, 1, 0)
                if ahead:
                    proj_v(i, c)
                scores(i, b, 1, 1)
                values(i, b, 0)
                scores(i, b, 2, 0)
                if ahead:
                    scores_for_max(i, c, 0)
                scores(i, b, 2, 1)
                if ahead:
                    scores_for_max(i, c, 1)
                values(i, b, 1)
                scores(i, b, 3, 0)
                if ahead:
                    scores_for_max(i, c, 2)
                scores(i, b, 3, 1)
                if ahead:
                    scores_for_max(i, c, 3)
                values(i, b, 2)
                if ahead:
                    scores_for_max(i, c, 4)
                scores(i, b, 4, 0)
                scores(i, b, 4, 1)
                if ahead:
                    scores_for_max(i, c, 5)
                values(i, b, 3)
                if ahead:
                    turn_max(i, c, 0)
                    scores_for_max(i, c, 6)
                if tail2:
                    out_proj(i, b - 2)
                if ahead:
                    scores_for_max(i, c, 7)

            proj_k(0, 0)
            proj_q(0, 0)
            proj_v(0, 0)
            for r in range(2 * TILES):
                scores_for_max(0, 0, r)
            turn_max(0, 0, 0)

            def pair(i, first, last):
                unit(i, 0, not first, not first, True)
                unit(i, 1, True, not first, not last)

            over_pairs(pe, pair)
            values(HP - 1, 1, JT - 1)
            sums(HP - 1, 0)
            out_proj(HP - 1, 0)
            sums(HP - 1, 1)
            out_proj(HP - 1, 1)

            def turn_tiles(k0, full):
                for t in range(T):
                    ins = pe.transpose(bank(k0 + t // 4)[:, P * (t % 4):P * (t % 4 + 1)], ya[:, t, :], ident[:, :])
                    if t % 4 == 3:
                        ins.then_inc(sem(full), 1)

            pe.wait_ge(sem("y_ready"), 1)
            turn_tiles(0, "yT_full")
            pe.wait_ge(sem("weights_loaded"), 16 * 9)
            for t in range(T):
                if t % 4 == 0:
                    pe.wait_ge(sem("yT_ready"), t // 4 + 1)
                ins = pe.matmul(bank(2)[:, E * t:E * (t + 1)], yT[:, t, :], rw[:, :], start=True, stop=True)
            ins.then_inc(sem("lg_full"), 1)
            for part, full in ((0, "shared_gate_full"), (1, "shared_up_full")):
                for k in range(2):
                    ins = pe.matmul(bank(3 + 2 * part + k)[0:FF, :], wsgu[:, FF * part:FF * (part + 1)],
                                    yT[:, 4 * k:4 * k + 4, :], start=True, stop=True)
                ins.then_inc(sem(full), 1)
            pe.wait_ge(sem("chosen_ready"), 1)
            pe.wait_ge(sem("consts2"), 8)
            ch = chosen[:, :, :].rearrange("p t e -> p (t e)")
            pe.matmul(bank(7), before[:, :], ch, start=True, stop=False)
            for s in range(1, T):
                ins = pe.matmul(bank(7)[:, E * s:], ones_b[:, :], ch[:, 0:E * (T - s)], start=False, stop=(s == T - 1))
            ins.then_inc(sem("queue_full"), 1)
            pe.wait_ge(sem("hs_ready"), 1)
            for k in range(2):
                pe.matmul(bank(k), wsdn[:, :], hs[:, :].rearrange("f (q k n) -> f k q n", k=2, n=P)[:, k, :, :],
                          start=True, stop=False)
            pe.wait_ge(sem("val_ready"), 1)
            for q in range(T // 2):
                ins = pe.transpose(bank(2)[:, P * q:P * (q + 1)], val[:, 2 * q:2 * q + 2, :].rearrange("p t e -> p (t e)"),
                                   ident[:, :])
            ins.then_inc(sem("valT_full"), 1)

            def gather(g, tiles):
                if tiles[0] == 0:
                    pe.wait_ge(sem("take_ready"), g + 1)
                for t in tiles:
                    for part in (yhi, ylo):
                        ins = pe.matmul(bank(4), part[:, t, :], take[:, t, :, :].rearrange("p e s -> p (e s)"),
                                        start=(t == 0 and part is yhi), stop=(t == T - 1 and part is ylo))
                if tiles[-1] == T - 1:
                    ins.then_inc(sem("g_full"), 1)

            def weight_rows(g):
                pe.wait_ge(sem("whg_ready"), g + 1)
                for t in range(T):
                    ins = pe.matmul(bank(7)[0:2 * EG, :], whg[:, t, :], take[:, t, :, :].rearrange("p e s -> p (e s)"),
                                    start=(t == 0), stop=(t == T - 1))
                ins.then_inc(sem("wr_full"), 1)

            def broadcast(g, p):
                if p % 2:
                    pe.wait_ge(sem("gsq_ready"), g * 2 + p // 2 + 1)
                elif not (isinstance(g, int) and g == 0 and p == 0):
                    pe.wait_ge(sem("give_odd_ready"), g * 2 + p // 2)
                for k in range(2):
                    if isinstance(g, int):
                        a = (k * E + EG * g + 2 * p) * 64
                        sel = spread[:, a:a + P]
                    else:
                        sel = spread[:, bass.ds(g * (EG * 64) + (k * E + 2 * p) * 64, P)]
                    ins = pe.matmul(bank(2 + k), sel, valT[:, :], start=True, stop=True)
                ins.then_inc(sem("bc_full"), 1)

            def scatter(g, p, last=False):
                pe.wait_ge(sem("elo_ready"), g + 1)
                pe.wait_ge(sem("give_odd_ready" if p % 2 else "give_even_ready"), g * 2 + p // 2 + 1)
                for part in (ehi, elo):
                    for k in range(2):
                        ins = pe.matmul(bank(k), part[:, p, :], give[p][:, 512 * k:512 * (k + 1)], start=False,
                                        stop=last and part is elo)
                ins.then_inc(sem("scattered"), 1)

            pe.wait_ge(sem("ylo_ready"), 1)
            gather(0, range(T))
            weight_rows(0)
            pe.wait_ge(sem("valT_ready"), 1)

            def group(g, first, last):
                pe.wait_ge(sem("xg_ready"), g + 1)
                pe.wait_ge(sem("wgu_loaded"), (g + 1) * 16)
                if not first:
                    pe.wait_ge(sem("hT_ready"), g)
                    pe.wait_ge(sem("ws_ready"), g)
                for e in range(EG):
                    a = 256 * (e // 2)
                    ins = pe.matmul(bank(5, 2)[64 * (e % 2):64 * (e % 2) + 64, a:a + 2 * FF], xg[:, CAP * e:CAP * (e + 1)],
                                    wgu[:, e, :], start=True, stop=True)
                ins.then_inc(sem("gu_full"), 1)
                if not first:
                    broadcast(g - 1, 3)
                    for p in range(PG):
                        scatter(g - 1, p)
                pe.wait_ge(sem("h_ready"), g + 1)
                for p in range(PG):
                    ins = pe.transpose(bank(5)[0:FF, P * p:P * (p + 1)], hh[:, p, :], ident[:, :])
                ins.then_inc(sem("ht_full"), 1)
                pe.wait_ge(sem("wm_ready"), g + 1)
                for p in range(PG):
                    ins = pe.matmul(bank(6)[:, 2 * p:2 * p + 2], wm[:, P * p:P * (p + 1)], ones_r[:, :],
                                    start=True, stop=True)
                ins.then_inc(sem("ws_full"), 1)
                broadcast(g, 0)
                pe.wait_ge(sem("hT_ready"), g + 1)
                pe.wait_ge(sem("wdn_loaded"), (g + 1) * 16)
                for e in range(EG):
                    a = D * (e // 2)
                    ins = pe.matmul(bank(7)[64 * (e % 2):64 * (e % 2) + 64, a:a + D], hT[:, CAP * e:CAP * (e + 1)],
                                    wdn[:, e, :], start=True, stop=True)
                ins.then_inc(sem("y_full"), 1)
                if not last:
                    gather(g + 1, range(0, T // 2))
                broadcast(g, 1)
                if not last:
                    gather(g + 1, range(T // 2, T))
                broadcast(g, 2)
                if not last:
                    pe.wait_ge(sem("ys_ready"), g + 1)
                    weight_rows(g + 1)

            over_groups(pe, group)
            broadcast(G - 1, 3)
            for p in range(PG):
                scatter(G - 1, p, last=(p == PG - 1))
            for k in range(2):
                pe.wait_ge(sem("outT_ready"), k + 1)
                for q in range(T // 2):
                    t = 2 * q + k
                    ins = pe.transpose(bank(2 + t // 4)[:, P * (t % 4):P * (t % 4 + 1)],
                                       outT[:, 512 * k + P * q:512 * k + P * (q + 1)], ident[:, :])
            ins.then_inc(sem("moe_full"), 1)

            pe.wait_ge(sem("hc_ready"), 1)
            turn_tiles(0, "hcT_full")
            for t in range(T):
                pe.wait_ge(sem("hcp_ready"), t // 4 + 1)
                ins = pe.matmul(bank(2 + t // 4)[:, P * (t % 4):P * (t % 4) + M], hcp[:, P * t:P * (t + 1)],
                                ctxT[:, t // TILES, :], start=True, stop=True)
            ins.then_inc(sem("sim_full"), 1)
            for t in range(T):
                ins = pe.matmul(bank(4)[:, t:t + 1], hcT[:, P * t:P * (t + 1)],
                                small[:, SMALL["w_sim"][0]:SMALL["w_sim"][0] + 1], start=True, stop=True)
            ins.then_inc(sem("s0_full"), 1)
            pe.wait_ge(sem("mbest_ready"), 1)
            pe.transpose(bank(7)[0:B, 0:P], mbest[:, :], ident[:, :]).then_inc(sem("mbestT_full"), 1)
            pe.wait_ge(sem("dm_ready"), 1)
            pe.matmul(bank(7)[:, 0:B], ones_f[0:B, :], dm[:, :], start=True, stop=True).then_inc(sem("negm_full"), 1)
            pe.wait_ge(sem("a_ready"), 1)
            for t in range(T):
                ins = pe.transpose(bank(5 + t // 4)[0:M, P * (t % 4):P * (t % 4 + 1)], aw[:, t, :], ident[:, :])
            ins.then_inc(sem("aT_full"), 1)
            pe.wait_ge(sem("e8_ready"), B)
            pe.matmul(bank(7)[:, 0:B], ones_f[:, :], es[:, :], start=True, stop=True)
            for b in range(B):
                for t in range(TILES):
                    k = TILES * b + t
                    ins = pe.matmul(bank(7)[:, 2 + b:3 + b], ya[:, k, :], e8[:, k:k + 1], start=(t == 0),
                                    stop=(t == TILES - 1))
            ins.then_inc(sem("hcb_full"), 1)
            pe.wait_ge(sem("aT_ready"), 1)
            for b in range(B):
                ins = pe.matmul(bank(2 + b), cs[0:M, b, :], aT[:, N * b:N * (b + 1)], start=True, stop=True)
            ins.then_inc(sem("hqh_full"), 1)
            pe.wait_ge(sem("wc_ready"), 2)
            pe.wait_ge(sem("f3_ready"), 1)
            for t in range(T):
                dst, tok = bank(t // 4)[:, P * (t % 4):P * (t % 4 + 1)], slice(P * t, P * (t + 1))
                pe.matmul(dst, hcT[:, tok], wc[:, t // TILES, :], start=True, stop=False)
                pe.matmul(dst, hqh[:, tok], wqv[:, 1, :], start=False, stop=False)
                ins = pe.matmul(dst, f3[:, tok], wqv[:, 2, :], start=False, stop=True)
                if t % 4 == 3:
                    ins.then_inc(sem("hcq_full"), 1)

            pe.wait_ge(sem("z_ready"), 1)
            turn_tiles(2, "zT_full")
            for b in range(B):
                pe.wait_ge(sem("zT_ready"), b + 1)
                pe.matmul(bank(4 + b), gw1[:, :], hcT[:, N * b:N * (b + 1)], start=True, stop=True)\
                    .then_inc(sem("gate_full"), 1)
            pe.wait_ge(sem("hsum_ready"), B)
            for b in range(B):
                ins = pe.matmul(bank(6)[:, E2 * b:E2 * (b + 1)], hsum[:, b:b + 1].broadcast_to([P, P]), gw2[:, :],
                                start=True, stop=True)
            pe.matmul(bank(7)[0:E2, 0:B], gw2[:, :], hsum[:, :], start=True, stop=True).then_inc(sem("gB_full"), 1)
            pe.wait_ge(sem("tw_loaded"), 32)
            for b in range(B):
                pe.matmul(bank(b), ident[:, :], w2[:, :, :].rearrange("p c d -> p (c d)"), start=True, stop=False)
                for e in range(E2):
                    pe.wait_ge(sem("diag_ready"), E2 * b + e + 1)
                    ins = pe.matmul(bank(b), diag[:, b, e, :], tw2[:, e, :, :].rearrange("p c d -> p (c d)"),
                                    start=False, stop=(e == E2 - 1))
                ins.then_inc(sem("mw2_full"), 1)
            for n in range(B * FC):
                b, c = n // FC, n % FC
                if c == 0:
                    pe.wait_ge(sem("mw1_ready"), E2 * (b + 1))
                if n >= 4:
                    pe.wait_ge(sem("u_ready"), n - 3)
                pe.matmul(bank(2 + n % 4), mw1[b][:, P * c:P * (c + 1)], hcT[:, N * b:N * (b + 1)], start=True, stop=True)\
                    .then_inc(sem("u_full"), 1)
            for b in range(B):
                pe.wait_ge(sem("u_ready"), FC * (b + 1))
                pe.wait_ge(sem("mw2_ready"), b + 1)
                if b == 0:
                    pe.wait_ge(sem("g_ready"), 2)
                for t in range(TILES):
                    dst = bank(6 + b)[:, D * t:D * (t + 1)]
                    for c in range(FC):
                        pe.matmul(dst, uT[b][:, c, P * t:P * (t + 1)], mw2[b][:, c, :], start=(c == 0), stop=False)
                    ins = pe.matmul(dst, gT[:, b:b + 1].broadcast_to([E2, P]), tb2[:, :], start=False, stop=True)
                ins.then_inc(sem("ffn_full"), 1)


_IN_NAMES = ["x", "ctx", "small", "wqkv", "wout", "rw", "wgu", "wdn", "wsgu", "wsdn", "wqv", "gw1", "gw2", "w1", "tw1",
             "w2", "tw2", "tb2"]


def lay_out(a):
    import numpy as np

    small = np.zeros((P, SMALL_WIDTH), np.float32)

    def put(name, value):
        start, end = SMALL[name]
        small[:, start:end] = value

    for name, key in (("ln_l_g", "L0_xattn_ln_l_g"), ("ln_l_b", "L0_xattn_ln_l_b"), ("ln_m_g", "L0_xattn_ln_m_g"),
                      ("ln_m_b", "L0_xattn_ln_m_b"), ("gate_b1", "L1_ffn_gate_b1")):
        put(name, a[key][:, None])
    for name, key in (("g_xattn", "g_xattn"), ("g_ffn", "g_ffn"), ("b_sim", "L1_xattn_b_sim"),
                      ("gate_b2", "L1_ffn_gate_b2"), ("b_qv_row", "L1_xattn_b_qv"), ("b2_row", "L1_ffn_b2")):
        put(name, a[key][None])
    put("w_sim", a["L1_xattn_w_sim"].reshape(3, P).T)
    small[0:8, SMALL["gate_b2_col"][0]] = a["L1_ffn_gate_b2"]
    put("b1", a["L1_ffn_b1"].reshape(4, P).T)
    put("Tb1", a["L1_ffn_Tb1"].reshape(8, 4, P).transpose(2, 1, 0).reshape(P, 32))
    wq = a["L0_xattn_Wq"].reshape(P, 8, P)
    wkv = a["L0_xattn_Wkv"].reshape(P, 2, 8, P)
    gate_up = np.concatenate([a["L0_ffn_w_gate"], a["L0_ffn_w_up"]], axis=2)
    laid = {
        "x": a["x"], "ctx": a["ctx_1024"], "small": small,
        "wqkv": np.concatenate([w.transpose(1, 0, 2) for w in (wq, wkv[:, 0], wkv[:, 1])], axis=2),
        "wout": a["L0_xattn_Wout"].reshape(8, P, P),
        "rw": a["L0_ffn_router_w"].T,
        "wgu": gate_up.reshape(8, 8, P, 192).transpose(0, 2, 1, 3),
        "wdn": a["L0_ffn_w_down"].reshape(8, 8, 96, P).transpose(0, 2, 1, 3),
        "wsgu": a["L0_ffn_ws_gate_up"], "wsdn": a["L0_ffn_ws_down"],
        "wqv": a["L1_xattn_W_qv"].reshape(4, P, P).transpose(1, 0, 2),
        "gw1": a["L1_ffn_gate_w1"].T, "gw2": a["L1_ffn_gate_w2"].T,
        "w1": a["L1_ffn_W1"].T, "tw1": a["L1_ffn_TW1"].transpose(2, 0, 1),
        "w2": a["L1_ffn_W2"].T.reshape(4, P, P).transpose(1, 0, 2),
        "tw2": a["L1_ffn_TW2"].transpose(0, 2, 1).reshape(8, 4, P, P).transpose(2, 0, 1, 3),
        "tb2": a["L1_ffn_Tb2"],
    }
    return {k: np.ascontiguousarray(v) for k, v in laid.items()}


def kernel(**inputs):
    import numpy as _np
    import concourse.bacc as _bacc
    from concourse import mybir as _mybir
    from concourse.bass_utils import run_bass_kernel_spmd as _run

    nc = _bacc.Bacc("TRN2", target_bir_lowering=False, num_devices=1)
    laid = lay_out({k: _np.asarray(v) for k, v in inputs.items()})
    arrays, args = {}, []
    for name in _IN_NAMES:
        arrays[f"in_{name}_dram"] = laid[name]
        args.append(nc.dram_tensor(f"in_{name}_dram", laid[name].shape, _mybir.dt.from_np(laid[name].dtype),
                                   kind="ExternalInput").ap())
    out = nc.dram_tensor("out_dram", laid["x"].shape, _mybir.dt.float32, kind="ExternalOutput").ap()
    flamingo_block(nc, *args, out)
    r = _run(nc, [arrays], core_ids=[0])
    return r.results[0]["out_dram"]
```

```python
from contextlib import ExitStack

import concourse.bass as bass
from concourse import mybir

ALU = mybir.AluOpType
ACT = mybir.ActivationFunctionType
AX = mybir.AxisListType
F32 = mybir.dt.float32
F32R = mybir.dt.float32r
BF16 = mybir.dt.bfloat16

P = 128
EPS = 1e-5

SMALL = {}


def _place(names):
    at = 0
    for name, width in names:
        SMALL[name] = (at, at + width)
        at += width
    return at


SMALL_WIDTH = _place([
    ("ln_l_g", 1), ("ln_l_b", 1), ("ln_m_g", 1), ("ln_m_b", 1),
    ("g_xattn", 2), ("g_ffn", 2), ("w_sim", 3), ("b_sim", 1),
    ("gate_b1", 1), ("gate_b2", 8), ("gate_b2_col", 1), ("b1", 4), ("Tb1", 32),
    ("b_qv_row", 128), ("b2_row", 128),
])


class Order:

    def __init__(self, eng, sem):
        self.eng, self.sem, self.n = eng, sem, 0

    def mark(self, ins):
        ins.then_inc(self.sem, 1)
        self.n += 1

    def settle(self):
        self.eng.wait_ge(self.sem, self.n)


def flamingo_block(nc, x_in, ctx_in, small_in, wqkv_in, wout_in, rw_in, wgu_in, wdn_in, wsgu_in, wsdn_in,
                   wqv_in, gw1_in, gw2_in, w1_in, tw1_in, w2_in, tw2_in, tb2_in, out):
    B, N, D = x_in.shape
    M = ctx_in.shape[1]
    TILES = N // P
    T = B * TILES
    HP = wqkv_in.shape[0]
    DH = 64
    SCALE = float(DH) ** -0.5
    KV = N + M
    KVP = KV + KV % 2
    JT = N // P + 1
    W_LAST = KV - N
    U = B * HP
    JW = [P] * TILES + [W_LAST]
    E, CAP, FF = rw_in.shape[1], 64, wdn_in.shape[1]
    G = wgu_in.shape[0]
    EG = E // G
    PG = EG // 2
    TOPK = 8
    E2, F2 = tb2_in.shape[0], w1_in.shape[1]
    FC = F2 // P
    RECIPS = 2
    E2P = 5
    XSTEPS = 11

    with ExitStack() as stack:
        def sb(name, shape, dt=F32):
            return stack.enter_context(nc.sbuf_tensor(name, shape, dt))

        sems = {}

        def sem(name):
            if name not in sems:
                sems[name] = stack.enter_context(nc.semaphore(name))
            return sems[name]

        psum = stack.enter_context(nc.psum_tensor("psum", [P, 8 * 512], F32))

        def bank(k, n=1):
            return psum[:, 512 * k:512 * (k + n)]

        xs = sb("xs", [P, T, D])
        cs = sb("cs", [P, B, D])
        small = sb("small", [P, SMALL_WIDTH])
        ident = sb("ident", [P, P])
        ones_f = sb("ones_f", [P, P])
        eps_t = sb("eps_t", [P, 1])
        eps2_t = sb("eps2_t", [P, 1])
        tg = sb("tg", [P, 4])
        sqrt_warm = sb("sqrt_warm", [P, 1])
        stats = sb("stats", [P, T + B, 6])
        mv = sb("mv", [P, T + B, 2])
        std = sb("std", [P, T + B])
        rstd = sb("rstd", [P, T + B])
        ya = sb("ya", [P, T, D])
        cn = sb("cn", [P, B, D])
        kvT = [sb(f"kvT{b}", [P, KV]) for b in range(B)]
        ctxT = sb("ctxT", [P, B, M])

        ones_b = sb("ones_b", [P, P], BF16)
        before = sb("before", [P, P], BF16)
        spread = sb("spread", [P, P * 64], BF16)
        slots = sb("slots", [P, CAP])
        slot_of = sb("slot_of", [P, 1])
        minus_slot = sb("minus_slot", [P, 1])
        own_e = sb("own_e", [2 * EG, EG, CAP])
        ones_r = sb("ones_r", [P, 2], F32R)
        wm = sb("wm", [P, EG * CAP], F32R)
        rw = sb("rw", [P, E])
        wgu = sb("wgu", [P, EG, 2 * FF])
        wdn = sb("wdn", [FF, EG, D])
        wsgu = sb("wsgu", [P, 2 * FF])
        wsdn = sb("wsdn", [FF, D])
        wqv = sb("wqv", [P, 4, D])
        gw1 = sb("gw1", [P, D])
        gw2 = sb("gw2", [P, E2])
        w1 = sb("w1", [P, F2])
        w2 = sb("w2", [P, F2 // P, D])
        tb2 = sb("tb2", [E2, D])
        ctxw = sb("ctxw", [P, B, M + 1])
        ctxv = sb("ctxv", [P, B, M])
        simv = sb("simv", [P, B, M])

        scope = ExitStack()

        def sb(name, shape, dt=F32):
            return scope.enter_context(nc.sbuf_tensor(name, shape, dt))

        wx = sb("wx", [P, 3 * P])
        wqk_hi = sb("wqk_hi", [P, 2 * P], F32R)
        wqk_lo = sb("wqk_lo", [P, 2 * P], F32R)
        kv_hi = [sb(f"kv_hi{b}", [P, N], F32R) for b in range(B)]
        kv_lo = [sb(f"kv_lo{b}", [P, N], F32R) for b in range(B)]
        wo = sb("wo", [P, D])
        qq = [sb(f"qq{b}", [P, 2, N], F32R) for b in range(B)]
        qlm = [sb(f"qlm{b}", [P, 2, N], F32R) for b in range(B)]
        kk = [sb(f"kk{b}", [P, 2, KVP], F32R) for b in range(B)]
        ko = [sb(f"ko{b}", [P, 2, KVP], F32R) for b in range(B)]
        vv = [sb(f"vv{b}", [P, JT, P]) for b in range(B)]
        pt = [sb(f"pt{b}", [P, JT, 2, N]) for b in range(B)]
        psm = [sb(f"psm{b}", [P, 2, N]) for b in range(B)]
        nmax = sb("nmax", [P, B, 2, TILES])
        mask4 = sb("mask4", [TILES, TILES, P])
        rsum = sb("rsum", [P, N])
        osb = [sb(f"osb{b}", [P, N]) for b in range(B)]
        onorm = sb("onorm", [P, N])

        scope.close()
        scope2 = stack.enter_context(ExitStack())

        def sb(name, shape, dt=F32):
            return scope2.enter_context(nc.sbuf_tensor(name, shape, dt))

        tw1 = sb("tw1", [P, E2, F2])
        tw2 = sb("tw2", [P, E2, FC, D])
        scope3 = ExitStack()

        def sb(name, shape, dt=F32):
            return scope3.enter_context(nc.sbuf_tensor(name, shape, dt))

        yhi = sb("yhi", [P, T, D], F32R)
        ylo = sb("ylo", [P, T, D], F32R)
        yT = sb("yT", [P, T, P])
        lg = sb("lg", [P, T, E])
        top = sb("top", [P, T, TOPK])
        rest = sb("rest", [P, T, E])
        chosen = sb("chosen", [P, T, E], BF16)
        wgt = sb("wgt", [P, T, E])
        den = sb("den", [P, T])
        rden = sb("rden", [P, T])
        whl = sb("whl", [P, T, E, 2], F32R)
        val = sb("val", [P, T, E])
        valT = sb("valT", [P, T // 2 * P], BF16)
        sth = sb("sth", [FF, T * P])
        hs = sb("hs", [FF, T * P])
        take = sb("take", [P, T, EG, CAP], F32R)
        give = [sb(f"give{p}", [P, T * P], F32R) for p in range(PG)]
        xg = sb("xg", [P, EG * CAP])
        th = sb("th", [P, PG, FF])
        hh = sb("hh", [P, PG, FF])
        hT = sb("hT", [FF, EG * CAP])
        whg = sb("whg", [P, T, 2 * EG], F32R)
        ws = sb("ws", [P, PG])
        gsq = sb("gsq", [P, T * P])
        ys = sb("ys", [P, PG, D])
        ehi = sb("ehi", [P, PG, D], F32R)
        elo = sb("elo", [P, PG, D], F32R)
        outT = sb("outT", [P, T * P])
        scope3.close()

        def sb(name, shape, dt=F32):
            return scope2.enter_context(nc.sbuf_tensor(name, shape, dt))

        hcT = sb("hcT", [P, T * P])
        relu_out = sb("relu_out", [P, B, N])
        simc = sb("simc", [P, T, M])
        nmx = sb("nmx", [P, T])
        aw = sb("aw", [P, T, M])
        asum = sb("asum", [P, T])
        aT = sb("aT", [M, T * P])
        hqh = sb("hqh", [P, T * P])
        f3 = sb("f3", [P, T * P])
        mi = sb("mi", [P, T])
        mbest = sb("mbest", [P, B])
        m2 = sb("m2", [B, 1])
        dm = sb("dm", [B, B])
        negm = sb("negm", [P, B])
        e8 = sb("e8", [P, T])
        es = sb("es", [P, B])
        rtot = sb("rtot", [P, B])
        hcb = sb("hcb", [P, B])
        wc = sb("wc", [P, B, D])
        row = sb("row", [P, D])
        hsum = sb("hsum", [P, B])
        gB = sb("gB", [P, B, E2])
        gT = sb("gT", [E2, B])
        tb = sb("tb", [P, B, FC, E2])
        mb1 = sb("mb1", [P, B, FC])
        mw1 = [sb(f"mw1{b}", [P, F2]) for b in range(B)]
        mw2 = [sb(f"mw2{b}", [P, FC, D]) for b in range(B)]
        diag = sb("diag", [P, B, E2P, P])
        uT = [sb(f"uT{b}", [P, FC, N]) for b in range(B)]
        res = sb("res", [P, T, D])

        def small_at(name, n=P):
            a, b = SMALL[name]
            return small[0:n, a:b]

        xbuf = [bank(0, 2), bank(2, 2)]
        sbank = [bank(4), bank(5)]
        obank = bank(6)
        mbank = bank(7)

        def bcast(g, p):
            return bank(4, 2) if isinstance(g, int) and g == G - 1 and p % 2 else bank(2, 2)

        def quarter(k):
            return bank((6, 0, 1, 7)[k])

        def xb(u, j):
            return xbuf[(u + j) % 2]

        def mb(i, c):
            last = isinstance(i, int) and 2 * i + c >= U - 2
            return bank(2 * (2 * i + c - (U - 2))) if last else mbank

        block = stack.enter_context(nc.Block())

        def over_pairs(eng, body):
            body(0, True, False)
            with eng.Fori(1, HP - 1) as i:
                body(i, False, False)
            body(HP - 1, False, True)

        def over_groups(eng, body):
            body(0, True, False)
            with eng.Fori(1, G - 1) as g:
                body(g, False, False)
            body(G - 1, False, True)

        @block.sync
        def _(sp):
            def load_x(b):
                sp.dma_start(xs[:, TILES * b:TILES * (b + 1), :],
                             x_in[b].rearrange("(t p) d -> p t d", p=P)).then_inc(sem(f"x_loaded{b}"), 16)

            load_x(0)
            sp.dma_start(cs[0:M, :, :], ctx_in.rearrange("b m d -> m b d")).then_inc(sem("ctx_loaded"), 16)
            sp.dma_start(small[:, :], small_in).then_inc(sem("small_loaded"), 16)
            load_x(1)
            sp.dma_start(wx[:, :], wqkv_in[0]).then_inc(sem("wx_loaded"), 16)
            sp.dma_start(wo[:, :], wout_in[0]).then_inc(sem("wo_loaded"), 16)

            def pair(i, first, last):
                if not last:
                    sp.wait_ge(sem("x_full"), i * (2 * XSTEPS) + XSTEPS + 3)
                    src = wqkv_in[i + 1] if isinstance(i, int) else wqkv_in[bass.ds(i + 1, 1)].rearrange("a p n -> p (a n)")
                    sp.dma_start(wx[:, :], src).then_inc(sem("wx_loaded"), 16)
                if not first:
                    sp.wait_ge(sem("mb_full"), i * 4)
                    src = wout_in[i] if isinstance(i, int) else wout_in[bass.ds(i, 1)].rearrange("a p n -> p (a n)")
                    sp.dma_start(wo[:, :], src).then_inc(sem("wo_loaded"), 16)

            later = ((rw, rw_in), (wsgu, wsgu_in), (wsdn, wsdn_in), (wgu, wgu_in[0]), (wdn, wdn_in[0]), (wqv, wqv_in),
                     (gw1, gw1_in), (gw2, gw2_in), (w1, w1_in), (w2, w2_in), (tb2, tb2_in))
            for dst, src in later:
                name = {"wgu": "wgu_loaded", "wdn": "wdn_loaded"}.get(dst.name, "weights_loaded")
                sp.dma_start(dst[(slice(None),) * len(dst.shape)], src).then_inc(sem(name), 16)

            over_pairs(sp, pair)
            sp.wait_ge(sem("x_added"), U + 1)
            sp.dma_start(tw1[:, :, :], tw1_in).then_inc(sem("tw_loaded"), 16)
            sp.dma_start(tw2[:, :, :, :], tw2_in).then_inc(sem("tw_loaded"), 16)

            def group(g, first, last):
                if last:
                    return
                sp.wait_ge(sem("gu_full"), g + 1)
                src = wgu_in[g + 1] if isinstance(g, int) else wgu_in[bass.ds(g + 1, 1)].rearrange("a p e n -> p (a e) n")
                sp.dma_start(wgu[:, :, :], src).then_inc(sem("wgu_loaded"), 16)
                sp.wait_ge(sem("y_full"), g + 1)
                src = wdn_in[g + 1] if isinstance(g, int) else wdn_in[bass.ds(g + 1, 1)].rearrange("a p e n -> p (a e) n")
                sp.dma_start(wdn[:, :, :], src).then_inc(sem("wdn_loaded"), 16)

            over_groups(sp, group)
            for k in range(T // 2):
                b, t = 2 * k // TILES, 2 * k % TILES
                sp.wait_ge(sem("out_ready"), k + 1)
                sp.dma_start(out[b, P * t:P * (t + 2)].rearrange("(t p) d -> p t d", p=P), res[:, 2 * k:2 * k + 2, :])\
                    .then_inc(sem("out_stored"), 16)
            sp.wait_ge(sem("out_stored"), 16 * (T // 2))

        @block.gpsimd
        def _(pool):
            po = Order(pool, sem("pool_self"))
            po.mark(pool.memset(ident[:, :], 0.0))
            po.mark(pool.memset(mask4[:, :, :], 0.0))
            po.mark(pool.memset(ones_f[:, :], 1.0))
            po.mark(pool.memset(eps_t[:, :], EPS))
            po.mark(pool.memset(eps2_t[:, :], EPS * EPS))
            po.settle()
            pool.affine_select(out=ident[:, :], in_=ident[:, :], compare_op=ALU.not_equal, fill=1.0,
                               base=0, pattern=[[-1, P]], channel_multiplier=1).then_inc(sem("consts"), 1)
            pool.affine_select(out=mask4[:, :, :], in_=mask4[:, :, :], compare_op=ALU.not_equal, fill=1.0,
                               base=0, pattern=[[-1, TILES], [0, P]], channel_multiplier=1).then_inc(sem("consts"), 1)
            for b in range(B):
                for t in (qlm[b], kk[b]):
                    pool.memset(t[:, :, :].bitcast(F32), 0.0).then_inc(sem("pads"), 1)
                pool.memset(ko[b][:, :, :].bitcast(F32), 1.0).then_inc(sem("pads"), 1)

            po.mark(pool.memset(spread[:, :], 0.0))
            po.mark(pool.memset(before[:, :], 1.0))
            po.mark(pool.memset(ones_b[:, :], 1.0))
            po.mark(pool.memset(own_e[:, :, :], 0.0))
            po.mark(pool.memset(ones_r[:, :].bitcast(F32), 1.0))
            po.mark(pool.memset(wm[:, :].bitcast(F32), 0.0))
            po.settle()
            pool.affine_select(out=spread[:, :], in_=spread[:, :], compare_op=ALU.not_equal, fill=1.0,
                               base=0, pattern=[[-1, P], [0, 64]], channel_multiplier=1).then_inc(sem("consts2"), 1)
            pool.affine_select(out=before[:, :], in_=before[:, :], compare_op=ALU.is_gt, fill=0.0,
                               base=0, pattern=[[1, P]], channel_multiplier=-1).then_inc(sem("consts2"), 1)
            for k in range(2):
                po.mark(pool.affine_select(out=own_e[:, :, :], in_=own_e[:, :, :], compare_op=ALU.not_equal, fill=1.0,
                                           base=-k, pattern=[[-2, EG], [0, CAP]], channel_multiplier=1))
                po.settle()
            pool.engine_nop().then_inc(sem("consts2"), 1)
            pool.iota(slots[:, :], pattern=[[1, CAP]], base=1, channel_multiplier=0,
                      allow_small_or_imprecise_dtypes=True).then_inc(sem("consts2"), 1)
            n = 4
            for sign, dst in ((1, slot_of), (-1, minus_slot)):
                for h in range(2):
                    pool.wait_ge(sem("consts2"), n)
                    pool.iota(dst[64 * h:64 * (h + 1), :], pattern=[[0, 1]], base=sign, channel_multiplier=sign,
                              allow_small_or_imprecise_dtypes=True).then_inc(sem("consts2"), 1)
                    n += 1

            pool.wait_ge(sem("consts2"), 8)

            def split_weights(i):
                pool.wait_ge(sem("wx_loaded"), (i + 2) * 16)
                pool.tensor_tensor(wqk_hi[:, :], wx[:, 0:2 * P], ones_f[:, 0:1].broadcast_to([P, 2 * P]), ALU.mult)\
                    .then_inc(sem("wqk_hi_ready"), 1)
                pool.wait_ge(sem("wqk_hi_ready"), i + 1)
                pool.tensor_tensor(wqk_lo[:, :], wx[:, 0:2 * P], wqk_hi[:, :].bitcast(F32), ALU.subtract)\
                    .then_inc(sem("wqk_lo_ready"), 1)

            def unit(i, b, split):
                pool.wait_ge(sem("exp_done"), i * (4 * JT) + 2 * JT * b + 4)
                if not (isinstance(i, int) and i == 0):
                    pool.wait_ge(sem("mb_full"), i * 4 + 2 * b - 3)
                pool.tensor_tensor(psm[b][:, :, :], pt[b][:, 0, :, :], pt[b][:, 1, :, :], ALU.add)\
                    .then_inc(sem("pool_added"), 1)
                for jt in range(2, JT):
                    w = JW[jt]
                    if split and jt == 3:
                        split_weights(i)
                    pool.wait_ge(sem("exp_done"), i * (4 * JT) + 2 * JT * b + 2 * jt + 2)
                    pool.wait_ge(sem("pool_added"), i * (2 * (JT - 1)) + (JT - 1) * b + jt - 1)
                    pool.tensor_tensor(psm[b][0:w, :, :], psm[b][0:w, :, :], pt[b][0:w, jt, :, :], ALU.add)\
                        .then_inc(sem("pool_added"), 1)

            def pair(i, first, last):
                unit(i, 0, not last)
                if not last:
                    unit(i, 1, False)

            over_pairs(pool, pair)

            def group_weights(g):
                c = 2 * EG * g
                src = whl[:, :, :, :].rearrange("p t e k -> p t (e k)")
                src = src[:, :, c:c + 2 * EG] if isinstance(g, int) else src[:, :, bass.ds(c, 2 * EG)]
                pool.tensor_copy(whg[:, :, :], src).then_inc(sem("whg_ready"), 1)

            pool.wait_ge(sem("whl_ready"), 2)
            group_weights(0)

            def group(g, first, last):
                if not last:
                    pool.wait_ge(sem("wr_full"), g + 1)
                    group_weights(g + 1)

            over_groups(pool, group)

        @block.scalar
        def _(act):
            act.wait_ge(sem("consts"), 2)
            act.activation(sqrt_warm[:, :], eps_t[:, :], ACT.Sqrt)

            def root_lat(b, n):
                act.wait_ge(sem("var0"), n)
                a, e = TILES * b, TILES * (b + 1)
                act.activation(std[:, a:e], mv[:, a:e, 1], ACT.Sqrt, scale=1.0 + EPS, bias=eps2_t[:, :])\
                    .then_inc(sem("std0"), 1)

            root_lat(0, 1)
            act.wait_ge(sem("var0"), 2)
            act.activation(std[0:M, T:T + B], mv[0:M, T:T + B, 1], ACT.Sqrt, bias=eps_t[0:M, :]).then_inc(sem("std0"), 1)
            act.wait_ge(sem("small_loaded"), 16)

            def save_lat(b, n):
                act.wait_ge(sem("lat_t"), n)
                act.activation(kvT[b][:, 0:N], bank(6 - b), ACT.Identity, scale=small_at("ln_l_g"),
                               bias=small_at("ln_l_b")).then_inc(sem("kv_ready"), 1)

            save_lat(0, TILES)
            for b in range(B):
                act.wait_ge(sem("lat_t"), TILES + B)
                act.activation(kvT[b][:, N:KV], bank(7)[:, P * b:P * b + M], ACT.Identity, scale=small_at("ln_m_g"),
                               bias=small_at("ln_m_b")).then_inc(sem("kv_ready"), 1)
            root_lat(1, 3)
            act.wait_ge(sem("pads"), 3 * B)

            def exp(i, b, jt, h):
                w = JW[jt]
                act.wait_ge(sem("s_full"), i * (4 * JT) + 2 * JT * b + 2 * jt + h + 1)
                act.activation(pt[b][0:w, jt, h, :], sbank[h][0:w, :], ACT.Exp, scale=SCALE)\
                    .then_inc(sem("exp_done"), 1)

            def round_k(i, c, h):
                b = c % 2
                if h == 0:
                    act.wait_ge(sem("x_full"), i * (2 * XSTEPS) + XSTEPS * c + 1)
                act.activation(kk[b][0:DH, h, 0:KV], xb(c, 0)[DH * h:DH * (h + 1), 0:KV], ACT.Copy)\
                    .then_inc(sem("k_hi"), 1)

            def round_q(i, c, h):
                b = c % 2
                if h == 0:
                    act.wait_ge(sem("x_full"), i * (2 * XSTEPS) + XSTEPS * c + 2)
                act.activation(qq[b][0:DH, h, :], xb(c, 1)[DH * h:DH * (h + 1), 0:N], ACT.Copy)\
                    .then_inc(sem("q_hi"), 1)

            def save_v(i, c):
                b = c % 2
                act.wait_ge(sem("x_full"), i * (2 * XSTEPS) + XSTEPS * c + 3)
                act.activation(vv[b][:, 0:TILES, :], xb(c, 2)[:, 0:N], ACT.Copy).then_inc(sem("v_ready"), 1)
                act.activation(vv[b][0:W_LAST, TILES, :], xb(c, 2)[0:W_LAST, N:N + P], ACT.Copy)\
                    .then_inc(sem("v_ready"), 1)

            def copy_k(i, c, h):
                b = c % 2
                act.wait_ge(sem("k_hi"), i * 4 + 2 * c + h + 1)
                act.activation(ko[b][0:DH, h, 0:KV], kk[b][0:DH, h, 0:KV].bitcast(F32), ACT.Copy)\
                    .then_inc(sem("k_dup"), 1)

            def copy_q(i, c, h):
                b = c % 2
                act.wait_ge(sem("q_hi"), i * 4 + 2 * c + h + 1)
                act.activation(qq[b][DH:P, h, :], qq[b][0:DH, h, :].bitcast(F32), ACT.Copy)\
                    .then_inc(sem("q_dup"), 1)

            def save_o(i, c):
                act.wait_ge(sem("av_done"), i * (2 * JT) + JT * c)
                if not (isinstance(i, int) and 2 * i + c - 1 < 2):
                    act.wait_ge(sem("normed"), i * 2 + c - 1)
                act.activation(osb[(c - 1) % 2][:, :], obank, ACT.Copy).then_inc(sem("o_saved"), 1)

            round_k(0, 0, 0)
            round_k(0, 0, 1)
            round_q(0, 0, 0)
            round_q(0, 0, 1)
            copy_q(0, 0, 0)
            copy_q(0, 0, 1)
            save_lat(1, 2 * TILES + 2 * B)
            save_v(0, 0)
            copy_k(0, 0, 0)
            copy_k(0, 0, 1)
            act.activation(tg[:, :], small[:, SMALL["g_xattn"][0]:SMALL["g_ffn"][1]], ACT.Tanh).then_inc(sem("gates"), 1)

            def unit(i, b, tail, ahead):
                c = b + 1
                if not (isinstance(i, int) and i == 0):
                    act.wait_ge(sem("pool_added"), i * (2 * (JT - 1)) + (JT - 1) * (b - 1))
                exp(i, b, 0, 0)
                if ahead:
                    round_k(i, c, 0)
                    round_k(i, c, 1)
                if tail:
                    save_o(i, b)
                if ahead:
                    round_q(i, c, 0)
                    round_q(i, c, 1)
                exp(i, b, 0, 1)
                exp(i, b, 1, 0)
                if ahead:
                    copy_q(i, c, 0)
                    copy_q(i, c, 1)
                    save_v(i, c)
                exp(i, b, 1, 1)
                exp(i, b, 2, 0)
                if ahead:
                    copy_k(i, c, 0)
                    copy_k(i, c, 1)
                exp(i, b, 2, 1)
                for jt in range(3, JT):
                    exp(i, b, jt, 0)
                    exp(i, b, jt, 1)

            def pair(i, first, last):
                unit(i, 0, not first, True)
                unit(i, 1, True, not last)

            over_pairs(act, pair)
            save_o(HP, 0)

            def root(n):
                for k in range(2):
                    act.wait_ge(sem("var"), 2 * n - 1 + k)
                    act.activation(std[:, TILES * k:TILES * (k + 1)], mv[:, TILES * k:TILES * (k + 1), 1], ACT.Sqrt,
                                   bias=eps_t[:, :]).then_inc(sem("std"), 1)

            root(1)
            for k in range(2):
                act.wait_ge(sem("yT_full"), k + 1)
                act.activation(yT[:, 4 * k:4 * k + 4, :], bank(k).rearrange("p (t n) -> p t n", n=P), ACT.Copy)\
                    .then_inc(sem("yT_ready"), 1)
            for k in range(2):
                act.wait_ge(sem("lg_full"), k + 1)
                act.activation(lg[:, TILES * k:TILES * (k + 1), :],
                               bank(2 + 5 * k)[:, 0:TILES * E].rearrange("p (t e) -> p t e", e=E), ACT.Copy)\
                    .then_inc(sem("lg_ready"), 1)
            act.wait_ge(sem("logits_shifted"), 1)
            act.activation(wgt[:, :, :], wgt[:, :, :], ACT.Exp).then_inc(sem("logits_exp"), 1)
            act.wait_ge(sem("shared_gate_full"), 1)
            act.activation(sth[:, :], bank(0, 2)[0:FF, :], ACT.Tanh, scale=0.5).then_inc(sem("sth_ready"), 1)
            act.wait_ge(sem("valT_full"), 1)
            act.activation(valT[:, :], bank(7), ACT.Copy).then_inc(sem("valT_ready"), 1)

            def save_gathered(n):
                act.wait_ge(sem("g_full"), n)
                act.activation(xg[:, :], bank(4), ACT.Copy).then_inc(sem("xg_ready"), 1)

            save_gathered(1)

            def even_give(g, n):
                act.wait_ge(sem("bc_full"), g * PG + 2 * n + 1)
                if not (isinstance(g, int) and g == 0 and n == 0):
                    act.wait_ge(sem("give_even_ready"), g * 2 + n)
                act.activation(gsq[:, :], bcast(g, 2 * n), ACT.Square, bias=minus_slot[:, 0:1]).then_inc(sem("gsq_ready"), 1)
                act.wait_ge(sem("gsq_ready"), g * 2 + n + 1)
                act.activation(give[2 * n][:, :], gsq[:, :], ACT.Relu, bias=ones_f[:, 0:1], scale=-2.0)\
                    .then_inc(sem("give_even_ready"), 1)

            def group(g, first, last):
                act.wait_ge(sem("gu_full"), g + 1)
                gate = bank(5, 2).rearrange("p (k n) -> p k n", k=PG)[:, :, 0:FF]
                act.activation(th[:, :, :], gate, ACT.Tanh, scale=0.5).then_inc(sem("th_ready"), 1)
                act.wait_ge(sem("ht_full"), g + 1)
                act.activation(hT[:, :], bank(5)[0:FF, :], ACT.Copy).then_inc(sem("hT_ready"), 1)
                even_give(g, 0)
                if not last:
                    save_gathered(g + 2)
                even_give(g, 1)

            over_groups(act, group)
            act.wait_ge(sem("scattered"), PG * G)
            act.activation(outT[:, 0:512], bank(0), ACT.Copy).then_inc(sem("outT_ready"), 1)

            root(2)
            for b in range(B):
                act.wait_ge(sem("hcT_full"), b + 1)
                act.activation(hcT[:, N * b:N * (b + 1)], bank(b), ACT.Copy).then_inc(sem("hcT_ready"), 1)
            for t in range(T):
                act.wait_ge(sem("nmx_ready"), t // TILES + 1)
                act.activation(aw[:, t, :], simc[:, t, :], ACT.Exp, bias=nmx[:, t:t + 1], accum_out=asum[:, t:t + 1]).then_inc(sem("aw_ready"), 1)
            for b in range(B):
                act.wait_ge(sem("aT_full"), b + 1)
                act.activation(aT[:, N * b:N * (b + 1)], bank(5 + b)[0:M, :], ACT.Copy).then_inc(sem("aT_ready"), 1)
            act.wait_ge(sem("hqh_full"), 1)
            act.activation(hqh[:, 0:N], bank(2), ACT.Copy).then_inc(sem("hqh_ready"), 1)
            act.wait_ge(sem("negm_ready"), 1)
            for b in range(B):
                act.activation(e8[:, TILES * b:TILES * (b + 1)], mi[:, TILES * b:TILES * (b + 1)], ACT.Exp,
                               bias=negm[:, b:b + 1], accum_out=es[:, b:b + 1]).then_inc(sem("e8_ready"), 1)
            act.wait_ge(sem("hqh_full"), 2)
            act.activation(hqh[:, N:2 * N], bank(3), ACT.Copy).then_inc(sem("hqh_ready"), 1)

            root(3)
            for k in range(2):
                act.wait_ge(sem("zT_full"), k + 1)
                act.activation(hcT[:, 512 * k:512 * (k + 1)], bank(2 + k), ACT.Copy).then_inc(sem("zT_ready"), 1)
            for b in range(B):
                act.wait_ge(sem("gate_full"), b + 1)
                act.activation(relu_out[:, b, :], bank(4 + b), ACT.Relu, bias=small_at("gate_b1"),
                               accum_out=hsum[:, b:b + 1]).then_inc(sem("hsum_ready"), 1)
            act.wait_ge(sem("g_ready"), 1)
            for b in range(B):
                for e in range(E2P):
                    act.activation(diag[:, b, e, :], ident[:, :], ACT.Copy, scale=gB[:, b, e:e + 1])\
                        .then_inc(sem("diag_ready"), 1)
            act.wait_ge(sem("mb1_ready"), 1)
            for n in range(B * FC):
                b, c = n // FC, n % FC
                act.wait_ge(sem("u_full"), n + 1)
                act.activation(uT[b][:, c, :], bank(2 + n % 4), ACT.Gelu_apprx_tanh, bias=mb1[:, b, c:c + 1])\
                    .then_inc(sem("u_ready"), 1)

        @block.vector
        def _(dve):
            vo = Order(dve, sem("dve_self"))

            def measure(src, a, rows, n):
                for t in range(n):
                    vo.mark(dve.bn_stats(stats[0:rows, a + t, :], src[0:rows, t, :]))
                vo.settle()
                for t in range(n):
                    ins = dve.bn_aggr(mv[0:rows, a + t, :], stats[0:rows, a + t, :])
                ins.then_inc(sem("var0"), 1)

            def normalise_first(src, dst, a, rows, n, k):
                dve.wait_ge(sem("std0"), k)
                vo.mark(dve.reciprocal(rstd[0:rows, a:a + n], std[0:rows, a:a + n]))
                vo.settle()
                dve.wait_ge(sem("var0"), k)
                for t in range(n):
                    dve.tensor_scalar(dst[0:rows, t, :], src[0:rows, t, :], mv[0:rows, a + t, 0:1],
                                      rstd[0:rows, a + t:a + t + 1], ALU.subtract, ALU.mult).then_inc(sem("lat_normed"), 1)

            def norm_stream(n, ready, before):
                def measure_half(k):
                    for t in range(TILES * k, TILES * (k + 1)):
                        vo.mark(dve.bn_stats(stats[:, t, :], xs[:, t, :]))
                    vo.settle()
                    for t in range(TILES * k, TILES * (k + 1)):
                        ins = dve.bn_aggr(mv[:, t, :], stats[:, t, :])
                    ins.then_inc(sem("var"), 1)

                def normalise_half(k):
                    dve.wait_ge(sem("std"), 2 * n - 1 + k)
                    vo.mark(dve.reciprocal(rstd[:, TILES * k:TILES * (k + 1)], std[:, TILES * k:TILES * (k + 1)]))
                    vo.settle()
                    dve.wait_ge(sem("var"), 2 * n - 1 + k)
                    for t in range(TILES * k, TILES * (k + 1)):
                        dve.tensor_scalar(ya[:, t, :], xs[:, t, :], mv[:, t, 0:1], rstd[:, t:t + 1],
                                          ALU.subtract, ALU.mult).then_inc(sem(ready), 1)

                before(0)
                measure_half(0)
                before(1)
                normalise_half(0)
                measure_half(1)
                normalise_half(1)

            dve.wait_ge(sem("x_loaded0"), 16)
            measure(xs[:, 0:TILES, :], 0, P, TILES)
            dve.wait_ge(sem("ctx_loaded"), 16)
            measure(cs, T, M, B)
            normalise_first(xs[:, 0:TILES, :], ya[:, 0:TILES, :], 0, P, TILES, 1)
            normalise_first(cs, cn, T, M, B, 2)
            dve.wait_ge(sem("x_loaded1"), 16)
            measure(xs[:, TILES:T, :], TILES, P, TILES)
            dve.wait_ge(sem("lat_t"), TILES + 2 * B)
            for b in range(B):
                dve.tensor_copy(ctxT[:, b, :], bank(4)[:, P * b:P * b + M]).then_inc(sem("ctxT_ready"), 1)

            def split_kv(b):
                dve.tensor_copy(kv_hi[b][:, :], kvT[b][:, 0:N]).then_inc(sem("kv_hi_ready"), 1)
                dve.wait_ge(sem("kv_hi_ready"), b + 1)
                dve.tensor_tensor(kv_lo[b][:, :], kvT[b][:, 0:N], kv_hi[b][:, :].bitcast(F32), ALU.subtract)\
                    .then_inc(sem("kv_lo_ready"), 1)

            normalise_first(xs[:, TILES:T, :], ya[:, TILES:T, :], TILES, P, TILES, 3)
            dve.wait_ge(sem("pads"), 3 * B)

            dve.engine_nop().then_inc(sem("x_added"), 1)
            dve.engine_nop().then_inc(sem("normed"), 1)

            def k_low(i, c, h):
                b = c % 2
                dve.wait_ge(sem("k_hi"), i * 4 + 2 * c + 2)
                dve.tensor_tensor(kk[b][DH:P, h, 0:KV], xb(c, 0)[DH * h:DH * (h + 1), 0:KV],
                                  kk[b][0:DH, h, 0:KV].bitcast(F32), ALU.subtract).then_inc(sem("k_lo"), 1)

            def q_low(i, c, h):
                b = c % 2
                dve.wait_ge(sem("q_hi"), i * 4 + 2 * c + 2)
                dve.tensor_tensor(qlm[b][0:DH, h, :], xb(c, 1)[DH * h:DH * (h + 1), 0:N],
                                  qq[b][0:DH, h, :].bitcast(F32), ALU.subtract).then_inc(sem("q_lo"), 1)

            def row_max(i, c, r):
                b, j = c % 2, 3 + r
                dve.wait_ge(sem("x_full"), i * (2 * XSTEPS) + XSTEPS * c + j + 1)
                dve.tensor_reduce(nmax[:, b, r // TILES, r % TILES:r % TILES + 1], xb(c, j)[:, 0:KV], AX.X, ALU.max,
                                  negate=True).then_inc(sem("max_done"), 1)

            def shift_rows(i, c, h):
                b = c % 2
                dve.wait_ge(sem("max_turned"), i * 4 + 2 * c + h + 1)
                dve.tensor_tensor(qlm[b][DH:DH + TILES, h, :].rearrange("p (t n) -> p t n", n=P),
                                  sbank[h][0:TILES, 0:P].unsqueeze(1).broadcast_to([TILES, TILES, P]),
                                  mask4[:, :, :], ALU.mult).then_inc(sem("shifts"), 1)

            def recip(i, c, part):
                if part == 0:
                    if isinstance(i, int) and 2 * i + c == U - 1:
                        dve.wait_ge(sem("last_sums_full"), 1)
                        dve.wait_ge(sem("normed"), U)
                    else:
                        dve.wait_ge(sem("mb_full"), i * 4 + 2 * c + 1)
                a, e = part * (N // RECIPS), (part + 1) * (N // RECIPS)
                dve.reciprocal(rsum[:, a:e], mb(i, c)[:, a:e]).then_inc(sem("recips"), 1)

            def normalise(i, c):
                dve.wait_ge(sem("recips"), i * (2 * RECIPS) + RECIPS * (c + 1))
                dve.wait_ge(sem("o_saved"), i * 2 + c + 1)
                dve.tensor_tensor(onorm[:, :], osb[c % 2][:, :], rsum[:, :], ALU.mult).then_inc(sem("normed"), 1)

            def residual(i, c):
                b = c % 2
                dve.wait_ge(sem("mb_full"), i * 4 + 2 * c + 2 - (isinstance(i, int) and 2 * i + c == U - 1))
                if not (isinstance(i, int) and 2 * i + c < 2):
                    dve.wait_ge(sem("x_added"), i * 2 + c + 1)
                if isinstance(i, int) and 2 * i + c == 0:
                    dve.wait_ge(sem("gates"), 1)
                acc = xs[:, TILES * b:TILES * (b + 1), :]
                dve.scalar_tensor_tensor(out=acc, in0=mb(i, c).rearrange("p (t d) -> p t d", d=D),
                                         scalar=tg[:, 0:1], in1=acc, op0=ALU.mult, op1=ALU.add)\
                    .then_inc(sem("x_added"), 1)

            def unit(i, b, tail, ahead):
                c = b + 1
                shift_rows(i, b, 1)
                if ahead:
                    k_low(i, c, 0)
                    k_low(i, c, 1)
                    q_low(i, c, 0)
                    q_low(i, c, 1)
                if isinstance(i, int) and i == 0 and b == 0:
                    dve.wait_ge(sem("kv_ready"), 2 * B)
                    split_kv(0)
                    split_kv(1)
                if tail:
                    recip(i, b - 2, 0)
                if ahead:
                    row_max(i, c, 0)
                    row_max(i, c, 1)
                if tail:
                    recip(i, b - 2, 1)
                if ahead:
                    row_max(i, c, 2)
                    row_max(i, c, 3)
                if tail:
                    normalise(i, b - 2)
                if ahead:
                    row_max(i, c, 4)
                    row_max(i, c, 5)
                    shift_rows(i, c, 0)
                    row_max(i, c, 6)
                if tail:
                    residual(i, b - 2)
                if ahead:
                    row_max(i, c, 7)

            for h in range(2):
                k_low(0, 0, h)
            for h in range(2):
                q_low(0, 0, h)
            for r in range(2 * TILES):
                row_max(0, 0, r)
                if r == TILES + 1:
                    shift_rows(0, 0, 0)

            dve.wait_ge(sem("small_loaded"), 16)
            dve.wait_ge(sem("ctxT_ready"), B)
            w_a = SMALL["w_sim"][0]
            for b in range(B):
                dve.tensor_scalar(ctxw[:, b, 0:M], ctxT[:, b, :], small[:, w_a + 2:w_a + 3], None, ALU.mult)\
                    .then_inc(sem("ctxw_ready"), 1)
                dve.tensor_copy(ctxw[:, b, M:M + 1], small[:, w_a:w_a + 1]).then_inc(sem("ctxw_ready"), 1)
                dve.tensor_scalar(ctxv[:, b, :], ctxT[:, b, :], small[:, w_a + 1:w_a + 2], None, ALU.mult)\
                    .then_inc(sem("ctxw_ready"), 1)

            def pair(i, first, last):
                unit(i, 0, not first, True)
                unit(i, 1, not first, not last)

            over_pairs(dve, pair)

            def last_unit(c):
                if c == 0:
                    for part in range(RECIPS):
                        recip(HP - 1, 0, part)
                    normalise(HP - 1, 0)
                    for part in range(RECIPS):
                        recip(HP - 1, 1, part)
                    residual(HP - 1, 0)
                    normalise(HP - 1, 1)
                else:
                    residual(HP - 1, 1)
                dve.wait_ge(sem("x_added"), U + c)

            norm_stream(1, "y_ready", last_unit)
            dve.wait_ge(sem("y_ready"), T)
            dve.tensor_copy(yhi[:, :, :], ya[:, :, :]).then_inc(sem("yhi_ready"), 1)
            dve.wait_ge(sem("yhi_ready"), 1)
            dve.tensor_tensor(ylo[:, :, :], ya[:, :, :], yhi[:, :, :].bitcast(F32), ALU.subtract).then_inc(sem("ylo_ready"), 1)
            for k in range(2):
                dve.wait_ge(sem("lg_ready"), k + 1)
                for t in range(TILES * k, TILES * (k + 1)):
                    vo.mark(dve.max(top[:, t, :], lg[:, t, :]))
                vo.settle()
                for t in range(TILES * k, TILES * (k + 1)):
                    vo.mark(dve.match_replace(out=rest[:, t, :], in_to_replace=top[:, t, :], in_values=lg[:, t, :],
                                              imm_value=-3.0e38))
            vo.settle()
            dve.tensor_tensor(chosen[:, :, :], rest[:, :, :], lg[:, :, :], ALU.not_equal).then_inc(sem("chosen_ready"), 1)
            dve.tensor_tensor(wgt[:, :, :], lg[:, :, :], top[:, :, 0:1].broadcast_to([P, T, E]), ALU.subtract)\
                .then_inc(sem("logits_shifted"), 1)
            dve.wait_ge(sem("chosen_ready"), 1)
            dve.wait_ge(sem("logits_exp"), 1)
            vo.mark(dve.tensor_tensor(wgt[:, :, :], wgt[:, :, :], chosen[:, :, :], ALU.mult))
            vo.settle()
            vo.mark(dve.reduce_sum(den[:, :], wgt[:, :, :], AX.X))
            vo.settle()
            vo.mark(dve.reciprocal(rden[:, :], den[:, :]))
            dve.wait_ge(sem("queue_full"), 1)
            dve.scalar_tensor_tensor(out=val[:, :, :], in0=bank(7).rearrange("p (t e) -> p t e", e=E), scalar=1.0,
                                     in1=chosen[:, :, :], op0=ALU.add, op1=ALU.mult).then_inc(sem("val_ready"), 1)
            dve.wait_ge(sem("consts2"), 8)
            dve.wait_ge(sem("val_ready"), 1)

            def build_take(g):
                for k in range(2):
                    tiles = slice(T // 2 * k, T // 2 * (k + 1))
                    v = val[:, tiles, EG * g:EG * (g + 1)] if isinstance(g, int) else val[:, tiles, bass.ds(EG * g, EG)]
                    dve.tensor_tensor(take[:, tiles, :, :], v.unsqueeze(3).broadcast_to([P, T // 2, EG, CAP]),
                                      slots[:, :].unsqueeze(1).unsqueeze(1).broadcast_to([P, T // 2, EG, CAP]), ALU.is_equal)\
                        .then_inc(sem("take_ready"), 1)

            build_take(0)
            vo.settle()
            vo.mark(dve.tensor_tensor(wgt[:, :, :], wgt[:, :, :], rden[:, :].unsqueeze(2).broadcast_to([P, T, E]),
                                      ALU.mult))
            vo.settle()
            dve.tensor_copy(whl[:, :, :, 0], wgt[:, :, :]).then_inc(sem("whl_ready"), 1)
            dve.wait_ge(sem("whl_ready"), 1)
            dve.tensor_tensor(whl[:, :, :, 1], wgt[:, :, :], whl[:, :, :, 0].bitcast(F32), ALU.subtract)\
                .then_inc(sem("whl_ready"), 1)
            dve.wait_ge(sem("sth_ready"), 1)
            vo.mark(dve.scalar_tensor_tensor(out=hs[:, :], in0=sth[:, :], scalar=1.0, in1=bank(0, 2)[0:FF, :],
                                             op0=ALU.add, op1=ALU.mult))
            vo.settle()
            dve.wait_ge(sem("shared_up_full"), 1)
            dve.scalar_tensor_tensor(out=hs[:, :], in0=hs[:, :], scalar=0.5, in1=bank(2, 2)[0:FF, :],
                                     op0=ALU.mult, op1=ALU.mult).then_inc(sem("hs_ready"), 1)

            def odd_give(g, n):
                dve.wait_ge(sem("bc_full"), g * PG + 2 * n + 2)
                dve.tensor_scalar(give[2 * n + 1][:, :], bcast(g, 2 * n + 1), slot_of[:, 0:1], None, ALU.is_equal)\
                    .then_inc(sem("give_odd_ready"), 1)

            def group(g, first, last):
                def keep_own():
                    dve.wait_ge(sem("wr_full"), g + 1)
                    dve.tensor_tensor(wm[0:2 * EG, :], bank(7)[0:2 * EG, :], own_e[:, :, :].rearrange("p e s -> p (e s)"),
                                      ALU.mult).then_inc(sem("wm_ready"), 1)

                if not first:
                    keep_own()
                if not first:
                    odd_give(g - 1, 1)
                gu = bank(5, 2).rearrange("p (k n) -> p k n", k=PG)
                dve.wait_ge(sem("th_ready"), g + 1)
                dve.scalar_tensor_tensor(out=hh[:, :, :], in0=th[:, :, :], scalar=1.0, in1=gu[:, :, 0:FF],
                                         op0=ALU.add, op1=ALU.mult).then_inc(sem("h_half"), 1)
                dve.wait_ge(sem("h_half"), g + 1)
                dve.scalar_tensor_tensor(out=hh[:, :, :], in0=hh[:, :, :], scalar=0.5, in1=gu[:, :, FF:2 * FF],
                                         op0=ALU.mult, op1=ALU.mult).then_inc(sem("h_ready"), 1)
                if first:
                    keep_own()
                if last:
                    odd_give(g, 0)
                else:
                    build_take(g + 1)
                dve.wait_ge(sem("ws_full"), g + 1)
                dve.wait_ge(sem("y_full"), g + 1)
                dve.tensor_copy(ws[:, :], bank(6)[:, 0:2 * PG].rearrange("p (k n) -> p k n", n=2)[:, :, 0])\
                    .then_inc(sem("ws_ready"), 1)
                dve.wait_ge(sem("ws_ready"), g + 1)
                dve.tensor_tensor(ys[:, :, :], bank(7).rearrange("p (k d) -> p k d", d=D),
                                  ws[:, :].unsqueeze(2).broadcast_to([P, PG, D]), ALU.mult).then_inc(sem("ys_ready"), 1)
                dve.wait_ge(sem("ys_ready"), g + 1)
                dve.tensor_copy(ehi[:, :, :], ys[:, :, :]).then_inc(sem("ehi_ready"), 1)
                dve.wait_ge(sem("ehi_ready"), g + 1)
                dve.tensor_tensor(elo[:, :, :], ys[:, :, :], ehi[:, :, :].bitcast(F32), ALU.subtract)\
                    .then_inc(sem("elo_ready"), 1)
                if not last:
                    odd_give(g, 0)

            over_groups(dve, group)
            odd_give(G - 1, 1)

            dve.wait_ge(sem("scattered"), PG * G)
            dve.tensor_copy(outT[:, 512:1024], bank(1)).then_inc(sem("outT_ready"), 1)

            def add_experts(k):
                dve.wait_ge(sem("moe_full"), k + 1)
                acc = xs[:, 4 * k:4 * k + 4, :]
                dve.scalar_tensor_tensor(out=acc, in0=bank(2 + k).rearrange("p (t d) -> p t d", d=D), scalar=tg[:, 2:3],
                                         in1=acc, op0=ALU.mult, op1=ALU.add).then_inc(sem("x2_ready"), 1)
                dve.wait_ge(sem("x2_ready"), k + 1)

            norm_stream(2, "hc_ready", add_experts)
            dve.wait_ge(sem("simv_full"), 1)
            vo.mark(dve.tensor_copy(simv[:, :, :], bank(6)[:, 0:B * M].rearrange("p (b m) -> p b m", b=B)))
            vo.mark(dve.tensor_scalar(row[:, :], small_at("b_qv_row"), tg[:, 1:2], None, ALU.mult))
            vo.settle()

            def sim_tiles(b):
                return bank(2 + b).rearrange("p (t n) -> p t n", n=P)

            for b in range(B):
                tiles = slice(TILES * b, TILES * (b + 1))
                dve.wait_ge(sem("sim_full"), b + 1)
                vo.mark(dve.tensor_tensor(simc[:, tiles, :], sim_tiles(b)[:, :, 0:M],
                                          simv[:, b, :].unsqueeze(1).broadcast_to([P, TILES, M]), ALU.add))
                vo.settle()
                dve.tensor_reduce(nmx[:, tiles], simc[:, tiles, :], AX.X, ALU.max, negate=True).then_inc(sem("nmx_ready"), 1)
            vo.settle()
            vo.mark(dve.tensor_tensor(xs[:, :, :], xs[:, :, :], row[:, :].unsqueeze(1).broadcast_to([P, T, D]), ALU.add))
            for b in range(B):
                tiles = slice(TILES * b, TILES * (b + 1))
                dve.wait_ge(sem("aw_ready"), TILES * (b + 1))
                vo.mark(dve.reciprocal(asum[:, tiles], asum[:, tiles]))
                vo.settle()
                dve.tensor_tensor(aw[:, tiles, :], aw[:, tiles, :], asum[:, tiles].unsqueeze(2).broadcast_to([P, TILES, M]),
                                  ALU.mult).then_inc(sem("a_ready"), 1)
            dve.wait_ge(sem("nmx_ready"), B)
            for b in range(B):
                tiles = slice(TILES * b, TILES * (b + 1))
                ins = dve.scalar_tensor_tensor(out=mi[:, tiles], in0=sim_tiles(b)[:, :, M], scalar=small_at("b_sim"),
                                               in1=nmx[:, tiles], op0=ALU.add, op1=ALU.subtract)
                vo.mark(ins)
            vo.settle()
            dve.tensor_reduce(mbest[:, :], mi[:, :].rearrange("p (b t) -> p b t", b=B), AX.X, ALU.max)\
                .then_inc(sem("mbest_ready"), 1)
            dve.wait_ge(sem("mbestT_full"), 1)
            vo.mark(dve.tensor_reduce(m2[:, :], bank(7)[0:B, 0:P], AX.X, ALU.max, negate=True))
            vo.settle()
            dve.tensor_scalar(dm[:, :], ident[0:B, 0:B], m2[:, 0:1], None, ALU.mult).then_inc(sem("dm_ready"), 1)
            dve.wait_ge(sem("negm_full"), 1)
            dve.tensor_copy(negm[:, :], bank(7)[:, 0:B]).then_inc(sem("negm_ready"), 1)

            def multiply(b):
                dve.wait_ge(sem("hqh_ready"), b + 1)
                dve.tensor_tensor(f3[:, N * b:N * (b + 1)], hcT[:, N * b:N * (b + 1)], hqh[:, N * b:N * (b + 1)], ALU.mult)\
                    .then_inc(sem("f3_ready"), 1)

            multiply(0)
            dve.wait_ge(sem("hcb_full"), 1)
            vo.mark(dve.reciprocal(rtot[:, :], bank(7)[:, 0:B]))
            vo.settle()
            vo.mark(dve.tensor_tensor(hcb[:, :], bank(7)[:, 2:2 + B], rtot[:, :], ALU.mult))
            vo.settle()
            for b in range(B):
                dve.scalar_tensor_tensor(out=wc[:, b, :], in0=wqv[:, 3, :], scalar=hcb[:, b:b + 1], in1=wqv[:, 0, :],
                                         op0=ALU.mult, op1=ALU.add).then_inc(sem("wc_ready"), 1)
            multiply(1)

            def add_context(k):
                dve.wait_ge(sem("hcq_full"), k + 1)
                acc = xs[:, 4 * k:4 * k + 4, :]
                dve.scalar_tensor_tensor(out=acc, in0=bank(k).rearrange("p (t d) -> p t d", d=D), scalar=tg[:, 1:2],
                                         in1=acc, op0=ALU.mult, op1=ALU.add).then_inc(sem("x3_ready"), 1)
                dve.wait_ge(sem("x3_ready"), k + 1)

            norm_stream(3, "z_ready", add_context)
            vo.mark(dve.tensor_scalar(row[:, :], small_at("b2_row"), tg[:, 3:4], None, ALU.mult))
            vo.settle()
            vo.mark(dve.tensor_tensor(xs[:, :, :], xs[:, :, :], row[:, :].unsqueeze(1).broadcast_to([P, T, D]), ALU.add))
            dve.wait_ge(sem("gB_full"), 1)
            dve.scalar_tensor_tensor(out=gB[:, :, :], in0=bank(6)[:, 0:B * E2].rearrange("p (b e) -> p b e", b=B),
                                     scalar=1.0 / N, in1=small_at("gate_b2").unsqueeze(1).broadcast_to([P, B, E2]),
                                     op0=ALU.mult, op1=ALU.add).then_inc(sem("g_ready"), 1)
            dve.scalar_tensor_tensor(out=gT[:, :], in0=bank(7)[0:E2, 0:B], scalar=1.0 / N,
                                     in1=small_at("gate_b2_col", E2).broadcast_to([E2, B]),
                                     op0=ALU.mult, op1=ALU.add).then_inc(sem("g_ready"), 1)
            dve.wait_ge(sem("g_ready"), 2)
            for b in range(B):
                vo.mark(dve.tensor_tensor(tb[:, b, :, :], small_at("Tb1").rearrange("p (c e) -> p c e", e=E2),
                                          gB[:, b, :].unsqueeze(1).broadcast_to([P, FC, E2]), ALU.mult))
            vo.settle()
            vo.mark(dve.reduce_sum(mb1[:, :, :], tb[:, :, :, :], AX.X))
            vo.settle()
            dve.tensor_tensor(mb1[:, :, :], mb1[:, :, :], small_at("b1").unsqueeze(1).broadcast_to([P, B, FC]), ALU.add)\
                .then_inc(sem("mb1_ready"), 1)
            dve.wait_ge(sem("weights_loaded"), 16 * 9)
            dve.wait_ge(sem("tw_loaded"), 32)
            for e in range(E2):
                for b in range(B):
                    if e:
                        dve.wait_ge(sem("mw1_ready"), B * (e - 1) + b + 1)
                    dve.scalar_tensor_tensor(out=mw1[b][:, :], in0=tw1[:, e, :], scalar=gB[:, b, e:e + 1],
                                             in1=mw1[b][:, :] if e else w1[:, :], op0=ALU.mult, op1=ALU.add)\
                        .then_inc(sem("mw1_ready"), 1)
            for e in range(E2P, E2):
                vo.settle()
                for b in range(B):
                    vo.mark(dve.scalar_tensor_tensor(out=mw2[b][:, :, :], in0=tw2[:, e, :, :], scalar=gB[:, b, e:e + 1],
                                                     in1=w2[:, :, :] if e == E2P else mw2[b][:, :, :], op0=ALU.mult,
                                                     op1=ALU.add))
            vo.settle()
            for b in range(B):
                dve.wait_ge(sem("mw2_full"), b + 1)
                dve.tensor_tensor(mw2[b][:, :, :], bank(b).rearrange("p (c d) -> p c d", d=D), mw2[b][:, :, :], ALU.add)\
                    .then_inc(sem("mw2_ready"), 1)
            dve.wait_ge(sem("bias_full"), 1)
            for b in range(B):
                acc = xs[:, TILES * b:TILES * (b + 1), :]
                vo.mark(dve.scalar_tensor_tensor(out=acc, in0=bank(7)[:, D * (b + 1):D * (b + 2)].unsqueeze(1).broadcast_to([P, TILES, D]),
                                                 scalar=tg[:, 3:4], in1=acc, op0=ALU.mult, op1=ALU.add))
            vo.settle()
            dve.engine_nop().then_inc(sem("bias_added"), 1)
            for k in range(T // 2):
                dve.wait_ge(sem("ffn_full"), k + 1)
                dve.scalar_tensor_tensor(out=res[:, 2 * k:2 * k + 2, :],
                                         in0=quarter(k)[:, 0:2 * D].rearrange("p (t d) -> p t d", d=D),
                                         scalar=tg[:, 3:4], in1=xs[:, 2 * k:2 * k + 2, :], op0=ALU.mult, op1=ALU.add)\
                    .then_inc(sem("out_ready"), 1)

        @block.tensor
        def _(pe):
            pe.wait_ge(sem("consts"), 2)
            for t in range(TILES):
                pe.wait_ge(sem("lat_normed"), t + 1)
                pe.transpose(bank(6)[:, P * t:P * (t + 1)], ya[:, t, :], ident[:, :]).then_inc(sem("lat_t"), 1)
            for b in range(B):
                pe.wait_ge(sem("lat_normed"), TILES + b + 1)
                pe.transpose(bank(7)[:, P * b:P * b + M], cn[0:M, b, :], ident[0:M, 0:M]).then_inc(sem("lat_t"), 1)
            pe.wait_ge(sem("ctx_loaded"), 16)
            for b in range(B):
                pe.transpose(bank(4)[:, P * b:P * b + M], cs[0:M, b, :], ident[0:M, 0:M]).then_inc(sem("lat_t"), 1)

            def turn_second_batch():
                for t in range(TILES):
                    pe.wait_ge(sem("lat_normed"), TILES + B + t + 1)
                    pe.transpose(bank(5)[:, P * t:P * (t + 1)], ya[:, TILES + t, :], ident[:, :]).then_inc(sem("lat_t"), 1)

            def project(i, c, j, at):
                dst, cols = xb(c, j)[:, 0:N], slice(at, at + P)
                if isinstance(i, int) and 2 * i + c < 2:
                    return pe.matmul(dst, wx[:, cols], kvT[c][:, 0:N], start=True, stop=True)
                pe.matmul(dst, wqk_hi[:, cols], kv_hi[c % 2][:, :], start=True, stop=False)
                pe.matmul(dst, wqk_lo[:, cols], kv_hi[c % 2][:, :], start=False, stop=False)
                return pe.matmul(dst, wqk_hi[:, cols], kv_lo[c % 2][:, :], start=False, stop=True)

            def proj_k(i, c):
                if isinstance(i, int) and 2 * i + c == 0:
                    pe.wait_ge(sem("kv_ready"), B)
                else:
                    if isinstance(i, int) and 2 * i + c == 1:
                        pe.wait_ge(sem("kv_ready"), 2 * B)
                    pe.wait_ge(sem("max_done"), i * (4 * TILES) + 2 * TILES * c - 1)
                if isinstance(i, int) and 2 * i + c < 2:
                    pe.wait_ge(sem("wx_loaded"), 16)
                else:
                    pe.wait_ge(sem("kv_lo_ready"), B)
                    pe.wait_ge(sem("wqk_lo_ready"), i + c // 2)
                project(i, c, 0, P)
                pe.matmul(xb(c, 0)[:, N:KV], wx[:, P:2 * P], kvT[c % 2][:, N:KV], start=True, stop=True)\
                    .then_inc(sem("x_full"), 1)

            def proj_q(i, c):
                if not (isinstance(i, int) and 2 * i + c == 0):
                    pe.wait_ge(sem("max_done"), i * (4 * TILES) + 2 * TILES * c)
                project(i, c, 1, 0).then_inc(sem("x_full"), 1)

            def proj_v(i, c):
                pe.wait_ge(sem("k_lo"), i * 4 + 2 * c + 2)
                for jt in range(JT):
                    w = JW[jt]
                    ins = pe.matmul(xb(c, 2)[0:w, P * jt:P * (jt + 1)], kvT[c % 2][:, P * jt:P * jt + w],
                                    wx[:, 2 * P:3 * P], start=True, stop=True)
                ins.then_inc(sem("x_full"), 1)

            def scores_for_max(i, c, r):
                b, j, h, t = c % 2, 3 + r, r // TILES, r % TILES
                if r == 0:
                    pe.wait_ge(sem("q_lo"), i * 4 + 2 * c + 2)
                elif r == 1:
                    pe.wait_ge(sem("v_ready"), i * 4 + 2 * c + 2)
                else:
                    pe.wait_ge(sem("max_done"), i * (4 * TILES) + 2 * TILES * c + r - 1)
                if t == 0:
                    pe.wait_ge(sem("q_dup"), i * 4 + 2 * c + h + 1)
                pe.matmul(xb(c, j)[:, 0:N], qq[b][:, h, P * t:P * (t + 1)], kk[b][:, h, 0:N], start=True, stop=True)
                pe.matmul(xb(c, j)[:, N:KVP], qq[b][:, h, P * t:P * (t + 1)], kk[b][:, h, N:KVP],
                          start=True, stop=True).then_inc(sem("x_full"), 1)

            def turn_max(i, c, h):
                pe.wait_ge(sem("max_done"), i * (4 * TILES) + 2 * TILES * c + TILES * (h + 1))
                if isinstance(i, int) and 2 * i + c == 0:
                    pe.wait_ge(sem("ctxT_ready" if h == 0 else "kv_ready"), B if h == 0 else 2 * B)
                else:
                    pe.wait_ge(sem("exp_done"), i * (4 * JT) + 2 * JT * c + h - 1)
                pe.transpose(sbank[h][0:TILES, 0:P], nmax[:, c % 2, h, :], ident[:, :]).then_inc(sem("max_turned"), 1)

            def scores(i, b, jt, h):
                w = JW[jt]
                if jt == 0:
                    pe.wait_ge(sem("k_dup"), i * 4 + 2 * b + h + 1)
                    pe.wait_ge(sem("shifts"), i * 4 + 2 * b + h + 1)
                else:
                    pe.wait_ge(sem("exp_done"), i * (4 * JT) + 2 * JT * b + 2 * jt + h - 1)
                pe.matmul(sbank[h][0:w, :], kk[b][:, h, P * jt:P * jt + w], qq[b][:, h, :], start=True, stop=False)
                pe.matmul(sbank[h][0:w, :], ko[b][0:DH + TILES, h, P * jt:P * jt + w], qlm[b][0:DH + TILES, h, :],
                          start=False, stop=True).then_inc(sem("s_full"), 1)

            def values(i, b, jt):
                w = JW[jt]
                if jt == 0:
                    if not (isinstance(i, int) and i == 0 and b == 0):
                        pe.wait_ge(sem("o_saved"), i * 2 + b)
                    pe.wait_ge(sem("v_ready"), i * 4 + 2 * b + 2)
                pe.wait_ge(sem("exp_done"), i * (4 * JT) + 2 * JT * b + 2 * jt + 2)
                for h in range(2):
                    ins = pe.matmul(obank[DH * h:DH * (h + 1), :], vv[b][0:w, jt, DH * h:DH * (h + 1)],
                                    pt[b][0:w, jt, h, :], start=(jt == 0), stop=(jt == JT - 1))
                ins.then_inc(sem("av_done"), 1)

            def sums(i, c):
                pe.wait_ge(sem("pool_added"), i * (2 * (JT - 1)) + (JT - 1) * (c + 1))
                if isinstance(i, int) and 2 * i + c == U - 2:
                    pe.wait_ge(sem("max_done"), U * 2 * TILES)
                elif not (isinstance(i, int) and 2 * i + c == 0):
                    pe.wait_ge(sem("x_added"), i * 2 + c + 1)
                for h in range(2):
                    ins = pe.matmul(mb(i, c)[DH * h:DH * (h + 1), :], ones_f[:, 0:DH], psm[c % 2][:, h, :],
                                    start=True, stop=True)
                ins.then_inc(sem("mb_full"), 1)

            def out_proj(i, c):
                pe.wait_ge(sem("normed"), i * 2 + c + 2)
                pe.wait_ge(sem("wo_loaded"), (i + c // 2 + 1) * 16)
                for t in range(TILES):
                    ins = pe.matmul(mb(i, c)[:, P * t:P * (t + 1)], onorm[:, P * t:P * (t + 1)], wo[:, :],
                                    start=True, stop=True)
                ins.then_inc(sem("mb_full"), 1)

            def last_sums(jt):
                w = JW[jt]
                for h in range(2):
                    ins = pe.matmul(mb(HP - 1, 1)[DH * h:DH * (h + 1), :], ones_f[0:w, 0:DH], pt[1][0:w, jt, h, :],
                                    start=(jt == 0), stop=(jt == JT - 1))
                if jt == JT - 1:
                    ins.then_inc(sem("last_sums_full"), 1)

            def last_unit():
                i, b = HP - 1, 1
                scores(i, b, 0, 0)
                turn_max(i, b, 1)
                values(i, 0, JT - 1)
                scores(i, b, 0, 1)
                sums(i, -1)
                for jt in range(1, JT):
                    scores(i, b, jt, 0)
                    scores(i, b, jt, 1)
                    values(i, b, jt - 1)
                    if jt == 2:
                        out_proj(i, -1)
                        sums(i, 0)
                    last_sums(jt - 1)
                pe.wait_ge(sem("exp_done"), U * 2 * JT)
                last_sums(JT - 1)
                values(i, b, JT - 1)
                out_proj(i, 0)
                out_proj(i, 1)

            def unit(i, b, tail, tail2, ahead):
                c = b + 1
                scores(i, b, 0, 0)
                if ahead and not (isinstance(i, int) and i == 0 and b == 0):
                    proj_k(i, c)
                turn_max(i, b, 1)
                if tail:
                    values(i - 1 if b == 0 else i, 1 - b, JT - 1)
                if ahead:
                    proj_q(i, c)
                scores(i, b, 0, 1)
                if tail2:
                    sums(i, b - 2)
                scores(i, b, 1, 0)
                if ahead:
                    proj_v(i, c)
                scores(i, b, 1, 1)
                values(i, b, 0)
                scores(i, b, 2, 0)
                if ahead:
                    scores_for_max(i, c, 0)
                scores(i, b, 2, 1)
                if ahead:
                    scores_for_max(i, c, 1)
                values(i, b, 1)
                scores(i, b, 3, 0)
                if ahead:
                    scores_for_max(i, c, 2)
                scores(i, b, 3, 1)
                if ahead:
                    scores_for_max(i, c, 3)
                values(i, b, 2)
                if ahead:
                    scores_for_max(i, c, 4)
                scores(i, b, 4, 0)
                scores(i, b, 4, 1)
                if ahead:
                    scores_for_max(i, c, 5)
                values(i, b, 3)
                if ahead:
                    turn_max(i, c, 0)
                    scores_for_max(i, c, 6)
                if tail2:
                    out_proj(i, b - 2)
                if ahead:
                    scores_for_max(i, c, 7)

            proj_k(0, 0)
            proj_q(0, 0)
            turn_second_batch()
            proj_v(0, 0)
            for r in range(2 * TILES):
                scores_for_max(0, 0, r)
                if r == TILES + 1:
                    turn_max(0, 0, 0)
            proj_k(0, 1)

            def pair(i, first, last):
                unit(i, 0, not first, not first, True)
                if last:
                    last_unit()
                else:
                    unit(i, 1, True, not first, True)

            over_pairs(pe, pair)

            def turn_tiles(k0, ready, full):
                for t in range(T):
                    pe.wait_ge(sem(ready), t + 1)
                    ins = pe.transpose(bank(k0 + t // 4)[:, P * (t % 4):P * (t % 4 + 1)], ya[:, t, :], ident[:, :])
                    if t % 4 == 3:
                        ins.then_inc(sem(full), 1)

            turn_tiles(0, "y_ready", "yT_full")
            pe.wait_ge(sem("weights_loaded"), 16 * 9)
            for t in range(T):
                k = t // TILES
                pe.wait_ge(sem("yT_ready"), k + 1)
                ins = pe.matmul(bank(2 + 5 * k)[:, E * (t % TILES):E * (t % TILES + 1)], yT[:, t, :], rw[:, :],
                                start=True, stop=True)
                if t % TILES == TILES - 1:
                    ins.then_inc(sem("lg_full"), 1)

            def shared(part, full):
                for k in range(2):
                    ins = pe.matmul(bank(2 * part + k)[0:FF, :], wsgu[:, FF * part:FF * (part + 1)],
                                    yT[:, 4 * k:4 * k + 4, :], start=True, stop=True)
                ins.then_inc(sem(full), 1)

            shared(0, "shared_gate_full")
            pe.wait_ge(sem("chosen_ready"), 1)
            pe.wait_ge(sem("lg_ready"), 2)
            pe.wait_ge(sem("consts2"), 8)
            ch = chosen[:, :, :].rearrange("p t e -> p (t e)")
            pe.matmul(bank(7), before[:, :], ch, start=True, stop=False)
            for s in range(1, T):
                ins = pe.matmul(bank(7)[:, E * s:], ones_b[:, :], ch[:, 0:E * (T - s)], start=False, stop=(s == T - 1))
            ins.then_inc(sem("queue_full"), 1)
            shared(1, "shared_up_full")
            pe.wait_ge(sem("val_ready"), 1)
            for q in range(T // 2):
                ins = pe.transpose(bank(7)[:, P * q:P * (q + 1)], val[:, 2 * q:2 * q + 2, :].rearrange("p t e -> p (t e)"),
                                   ident[:, :])
            ins.then_inc(sem("valT_full"), 1)

            def gather(g, tiles):
                pe.wait_ge(sem("take_ready"), 2 * g + 1 + tiles[0] // (T // 2))
                for t in tiles:
                    for part in (yhi, ylo):
                        ins = pe.matmul(bank(4), part[:, t, :], take[:, t, :, :].rearrange("p e s -> p (e s)"),
                                        start=(t == 0 and part is yhi), stop=(t == T - 1 and part is ylo))
                if tiles[-1] == T - 1:
                    ins.then_inc(sem("g_full"), 1)

            def weight_rows(g):
                pe.wait_ge(sem("whg_ready"), g + 1)
                for t in range(T):
                    ins = pe.matmul(bank(7)[0:2 * EG, :], whg[:, t, :], take[:, t, :, :].rearrange("p e s -> p (e s)"),
                                    start=(t == 0), stop=(t == T - 1))
                ins.then_inc(sem("wr_full"), 1)

            def broadcast(g, p):
                if isinstance(g, int) and g == G - 1 and p > 0:
                    if p == 1:
                        pe.wait_ge(sem("hT_ready"), G)
                    else:
                        pe.wait_ge(sem("gsq_ready" if p == 2 else "give_odd_ready"), g * 2 + 1)
                elif p % 2:
                    pe.wait_ge(sem("gsq_ready"), g * 2 + p // 2 + 1)
                elif not (isinstance(g, int) and g == 0 and p == 0):
                    pe.wait_ge(sem("give_odd_ready"), g * 2 + p // 2)
                for k in range(2):
                    if isinstance(g, int):
                        a = (k * E + EG * g + 2 * p) * 64
                        sel = spread[:, a:a + P]
                    else:
                        sel = spread[:, bass.ds(g * (EG * 64) + (k * E + 2 * p) * 64, P)]
                    ins = pe.matmul(bcast(g, p)[:, 512 * k:512 * (k + 1)], sel, valT[:, :], start=True, stop=True)
                ins.then_inc(sem("bc_full"), 1)

            def scatter(g, p, last=False):
                pe.wait_ge(sem("elo_ready"), g + 1)
                pe.wait_ge(sem("give_odd_ready" if p % 2 else "give_even_ready"), g * 2 + p // 2 + 1)
                for part in (ehi, elo):
                    for k in range(2):
                        ins = pe.matmul(bank(k), part[:, p, :], give[p][:, 512 * k:512 * (k + 1)], start=False,
                                        stop=last and part is elo)
                ins.then_inc(sem("scattered"), 1)

            pe.wait_ge(sem("ylo_ready"), 1)
            gather(0, range(0, T // 2))
            gather(0, range(T // 2, T))
            def group(g, first, last):
                pe.wait_ge(sem("xg_ready"), g + 1)
                pe.wait_ge(sem("wgu_loaded"), (g + 1) * 16)
                if not first:
                    pe.wait_ge(sem("hT_ready"), g)
                    pe.wait_ge(sem("ws_ready"), g)
                for e in range(EG):
                    a = 256 * (e // 2)
                    ins = pe.matmul(bank(5, 2)[64 * (e % 2):64 * (e % 2) + 64, a:a + 2 * FF], xg[:, CAP * e:CAP * (e + 1)],
                                    wgu[:, e, :], start=True, stop=True)
                ins.then_inc(sem("gu_full"), 1)
                if first:
                    pe.wait_ge(sem("valT_ready"), 1)
                    weight_rows(0)
                    pe.wait_ge(sem("hs_ready"), 1)
                    for k in range(2):
                        pe.matmul(bank(k), wsdn[:, :], hs[:, :].rearrange("f (q k n) -> f k q n", k=2, n=P)[:, k, :, :],
                                  start=True, stop=False)
                if not first:
                    broadcast(g - 1, 3)
                    for p in range(PG):
                        scatter(g - 1, p)
                pe.wait_ge(sem("h_ready"), g + 1)
                for p in range(PG):
                    ins = pe.transpose(bank(5)[0:FF, P * p:P * (p + 1)], hh[:, p, :], ident[:, :])
                ins.then_inc(sem("ht_full"), 1)
                pe.wait_ge(sem("wm_ready"), g + 1)
                for p in range(PG):
                    ins = pe.matmul(bank(6)[:, 2 * p:2 * p + 2], wm[:, P * p:P * (p + 1)], ones_r[:, :],
                                    start=True, stop=True)
                ins.then_inc(sem("ws_full"), 1)
                broadcast(g, 0)
                if last:
                    broadcast(g, 1)
                pe.wait_ge(sem("hT_ready"), g + 1)
                pe.wait_ge(sem("wdn_loaded"), (g + 1) * 16)
                for e in range(EG):
                    a = D * (e // 2)
                    ins = pe.matmul(bank(7)[64 * (e % 2):64 * (e % 2) + 64, a:a + D], hT[:, CAP * e:CAP * (e + 1)],
                                    wdn[:, e, :], start=True, stop=True)
                ins.then_inc(sem("y_full"), 1)
                if not last:
                    gather(g + 1, range(0, T // 2))
                if not last:
                    broadcast(g, 1)
                    gather(g + 1, range(T // 2, T))
                broadcast(g, 2)
                if not last:
                    pe.wait_ge(sem("ys_ready"), g + 1)
                    weight_rows(g + 1)

            over_groups(pe, group)
            broadcast(G - 1, 3)
            for p in range(PG):
                scatter(G - 1, p, last=(p == PG - 1))
            pe.wait_ge(sem("ctxw_ready"), 3 * B)
            pe.matmul(bank(6)[:, 0:B * M], ones_f[:, :], ctxv[:, :, :].rearrange("p b m -> p (b m)"), start=True, stop=True)\
                .then_inc(sem("simv_full"), 1)
            pe.wait_ge(sem("outT_ready"), 2)
            for t in range(T):
                q, k = t // 2, t % 2
                ins = pe.transpose(bank(2 + t // 4)[:, P * (t % 4):P * (t % 4 + 1)],
                                   outT[:, 512 * k + P * q:512 * k + P * (q + 1)], ident[:, :])
                if t % 4 == 3:
                    ins.then_inc(sem("moe_full"), 1)

            turn_tiles(0, "hc_ready", "hcT_full")
            for t in range(T):
                b = t // TILES
                pe.wait_ge(sem("hcT_ready"), b + 1)
                ins = pe.matmul(bank(2 + b)[:, P * (t % TILES):P * (t % TILES) + M + 1], hcT[:, P * t:P * (t + 1)],
                                ctxw[:, b, :], start=True, stop=True)
                if t % TILES == TILES - 1:
                    ins.then_inc(sem("sim_full"), 1)

            def turn_weights(b):
                pe.wait_ge(sem("a_ready"), b + 1)
                for t in range(TILES):
                    ins = pe.transpose(bank(5 + b)[0:M, P * t:P * (t + 1)], aw[:, TILES * b + t, :], ident[:, :])
                ins.then_inc(sem("aT_full"), 1)

            def attend(b):
                pe.wait_ge(sem("aT_ready"), b + 1)
                pe.wait_ge(sem("mbest_ready"), 1)
                pe.matmul(bank(2 + b), cs[0:M, b, :], aT[:, N * b:N * (b + 1)], start=True, stop=True)\
                    .then_inc(sem("hqh_full"), 1)

            turn_weights(0)
            pe.wait_ge(sem("mbest_ready"), 1)
            pe.transpose(bank(7)[0:B, 0:P], mbest[:, :], ident[:, :]).then_inc(sem("mbestT_full"), 1)
            turn_weights(1)
            attend(0)
            pe.wait_ge(sem("dm_ready"), 1)
            pe.matmul(bank(7)[:, 0:B], ones_f[0:B, :], dm[:, :], start=True, stop=True).then_inc(sem("negm_full"), 1)
            attend(1)
            pe.wait_ge(sem("e8_ready"), B)
            pe.matmul(bank(7)[:, 0:B], ones_f[:, :], es[:, :], start=True, stop=True)
            for b in range(B):
                for t in range(TILES):
                    k = TILES * b + t
                    ins = pe.matmul(bank(7)[:, 2 + b:3 + b], ya[:, k, :], e8[:, k:k + 1], start=(t == 0),
                                    stop=(t == TILES - 1))
            ins.then_inc(sem("hcb_full"), 1)
            pe.wait_ge(sem("hcT_ready"), B)
            for n, (left, right) in enumerate(((hqh, 1), (hcT, 0), (f3, 2))):
                for t in range(T):
                    b = t // TILES
                    if right == 1:
                        pe.wait_ge(sem("hqh_ready"), b + 1)
                    elif right == 0:
                        pe.wait_ge(sem("wc_ready"), b + 1)
                    else:
                        pe.wait_ge(sem("f3_ready"), b + 1)
                    w = wc[:, b, :] if right == 0 else wqv[:, right, :]
                    ins = pe.matmul(bank(b)[:, P * (t % TILES):P * (t % TILES + 1)], left[:, P * t:P * (t + 1)], w,
                                    start=(n == 0 and t % TILES == 0), stop=(n == 2 and t % TILES == TILES - 1))
                    if n == 2 and t % TILES == TILES - 1:
                        ins.then_inc(sem("hcq_full"), 1)

            turn_tiles(2, "z_ready", "zT_full")
            for b in range(B):
                pe.wait_ge(sem("zT_ready"), b + 1)
                pe.matmul(bank(4 + b), gw1[:, :], hcT[:, N * b:N * (b + 1)], start=True, stop=True)\
                    .then_inc(sem("gate_full"), 1)
            pe.wait_ge(sem("hsum_ready"), B)
            for b in range(B):
                ins = pe.matmul(bank(6)[:, E2 * b:E2 * (b + 1)], hsum[:, b:b + 1].broadcast_to([P, P]), gw2[:, :],
                                start=True, stop=True)
            pe.matmul(bank(7)[0:E2, 0:B], gw2[:, :], hsum[:, :], start=True, stop=True).then_inc(sem("gB_full"), 1)
            pe.wait_ge(sem("tw_loaded"), 32)
            for b in range(B):
                for e in range(E2P):
                    pe.wait_ge(sem("diag_ready"), E2P * b + e + 1)
                    ins = pe.matmul(bank(b), diag[:, b, e, :], tw2[:, e, :, :].rearrange("p c d -> p (c d)"),
                                    start=(e == 0), stop=(e == E2P - 1))
                ins.then_inc(sem("mw2_full"), 1)
                if b == 0:
                    pe.wait_ge(sem("g_ready"), 2)
                    for k in range(B):
                        ins = pe.matmul(bank(7)[:, D * (k + 1):D * (k + 2)], gT[:, k:k + 1].broadcast_to([E2, P]), tb2[:, :],
                                        start=True, stop=True)
                    ins.then_inc(sem("bias_full"), 1)
            for n in range(B * FC):
                b, c = n // FC, n % FC
                if n == 0:
                    pe.wait_ge(sem("mw1_ready"), B * E2)
                if n >= 4:
                    pe.wait_ge(sem("u_ready"), n - 3)
                pe.matmul(bank(2 + n % 4), mw1[b][:, P * c:P * (c + 1)], hcT[:, N * b:N * (b + 1)], start=True, stop=True)\
                    .then_inc(sem("u_full"), 1)
            for b in range(B):
                pe.wait_ge(sem("u_ready"), FC * (b + 1))
                pe.wait_ge(sem("mw2_ready"), b + 1)
                for t in range(TILES):
                    k = (TILES * b + t) // 2
                    if k == 1 and t % 2 == 0:
                        pe.wait_ge(sem("mw2_ready"), B)
                    if k == 3 and t % 2 == 0:
                        pe.wait_ge(sem("bias_added"), 1)
                    dst = quarter(k)[:, D * (t % 2):D * (t % 2 + 1)]
                    for c in range(FC):
                        ins = pe.matmul(dst, uT[b][:, c, P * t:P * (t + 1)], mw2[b][:, c, :], start=(c == 0),
                                        stop=(c == FC - 1))
                    if t % 2:
                        ins.then_inc(sem("ffn_full"), 1)


_IN_NAMES = ["x", "ctx", "small", "wqkv", "wout", "rw", "wgu", "wdn", "wsgu", "wsdn", "wqv", "gw1", "gw2", "w1", "tw1",
             "w2", "tw2", "tb2"]


def lay_out(a):
    import numpy as np

    small = np.zeros((P, SMALL_WIDTH), np.float32)

    def put(name, value):
        start, end = SMALL[name]
        small[:, start:end] = value

    for name, key in (("ln_l_g", "L0_xattn_ln_l_g"), ("ln_l_b", "L0_xattn_ln_l_b"), ("ln_m_g", "L0_xattn_ln_m_g"),
                      ("ln_m_b", "L0_xattn_ln_m_b"), ("gate_b1", "L1_ffn_gate_b1")):
        put(name, a[key][:, None])
    for name, key in (("g_xattn", "g_xattn"), ("g_ffn", "g_ffn"), ("b_sim", "L1_xattn_b_sim"),
                      ("gate_b2", "L1_ffn_gate_b2"), ("b_qv_row", "L1_xattn_b_qv"), ("b2_row", "L1_ffn_b2")):
        put(name, a[key][None])
    put("w_sim", a["L1_xattn_w_sim"].reshape(3, P).T)
    small[0:8, SMALL["gate_b2_col"][0]] = a["L1_ffn_gate_b2"]
    put("b1", a["L1_ffn_b1"].reshape(4, P).T)
    put("Tb1", a["L1_ffn_Tb1"].reshape(8, 4, P).transpose(2, 1, 0).reshape(P, 32))
    wq = a["L0_xattn_Wq"].reshape(P, 8, P)
    wkv = a["L0_xattn_Wkv"].reshape(P, 2, 8, P)
    gate_up = np.concatenate([a["L0_ffn_w_gate"], a["L0_ffn_w_up"]], axis=2)
    laid = {
        "x": a["x"], "ctx": a["ctx_1024"], "small": small,
        "wqkv": np.concatenate([w.transpose(1, 0, 2) for w in (wq, wkv[:, 0], wkv[:, 1])], axis=2),
        "wout": a["L0_xattn_Wout"].reshape(8, P, P),
        "rw": a["L0_ffn_router_w"].T,
        "wgu": gate_up.reshape(8, 8, P, 192).transpose(0, 2, 1, 3),
        "wdn": a["L0_ffn_w_down"].reshape(8, 8, 96, P).transpose(0, 2, 1, 3),
        "wsgu": a["L0_ffn_ws_gate_up"], "wsdn": a["L0_ffn_ws_down"],
        "wqv": a["L1_xattn_W_qv"].reshape(4, P, P).transpose(1, 0, 2),
        "gw1": a["L1_ffn_gate_w1"].T, "gw2": a["L1_ffn_gate_w2"].T,
        "w1": a["L1_ffn_W1"].T, "tw1": a["L1_ffn_TW1"].transpose(2, 0, 1),
        "w2": a["L1_ffn_W2"].T.reshape(4, P, P).transpose(1, 0, 2),
        "tw2": a["L1_ffn_TW2"].transpose(0, 2, 1).reshape(8, 4, P, P).transpose(2, 0, 1, 3),
        "tb2": a["L1_ffn_Tb2"],
    }
    return {k: np.ascontiguousarray(v) for k, v in laid.items()}


def kernel(**inputs):
    import numpy as _np
    import concourse.bacc as _bacc
    from concourse import mybir as _mybir
    from concourse.bass_utils import run_bass_kernel_spmd as _run

    nc = _bacc.Bacc("TRN2", target_bir_lowering=False, num_devices=1)
    laid = lay_out({k: _np.asarray(v) for k, v in inputs.items()})
    arrays, args = {}, []
    for name in _IN_NAMES:
        arrays[f"in_{name}_dram"] = laid[name]
        args.append(nc.dram_tensor(f"in_{name}_dram", laid[name].shape, _mybir.dt.from_np(laid[name].dtype),
                                   kind="ExternalInput").ap())
    out = nc.dram_tensor("out_dram", laid["x"].shape, _mybir.dt.float32, kind="ExternalOutput").ap()
    flamingo_block(nc, *args, out)
    r = _run(nc, [arrays], core_ids=[0])
    return r.results[0]["out_dram"]
```
